# Optimizing a Trainium2 kernel written in Bass

```python
import numpy as np
import jax
import jax.numpy as jnp

def _softmax(x, axis=-1):
    return jax.nn.softmax(x, axis=axis)

def _gelu(x):
    return jax.nn.gelu(x, approximate=True)

def _silu(x):
    return jax.nn.silu(x)

def _sigmoid(x):
    return jax.nn.sigmoid(x)

def _layernorm(x, axis=-1, eps=1e-05):
    m = jnp.mean(x, axis=axis, keepdims=True)
    v = jnp.var(x, axis=axis, keepdims=True)
    return (x - m) / jnp.sqrt(v + eps)

def _scatter_add(tgt, idx, src, axis=0):
    return tgt.at[idx].add(src)

def _segment_sum(src, seg, n):
    return jax.ops.segment_sum(src, seg, n)
kernel_name = 'mk_adj_ffn_d2_adj_r2_936846'

def setup_inputs(seed: int=0):
    np.random.seed(seed)
    _w = jnp.asarray

    def _rec_inputs():
        import jax
        import jax.numpy as jnp
        _gk = jax.random.key(seed)
        x = -0.0005207 + 1.001 * jax.random.normal(jax.random.fold_in(_gk, 1), (4096, 128), jnp.float32)
        _w = (1.0 + jnp.arange(4096, dtype=jnp.float32)) ** (-0.5)
        _w = _w / _w.mean()
        _pij = jnp.clip(0.000488281 * _w[:, None] * _w[None, :], 0.0, 1.0)
        _a = jax.random.uniform(jax.random.fold_in(_gk, 2), (4096, 4096)) < _pij
        adj = _a.astype(jnp.int32)
        return (x, adj)
    x, adj = _rec_inputs()

    def _L0_gnn_setup():
        import jax, jax.numpy as jnp
        import numpy as np
        N, D, H = (4096, 128, 128)
        KEEP_RATIO = 0.5
        TEMP = 1.0
        COS_EPS = 0.0001
        NEG = -9000000000000000.0

        def _cos_normalize(x):
            n = jnp.linalg.norm(x, axis=-1, keepdims=True)
            return x / jnp.maximum(n, COS_EPS)
        key = jax.random.key(seed)
        k1, k2, k3, k4 = jax.random.split(key, 4)
        features = jax.random.normal(k1, (N, D), dtype=jnp.float32)
        adj = jax.random.randint(k2, (N, N), 0, 2, dtype=jnp.int32)
        Wq = jax.random.normal(k3, (H, D), dtype=jnp.float32) * 0.001
        Wk = jax.random.normal(k4, (H, D), dtype=jnp.float32) * 0.001
        return {'features': features, 'adj': adj, 'Wq': Wq, 'Wk': Wk}
    _L0_gnn_all = _L0_gnn_setup()
    _L0_gnn_in = {k: v for k, v in _L0_gnn_all.items() if k in ('Wq', 'Wk')}
    del _L0_gnn_all

    def _L0_ffn_setup():
        import math
        import jax, jax.numpy as jnp
        import numpy as np
        CAPACITY_FACTOR = 1.25
        TOP_K = 2
        LN_EPS = 1e-05

        def _layer_norm(x, gamma, beta):
            mu = jnp.mean(x, axis=-1, keepdims=True)
            var = jnp.var(x, axis=-1, keepdims=True)
            return (x - mu) * jax.lax.rsqrt(var + LN_EPS) * gamma + beta
        key = jax.random.key(seed)
        ks = jax.random.split(key, 4)
        B, S, D, F, E = (8, 2048, 128, 256, 8)
        x = jax.random.normal(ks[0], (B, S, D), dtype=jnp.float32)
        Wr = jax.random.normal(ks[1], (D, E), dtype=jnp.float32) / np.sqrt(D)
        br = jnp.zeros((E,), jnp.float32)
        W1 = jax.random.normal(ks[2], (E, D, F), dtype=jnp.float32) / np.sqrt(D)
        b1 = jnp.zeros((E, F), jnp.float32)
        W2 = jax.random.normal(ks[3], (E, F, D), dtype=jnp.float32) / np.sqrt(F)
        b2 = jnp.zeros((E, D), jnp.float32)
        gamma = jnp.ones((D,), jnp.float32)
        beta = jnp.zeros((D,), jnp.float32)
        return {'x': x, 'Wr': Wr, 'br': br, 'W1': W1, 'b1': b1, 'W2': W2, 'b2': b2, 'gamma': gamma, 'beta': beta}
    _L0_ffn_all = _L0_ffn_setup()
    _L0_ffn_in = {k: v for k, v in _L0_ffn_all.items() if k in ('Wr', 'br', 'W1', 'b1', 'W2', 'b2', 'gamma', 'beta')}
    del _L0_ffn_all

    def _L1_gnn_setup():
        import jax, jax.numpy as jnp
        import numpy as np
        N, D_IN, D_OUT = (5000, 128, 128)
        key = jax.random.key(seed)
        k1, k2, k3, k4 = jax.random.split(key, 4)

        def xavier(k, shape, gain=1.414):
            fan_in, fan_out = (shape[0], shape[1])
            bound = gain * np.sqrt(6.0 / (fan_in + fan_out))
            return jax.random.uniform(k, shape, jnp.float32, -bound, bound)
        return {'input': jax.random.normal(k1, (N, D_IN), jnp.float32), 'adj': jax.random.randint(k2, (N, N), 0, 2, jnp.int32), 'M': N, 'W': xavier(k3, (D_IN, D_OUT)), 'b': jnp.zeros((D_OUT,), jnp.float32), 'a': xavier(k4, (D_OUT, 1))}
    _L1_gnn_all = _L1_gnn_setup()
    _L1_gnn_in = {k: v for k, v in _L1_gnn_all.items() if k in ('W', 'b', 'a')}
    del _L1_gnn_all

    def _L1_ffn_setup():
        import jax, jax.numpy as jnp
        import numpy as np
        B, S, D, E, H, K = (4, 2048, 128, 8, 256, 2)
        key = jax.random.key(seed)
        ks = jax.random.split(key, 6)
        x = jax.random.normal(ks[0], (B, S, D), jnp.float32)
        Wg = jax.random.normal(ks[1], (D, E), jnp.float32) * 0.02
        bg = jnp.zeros((E,), jnp.float32)
        W1 = jax.random.normal(ks[2], (E, D, H), jnp.float32) * 0.02
        b1 = jnp.zeros((E, H), jnp.float32)
        W2 = jax.random.normal(ks[3], (E, H, D), jnp.float32) * 0.02
        b2 = jnp.zeros((E, D), jnp.float32)
        return {'x': x, 'Wg': Wg, 'bg': bg, 'W1': W1, 'b1': b1, 'W2': W2, 'b2': b2}
    _L1_ffn_all = _L1_ffn_setup()
    _L1_ffn_in = {k: v for k, v in _L1_ffn_all.items() if k in ('Wg', 'bg', 'W1', 'b1', 'W2', 'b2')}
    del _L1_ffn_all
    return {'x': x, 'adj': adj, 'L0_gnn_Wq': _L0_gnn_in['Wq'], 'L0_gnn_Wk': _L0_gnn_in['Wk'], 'L0_ffn_Wr': _L0_ffn_in['Wr'], 'L0_ffn_br': _L0_ffn_in['br'], 'L0_ffn_W1': _L0_ffn_in['W1'], 'L0_ffn_b1': _L0_ffn_in['b1'], 'L0_ffn_W2': _L0_ffn_in['W2'], 'L0_ffn_b2': _L0_ffn_in['b2'], 'L0_ffn_gamma': _L0_ffn_in['gamma'], 'L0_ffn_beta': _L0_ffn_in['beta'], 'L1_gnn_W': _L1_gnn_in['W'], 'L1_gnn_b': _L1_gnn_in['b'], 'L1_gnn_a': _L1_gnn_in['a'], 'L1_ffn_Wg': _L1_ffn_in['Wg'], 'L1_ffn_bg': _L1_ffn_in['bg'], 'L1_ffn_W1': _L1_ffn_in['W1'], 'L1_ffn_b1': _L1_ffn_in['b1'], 'L1_ffn_W2': _L1_ffn_in['W2'], 'L1_ffn_b2': _L1_ffn_in['b2']}

def reference(x, adj, L0_gnn_Wq, L0_gnn_Wk, L0_ffn_Wr, L0_ffn_br, L0_ffn_W1, L0_ffn_b1, L0_ffn_W2, L0_ffn_b2, L0_ffn_gamma, L0_ffn_beta, L1_gnn_W, L1_gnn_b, L1_gnn_a, L1_ffn_Wg, L1_ffn_bg, L1_ffn_W1, L1_ffn_b1, L1_ffn_W2, L1_ffn_b2):
    import jax
    import jax.numpy as jnp

    def _L0_gnn_ref(features, adj, Wq, Wk):
        import jax, jax.numpy as jnp
        import numpy as np
        N, D, H = (4096, 128, 128)
        KEEP_RATIO = 0.5
        TEMP = 1.0
        COS_EPS = 0.0001
        NEG = -9000000000000000.0

        def _cos_normalize(x):
            n = jnp.linalg.norm(x, axis=-1, keepdims=True)
            return x / jnp.maximum(n, COS_EPS)
        Qn = _cos_normalize(features @ Wq.T)
        Kn = _cos_normalize(features @ Wk.T)
        raw_att = Kn @ Qn.T
        att = jnp.where(adj > 0, raw_att, NEG) * TEMP
        att = jax.nn.softmax(att, axis=1)
        prop_fea = att @ features
        adj_mask = (jnp.sum(adj, axis=1) > 0).astype(features.dtype)[:, None]
        prop_fea = adj_mask * prop_fea + (1.0 - adj_mask) * features
        return (1.0 - KEEP_RATIO) * prop_fea + KEEP_RATIO * features

    def _L0_ffn_ref(x, Wr, br, W1, b1, W2, b2, gamma, beta):
        import math
        import jax, jax.numpy as jnp
        import numpy as np
        CAPACITY_FACTOR = 1.25
        TOP_K = 2
        LN_EPS = 1e-05

        def _layer_norm(x, gamma, beta):
            mu = jnp.mean(x, axis=-1, keepdims=True)
            var = jnp.var(x, axis=-1, keepdims=True)
            return (x - mu) * jax.lax.rsqrt(var + LN_EPS) * gamma + beta
        B, S, D = x.shape
        E = Wr.shape[1]
        N = B * S
        K = TOP_K
        logits = jnp.mean(x, axis=1) @ Wr + br
        routing_weights = jax.nn.softmax(logits, axis=-1)
        capacity = float(math.ceil(N * CAPACITY_FACTOR / E))
        expected_loads = routing_weights.sum(axis=0) * (N / B)
        scale = jnp.where(expected_loads > capacity, capacity / expected_loads, 1.0)
        routing_weights = jax.nn.softmax(routing_weights * scale, axis=-1)
        rw_tok = jnp.broadcast_to(routing_weights[:, None, :], (B, S, E)).reshape(N, E)
        top_w, top_i = jax.lax.top_k(rw_tok, K)
        top_w = jax.nn.softmax(top_w, axis=-1)
        xf = x.reshape(N, D)
        h = jax.nn.gelu(jnp.einsum('nd,edf->enf', xf, W1) + b1[:, None, :], approximate=False)
        y = jnp.einsum('enf,efd->end', h, W2) + b2[:, None, :]
        w_dense = jnp.zeros((N, E), x.dtype).at[jnp.arange(N)[:, None], top_i].add(top_w)
        out = jnp.einsum('ne,end->nd', w_dense, y).reshape(B, S, D)
        out = _layer_norm(out + x, gamma, beta)
        return out

    def _L1_gnn_ref(input, adj, M, W, b, a):
        import jax, jax.numpy as jnp
        import numpy as np
        N, D_IN, D_OUT = (5000, 128, 128)
        h = jnp.tanh(input @ W + b)
        inp = input @ W
        e = (h @ a)[:, 0]
        valid = jnp.sum(h, axis=1) != 0
        mask = (adj[:M] > 0) & valid[None, :]
        neg = jnp.asarray(-1e+30, h.dtype)
        scores = jnp.where(mask, e[None, :], neg)
        m = jnp.max(scores, axis=1, keepdims=True)
        w = jnp.where(mask, jnp.exp(scores - m), 0.0)
        denom = jnp.sum(w, axis=1, keepdims=True)
        att = w / jnp.maximum(denom, 1e-30)
        return att @ inp

    def _L1_ffn_ref(x, Wg, bg, W1, b1, W2, b2):
        import jax, jax.numpy as jnp
        import numpy as np
        B, S, D, E, H, K = (4, 2048, 128, 8, 256, 2)
        Bv, Sv, Dv = x.shape
        gate_scores = x @ Wg + bg
        _, idx = jax.lax.top_k(gate_scores, K)
        mask = jax.nn.one_hot(idx, E, dtype=x.dtype).sum(axis=-2)
        xf = x.reshape(-1, Dv)
        mf = mask.reshape(-1, E)
        h = jax.nn.gelu(jnp.einsum('td,edh->teh', xf, W1) + b1[None], approximate=False)
        y = jnp.einsum('teh,ehd->ted', h, W2) + b2[None]
        out = jnp.einsum('ted,te->td', y, mf)
        return out.reshape(Bv, Sv, Dv)
    x = x + _L0_gnn_ref(_layernorm(x, axis=-1), adj, L0_gnn_Wq, L0_gnn_Wk)
    x = x + _L0_ffn_ref(_layernorm(x, axis=-1)[None], L0_ffn_Wr, L0_ffn_br, L0_ffn_W1, L0_ffn_b1, L0_ffn_W2, L0_ffn_b2, L0_ffn_gamma, L0_ffn_beta)[0]
    x = x + _L1_gnn_ref(_layernorm(x, axis=-1), adj, 4096, L1_gnn_W, L1_gnn_b, L1_gnn_a)
    x = x + _L1_ffn_ref(_layernorm(x, axis=-1)[None], L1_ffn_Wg, L1_ffn_bg, L1_ffn_W1, L1_ffn_b1, L1_ffn_W2, L1_ffn_b2)[0]
    return x

_drawn_inputs = setup_inputs


def setup_inputs(seed=0):
    import zlib

    import numpy as np

    out = dict(_drawn_inputs(seed))
    spreads = {'L0_ffn_br': (0.0, 0.1),
     'L0_ffn_b1': (0.0, 0.427),
     'L0_ffn_b2': (0.0, 0.318),
     'L0_ffn_gamma': (1.0, 0.2),
     'L0_ffn_beta': (0.0, 0.1),
     'L1_gnn_b': (0.0, 0.762),
     'L1_ffn_bg': (0.0, 0.1),
     'L1_ffn_b1': (0.0, 0.8),
     'L1_ffn_b2': (0.0, 0.1)}
    factors = {'L0_gnn_Wq': 5.365,
     'L0_gnn_Wk': 5.389,
     'L0_ffn_Wr': 8.0,
     'L1_ffn_W1': 3.021,
     'L1_ffn_W2': 2.744}
    for name, (base, spread) in spreads.items():
        noise = np.random.default_rng([zlib.crc32(name.encode()), seed]).standard_normal(out[name].shape)
        drawn = base * np.exp(spread * noise) if base else spread * noise
        out[name] = jnp.asarray(drawn.astype(out[name].dtype))
    for name, factor in factors.items():
        out[name] = (out[name] * factor).astype(out[name].dtype)
    return out
```

```python
from contextlib import ExitStack

import numpy as np

import concourse.bass as bass
from concourse import mybir

F32 = mybir.dt.float32
F16 = mybir.dt.float16
BF16 = mybir.dt.bfloat16
FP8 = mybir.dt.float8e4
I32 = mybir.dt.int32
U32 = mybir.dt.uint32
ALU = mybir.AluOpType
ACT = mybir.ActivationFunctionType
AX = mybir.AxisListType

P = 128
N = 4096
D = 128
TILES = N // P
SUB = 4
GROUP = SUB * P
GROUPS = N // GROUP
PAIRS = TILES // 2
E = 8
F = 256
FH = F // P
LN_EPS = 1e-5
QK_SCALE = 64.0
V_SCALE = 16.0
SLOTS = 2


class Chain:

    def __init__(self, eng, sem, turn=0, per_turn=0):
        self.eng, self.sem, self.base, self.n = eng, sem, turn * per_turn, 0

    def mark(self, ins):
        self.n += 1
        ins.then_inc(self.sem, 1)

    def wait(self):
        self.eng.wait_ge(self.sem, self.base + self.n)

    def link(self, ins):
        self.mark(ins)
        self.wait()


def row_statistics(nc, ch, stats, mean, var, t0, t1):
    me, mo, ve, vo = (stats[:, :, i] for i in (1, 4, 2, 5))
    ch.mark(nc.vector.tensor_tensor(mean, me, mo, ALU.add))
    ch.mark(nc.vector.tensor_tensor(t0, me, mo, ALU.subtract))
    ch.link(nc.vector.tensor_tensor(t1, ve, vo, ALU.add))
    ch.mark(nc.vector.tensor_scalar(mean, mean, 0.5, None, ALU.mult))
    ch.link(nc.vector.scalar_tensor_tensor(out=t0, in0=t0, scalar=0.25, in1=t0, op0=ALU.mult, op1=ALU.mult))
    ch.link(nc.vector.scalar_tensor_tensor(out=var, in0=t1, scalar=1.0 / D, in1=t0, op0=ALU.mult, op1=ALU.add))


ROW_STATISTICS_STEPS = 6


def inverse_root(nc, ch, y, v, t0, t1):
    ch.mark(nc.vector.tensor_scalar(t0.bitcast(I32), v.bitcast(I32), 1, None, ALU.arith_shift_right))
    ch.link(nc.vector.tensor_scalar(t1, v, -0.5, None, ALU.mult))
    ch.link(nc.vector.tensor_scalar(y.bitcast(I32), t0.bitcast(I32), -1.0, float(0x5F3759DF), ALU.mult, ALU.add))
    for _ in range(4):
        ch.link(nc.vector.tensor_tensor(t0, t1, y, ALU.mult))
        ch.link(nc.vector.tensor_tensor(t0, t0, y, ALU.mult))
        ch.link(nc.vector.scalar_tensor_tensor(out=y, in0=t0, scalar=1.5, in1=y, op0=ALU.add, op1=ALU.mult))


INVERSE_ROOT_STEPS = 15


def prepare(nc, io, sb, ps):
    with ExitStack() as ctx:
        small = lambda name, shape, dt=F32: ctx.enter_context(nc.sbuf_tensor(name, shape, dt))
        sem = lambda name: ctx.enter_context(nc.semaphore(name))
        room = sb["mask"][:, :].bitcast(F32)
        x = room[:, 0:4096].rearrange("p (t d) -> p t d", d=D)
        qk = room[:, 4096:12288].rearrange("p (g n) -> p g n", g=GROUPS)
        square = room[:, 12288:14336].rearrange("p (u s h) -> p u s h", u=2, h=D)
        feat = room[:, 14336:15360].rearrange("p (u s d) -> p u s d", u=2, d=D)
        featT = room[:, 15360:16384].rearrange("p (u n) -> p u n", u=2)
        unit = room[:, 16384:18432].rearrange("p (u s h) -> p u s h", u=2, h=D)
        w_qk = small("w_qk", [P, 2 * D])
        stats = small("stats0", [P, TILES, 6])
        mean, var, rstd, t0, t1 = (small(n, [P, TILES]) for n in ("mean0", "var0", "rstd0", "t00", "t01"))
        ss, rnorm, t2, t3 = (small(n, [P, 2 * TILES]) for n in ("ss", "rnorm", "t02", "t03"))
        hi, lo = sb["qT"][:, 0, :], sb["qT"][:, 1, :]
        kt = sb["x1"][:, :, :].bitcast(F16)
        v16 = sb["v16"]

        x_in = [sem(f"x_in{i}") for i in range(4)]
        w_in = sem("w_in")
        ident_ready = sem("ident_ready")
        dve_chain = sem("dve_chain0")
        feat_ready = sem("feat_ready")
        feat_turned = sem("feat_turned")
        v_hi_ready = sem("v_hi_ready")
        v_lo_ready = sem("v_lo_ready")
        feat_spilled = [sem(f"feat_spilled{u}") for u in range(2)]
        featT_ready = sem("featT_ready")
        qk_ready = sem("qk_ready")
        qk_copied = sem("qk_copied")
        qk_squared = sem("qk_squared")
        ss_ready = sem("ss_ready")
        unit_ready = sem("unit_ready")
        unit_turned = sem("unit_turned")
        unit_hi = sem("unit_hi")
        unit_lo = sem("unit_lo")

        with nc.Block() as block:

            @block.sync
            def _(sp):
                x_tiles = io["x"].rearrange("(t p) d -> p t d", p=P)
                for i in range(4):
                    sp.dma_start(x[:, 8 * i:8 * i + 8, :], x_tiles[:, 8 * i:8 * i + 8, :]).then_inc(x_in[i], 16)
                sp.dma_start(w_qk[:, 0:D], io["WqT"]).then_inc(w_in, 16)
                sp.dma_start(w_qk[:, D:2 * D], io["WkT"]).then_inc(w_in, 16)
                with sp.Fori(0, GROUPS // 2) as i:
                    for u in range(2):
                        sp.wait_ge(feat_ready, 2 * i + u + 1)
                        sp.dma_start(io["feat"][:, 2 * i + u, :, :], feat[:, u, :, :]).then_inc(feat_spilled[u], 16)
                for u in range(2):
                    sp.wait_ge(feat_spilled[u], 16 * (SLOTS // 2) + 16 * (GROUPS // 2))

            @block.gpsimd
            def _(pool):
                nc.gpsimd.memset(sb["ident"][:, :], 0.0).then_inc(ident_ready, 1)
                pool.wait_ge(ident_ready, 1)
                nc.gpsimd.affine_select(out=sb["ident"][:, :], in_=sb["ident"][:, :], compare_op=ALU.not_equal,
                                        fill=1.0, base=0, pattern=[[-1, P]], channel_multiplier=1).then_inc(ident_ready, 1)
                nc.gpsimd.memset(v16[:, :, D:D + 1], V_SCALE).then_inc(ident_ready, 1)
                pool.wait_ge(ident_ready, 3)

            @block.vector
            def _(dve):
                dve.sem_inc(v_lo_ready, SLOTS)
                dve.sem_inc(unit_lo, SLOTS)
                for u in range(2):
                    dve.sem_inc(feat_spilled[u], 16)
                ch = Chain(dve, dve_chain)
                for t in range(TILES):
                    if t % 8 == 0:
                        dve.wait_ge(x_in[t // 8], 16)
                    ins = nc.vector.bn_stats(stats[:, t, :], x[:, t, :])
                ch.link(ins)
                row_statistics(nc, ch, stats, mean[:, :], var[:, :], t0[:, :], t1[:, :])
                ch.link(nc.vector.tensor_scalar(var[:, :], var[:, :], LN_EPS, None, ALU.add))
                inverse_root(nc, ch, rstd[:, :], var[:, :], t0[:, :], t1[:, :])

                with dve.Fori(0, GROUPS // 2) as i:
                    for u in range(2):
                        g = 2 * i + u
                        dve.wait_ge(feat_turned, g + 1)
                        dve.wait_ge(v_hi_ready, g + 1)
                        dve.wait_ge(v_lo_ready, g + 1)
                        dve.wait_ge(feat_spilled[u], 16 * i + 16)
                        for s in range(SUB):
                            t = bass.ds(g * SUB + s, 1)
                            ins = nc.vector.tensor_scalar(feat[:, u, s, :], x[:, t, :].rearrange("p a d -> p (a d)"), mean[:, t], rstd[:, t],
                                                          ALU.subtract, ALU.mult)
                        ins.then_inc(feat_ready, 1)
                        dve.wait_ge(v_hi_ready, SLOTS + g + 1)
                        dve.wait_ge(feat_ready, g + 1)
                        tiles = bass.ds(g * SUB, SUB)
                        nc.vector.scalar_tensor_tensor(out=v16[:, tiles, D + 1:], in0=feat[:, u, :, :], scalar=V_SCALE,
                                                       in1=v16[:, tiles, 0:D], op0=ALU.mult, op1=ALU.subtract)\
                            .then_inc(v_lo_ready, 1)
                        dve.wait_ge(feat_turned, SLOTS + g + 1)
                        nc.vector.tensor_copy(featT[:, u, :], ps[:, u, :]).then_inc(featT_ready, 1)
                        dve.wait_ge(qk_squared, g + 1)
                        nc.vector.tensor_reduce(ss[:, bass.ds(g * 8, 8)], square[:, u, :, :], AX.X, ALU.add)\
                            .then_inc(ss_ready, 1)
                dve.wait_ge(ss_ready, GROUPS)
                ch.link(nc.vector.tensor_scalar(ss[:, :], ss[:, :], 1e-8, None, ALU.max))
                inverse_root(nc, ch, rnorm[:, :], ss[:, :], t2[:, :], t3[:, :])
                ch.link(nc.vector.tensor_scalar(rnorm[:, :], rnorm[:, :], QK_SCALE, None, ALU.mult))
                dve.wait_ge(qk_copied, GROUPS)
                with dve.Fori(0, GROUPS // 2) as i:
                    for u in range(2):
                        g = 2 * i + u
                        dve.wait_ge(unit_turned, g + 1)
                        scale = rnorm[:, bass.ds(g * 8, 8)].unsqueeze(2).to_broadcast([P, 8, D])
                        raw = qk[:, bass.ds(g, 1), :].rearrange("p a (s h) -> p (a s) h", h=D)
                        nc.vector.tensor_tensor(unit[:, u, :, :], raw, scale, ALU.mult).then_inc(unit_ready, 1)
                        dve.wait_ge(unit_turned, SLOTS + g + 1)
                        dve.wait_ge(unit_hi, g + 1)
                        cols = bass.ds(g * GROUP, GROUP)
                        nc.vector.tensor_tensor(lo[:, cols], ps[:, 2 * u, :], hi[:, cols], ALU.subtract)
                        k_lo = kt[:, bass.ds(g, 1), GROUP:].rearrange("p a n -> p (a n)")
                        k_hi = kt[:, bass.ds(g, 1), 0:GROUP].rearrange("p a n -> p (a n)")
                        nc.vector.tensor_tensor(k_lo, ps[:, 2 * u + 1, :], k_hi, ALU.subtract).then_inc(unit_lo, 1)
                dve.wait_ge(unit_lo, SLOTS + GROUPS)

            @block.scalar
            def _(act):
                act.sem_inc(v_hi_ready, SLOTS)
                with act.Fori(0, GROUPS // 2) as i:
                    for u in range(2):
                        g = 2 * i + u
                        act.wait_ge(feat_ready, g + 1)
                        tiles = bass.ds(g * SUB, SUB)
                        nc.scalar.activation(v16[:, tiles, 0:D], feat[:, u, :, :], ACT.Copy, scale=V_SCALE)\
                            .then_inc(v_hi_ready, 1)
                        act.wait_ge(qk_ready, g + 1)
                        products = ps[:, 2 + 2 * u:4 + 2 * u, :].rearrange("p b n -> p (b n)")
                        nc.scalar.activation(qk[:, bass.ds(g, 1), :].rearrange("p a n -> p (a n)"), products, ACT.Copy)\
                            .then_inc(qk_copied, 1)
                        nc.scalar.activation(square[:, u, :, :].rearrange("p s h -> p (s h)"), products, ACT.Square)\
                            .then_inc(qk_squared, 1)
                with act.Fori(0, GROUPS // 2) as i:
                    for u in range(2):
                        g = 2 * i + u
                        act.wait_ge(unit_turned, SLOTS + g + 1)
                        cols = bass.ds(g * GROUP, GROUP)
                        nc.scalar.activation(hi[:, cols], ps[:, 2 * u, :], ACT.Copy)
                        nc.scalar.activation(kt[:, bass.ds(g, 1), 0:GROUP].rearrange("p a n -> p (a n)"),
                                             ps[:, 2 * u + 1, :], ACT.Copy).then_inc(unit_hi, 1)
                act.wait_ge(unit_hi, GROUPS)

            @block.tensor
            def _(pe):
                pe.sem_inc(feat_turned, SLOTS)
                pe.sem_inc(unit_turned, SLOTS)
                pe.wait_ge(ident_ready, 2)
                pe.wait_ge(w_in, 32)
                with pe.Fori(0, GROUPS // 2) as i:
                    for u in range(2):
                        g = 2 * i + u
                        pe.wait_ge(feat_ready, g + 1)
                        for s in range(SUB):
                            ins = nc.tensor.transpose(ps[:, u, s * P:(s + 1) * P], feat[:, u, s, :], sb["ident"][:, :])
                        ins.then_inc(feat_turned, 1)
                        pe.wait_ge(featT_ready, g + 1)
                        for s in range(SUB):
                            bank, half = 2 + 2 * u + s // 2, s % 2
                            ins = nc.tensor.matmul(ps[:, bank, half * 2 * D:(half + 1) * 2 * D],
                                                   featT[:, u, s * P:(s + 1) * P], w_qk[:, :], start=True, stop=True)
                        ins.then_inc(qk_ready, 1)
                with pe.Fori(0, GROUPS // 2) as i:
                    for u in range(2):
                        g = 2 * i + u
                        pe.wait_ge(unit_ready, g + 1)
                        pe.wait_ge(unit_lo, g + 1)
                        for side in range(2):
                            for s in range(SUB):
                                ins = nc.tensor.transpose(ps[:, 2 * u + side, s * P:(s + 1) * P],
                                                          unit[:, u, 2 * s + side, :], sb["ident"][:, :])
                        ins.then_inc(unit_turned, 1)


EPILOGUE_STEPS = 13


def attend(nc, io, sb, ps):
    with ExitStack() as ctx:
        buf = lambda name, shape, dt=F32: ctx.enter_context(nc.sbuf_tensor(name, shape, dt))
        sem = lambda name: ctx.enter_context(nc.semaphore(name))
        LOADS = 4
        TURNS = PAIRS // LOADS
        W = 2 * GROUP
        adj = buf("adj", [P, LOADS, W], I32)
        exps = buf("exps", [P, SLOTS, W])
        probs = adj[:, :, :].bitcast(F32)
        p_hi = buf("p_hi", [P, SLOTS, W], F16)
        p_lo = buf("p_lo", [P, SLOTS, W], F16)
        sums = buf("sums", [P, SUB, 2 * D + 1])
        x_feat = buf("x_feat", [P, 2, SUB, D])
        cols = [buf(n, [P, SUB]) for n in ("no_edge", "denominator", "keep")]
        qT, v16, mask = sb["qT"], sb["v16"], sb["mask"]
        kT = sb["x1"][:, :, :].bitcast(F16)

        adj_landed = [sem(f"adj_landed{u}") for u in range(LOADS)]
        rows_landed = sem("rows_landed")
        scores_ready = sem("scores_ready")
        exps_ready = sem("exps_ready")
        masked = sem("masked")
        mask_kept = sem("mask_kept")
        hi_ready = sem("hi_ready")
        lo_ready = sem("lo_ready")
        pair_used = sem("pair_used")
        sums_copied = sem("sums_copied")
        rows_done = sem("rows_done")
        epilogue_chain = sem("epilogue_chain")

        def chunks(eng, chunk):
            with eng.Fori(0, GROUPS - 1) as c:
                chunk(c, False)
            chunk(GROUPS - 1, True)

        def steps(eng, c, last_chunk, step):
            def turn(m, first, last):
                for u in range(LOADS):
                    step(c, m, u, first and u == 0, last and u == LOADS - 1, last_chunk and last and u >= LOADS - 2)
            turn(0, True, False)
            with eng.Fori(1, TURNS - 1) as m:
                turn(m, False, False)
            turn(TURNS - 1, False, True)

        with nc.Block() as block:

            @block.sync
            def _(sp):
                def turn(c, m):
                    for u in range(LOADS):
                        step = PAIRS * c + LOADS * m + u
                        sp.wait_ge(lo_ready, step + 1)
                        sp.wait_ge(mask_kept, step + 1)
                        sp.dma_start(adj[:, u, :], io["adj"][bass.ds(step, 1), :, :].rearrange("a p n -> (a p) n"))\
                            .then_inc(adj_landed[u], 16)

                with sp.Fori(0, GROUPS) as c:
                    turn(c, 0)
                    sp.wait_ge(rows_done, c + 1)
                    for r, rows in enumerate((io["x"].rearrange("(g s p) d -> p g s d", p=P, s=SUB), io["feat"])):
                        sp.dma_start(x_feat[:, r, :, :], rows[:, bass.ds(c, 1), :, :].rearrange("p a s d -> p (a s) d"))\
                            .then_inc(rows_landed, 16)
                    with sp.Fori(1, TURNS) as m:
                        turn(c, m)

            @block.tensor
            def _(pe):
                pe.sem_inc(pair_used, SLOTS)

                def scores(c, jp, u):
                    for h in range(2):
                        j = bass.ds(jp * 2 * P + h * P, P)
                        out = ps[:, 2 * (u % 2) + h, :]
                        for n, (q_half, k_half) in enumerate(((0, 0), (0, 1), (1, 0))):
                            keys = kT[:, bass.ds(c, 1), k_half * GROUP:(k_half + 1) * GROUP].rearrange("p a n -> p (a n)")
                            ins = nc.tensor.matmul(out, qT[:, q_half, j], keys, start=(n == 0), stop=(n == 2))
                    ins.then_inc(scores_ready, 1)

                def step(c, m, u, first, last, no_next):
                    jp = LOADS * m + u
                    k = PAIRS * c + jp
                    if not no_next:
                        pe.wait_ge(exps_ready, k + 1)
                        if isinstance(m, int) and jp + 2 >= PAIRS:
                            scores(c + 1, jp + 2 - PAIRS, u)
                        else:
                            scores(c, jp + 2, u)
                    pe.wait_ge(hi_ready, k + 1)
                    pe.wait_ge(lo_ready, LOADS + k + 1)
                    if first:
                        pe.wait_ge(sums_copied, 2 * (c + 1))
                    for h in range(2):
                        v = v16[:, bass.ds(2 * jp + h, 1), :].rearrange("p a n -> p (a n)")
                        for s in range(SUB):
                            i = slice(h * GROUP + s * P, h * GROUP + (s + 1) * P)
                            start, stop = first and h == 0, last and h == 1
                            for half in ("hi", "lo") if start else ("lo", "hi"):
                                if half == "hi":
                                    ins = nc.tensor.matmul(ps[:, 4 + s, 0:2 * D + 1], p_hi[:, u % 2, i], v,
                                                           start=start, stop=stop)
                                else:
                                    ins = nc.tensor.matmul(ps[:, 4 + s, 0:D + 1], p_lo[:, u % 2, i], v[:, 0:D + 1],
                                                           start=False, stop=False)
                    ins.then_inc(pair_used, 1)

                scores(0, 0, 0)
                scores(0, 1, 1)
                chunks(pe, lambda c, last: steps(pe, c, last, step))

            @block.scalar
            def _(act):
                act.sem_inc(sums_copied, 2)
                act.sem_inc(mask_kept, LOADS)

                def exponentials(k, u):
                    act.wait_ge(scores_ready, k + 1)
                    act.wait_ge(masked, k + 1)
                    nc.scalar.activation(exps[:, u % 2, :], ps[:, 2 * (u % 2):2 * (u % 2) + 2, :].rearrange("p b n -> p (b n)"),
                                         ACT.Exp, scale=1.0 / QK_SCALE ** 2).then_inc(exps_ready, 1)

                def step(c, m, u, first, last, no_next):
                    k = PAIRS * c + LOADS * m + u
                    if not (no_next and last):
                        exponentials(k + 1, u + 1)
                    act.wait_ge(masked, SLOTS + k + 1)
                    nc.scalar.activation(mask[:, bass.ds(k * W, W)], probs[:, u, :], ACT.Sign).then_inc(mask_kept, 1)

                def chunk(c, last):
                    steps(act, c, last, step)
                    act.wait_ge(pair_used, SLOTS + PAIRS * (c + 1))
                    act.wait_ge(rows_done, c + 1)
                    for s in range(2):
                        ins = nc.scalar.activation(sums[:, s, :], ps[:, 4 + s, 0:2 * D + 1], ACT.Copy)
                    ins.then_inc(sums_copied, 1)

                act.wait_ge(scores_ready, 1)
                nc.scalar.activation(exps[:, 0, :], ps[:, 0:2, :].rearrange("p b n -> p (b n)"),
                                     ACT.Exp, scale=1.0 / QK_SCALE ** 2).then_inc(exps_ready, 1)
                chunks(act, chunk)

            @block.vector
            def _(dve):
                dve.sem_inc(masked, SLOTS)
                dve.sem_inc(rows_done, 1)

                def step(c, m, u, first, last, no_next):
                    k = PAIRS * c + LOADS * m + u
                    dve.wait_ge(adj_landed[u], 16 * (TURNS * c + m + 1))
                    dve.wait_ge(exps_ready, k + 1)
                    nc.vector.scalar_tensor_tensor(out=probs[:, u, :], in0=adj[:, u, :], scalar=0.0,
                                                   in1=exps[:, u % 2, :], op0=ALU.is_gt, op1=ALU.mult)\
                        .then_inc(masked, 1)
                    dve.wait_ge(masked, SLOTS + k + 1)
                    dve.wait_ge(pair_used, k + 1)
                    nc.vector.tensor_copy(p_hi[:, u % 2, :], probs[:, u, :]).then_inc(hi_ready, 1)

                def chunk(c, last):
                    steps(dve, c, last, step)
                    dve.wait_ge(pair_used, SLOTS + PAIRS * (c + 1))
                    for s in range(2, SUB):
                        ins = nc.vector.tensor_copy(sums[:, s, :], ps[:, 4 + s, 0:2 * D + 1])
                    ins.then_inc(sums_copied, 1)
                    ch = Chain(dve, epilogue_chain, c, EPILOGUE_STEPS)
                    x, feat = x_feat[:, 0, :, :], x_feat[:, 1, :, :]
                    no_edge, den, keep = (t[:, :] for t in cols)
                    dve.wait_ge(sums_copied, 2 * (c + 2))
                    ch.mark(nc.vector.tensor_scalar(no_edge, sums[:, :, D], 0.0, None, ALU.is_le))
                    ch.link(nc.vector.tensor_tensor(sums[:, :, 0:D], sums[:, :, 0:D], sums[:, :, D + 1:], ALU.add))
                    ch.mark(nc.vector.tensor_tensor(den, sums[:, :, D], no_edge, ALU.add))
                    ch.link(nc.vector.tensor_scalar(keep, no_edge, 0.5, 0.5, ALU.mult, ALU.add))
                    ch.link(nc.vector.reciprocal(den, den))
                    ch.link(nc.vector.tensor_scalar(den, den, 0.5, None, ALU.mult))
                    dve.wait_ge(rows_landed, 32 * (c + 1))
                    for s in range(SUB):
                        ch.mark(nc.vector.scalar_tensor_tensor(out=x[:, s, :], in0=feat[:, s, :], scalar=keep[:, s:s + 1],
                                                               in1=x[:, s, :], op0=ALU.mult, op1=ALU.add))
                    ch.wait()
                    for s in range(SUB):
                        rows = sb["x1"][:, bass.ds(c, 1), s * D:(s + 1) * D].rearrange("p a d -> p (a d)")
                        ins = nc.vector.scalar_tensor_tensor(out=rows, in0=sums[:, s, 0:D], scalar=den[:, s:s + 1],
                                                             in1=x[:, s, :], op0=ALU.mult, op1=ALU.add)
                        if s < SUB - 1:
                            ch.mark(ins)
                    ins.then_inc(rows_done, 1)
                    assert ch.n == EPILOGUE_STEPS

                chunks(dve, chunk)

            @block.gpsimd
            def _(pool):
                pool.sem_inc(lo_ready, LOADS)

                def step(c, m, u, first, last, no_next):
                    k = PAIRS * c + LOADS * m + u
                    pool.wait_ge(hi_ready, k + 1)
                    pool.wait_ge(pair_used, k + 1)
                    nc.gpsimd.tensor_tensor(p_lo[:, u % 2, :], probs[:, u, :], p_hi[:, u % 2, :], ALU.subtract)\
                        .then_inc(lo_ready, 1)

                with pool.Fori(0, GROUPS) as c:
                    with pool.Fori(0, TURNS) as m:
                        for u in range(LOADS):
                            step(c, m, u, False, False, False)


def tiles_of(ap):
    return ap.rearrange("p g (s d) -> p (g s) d", d=D)


def row(ap, t):
    return ap[:, bass.ds(t, 1), :].rearrange("p a d -> p (a d)")


def group_of(ap, g):
    return ap[:, bass.ds(g * SUB, SUB), :].rearrange("p s d -> p (s d)")


def mix_shared_experts(nc, io, sb, ps):
    with ExitStack() as ctx:
        buf = lambda name, shape, dt=F32: ctx.enter_context(nc.sbuf_tensor(name, shape, dt))
        sem = lambda name: ctx.enter_context(nc.semaphore(name))
        x1 = tiles_of(sb["x1"][:, :, :])
        xn = buf("xn1", [P, TILES, D])
        stage = buf("stage1", [P, SLOTS, GROUP])
        xT = buf("xT1", [P, SLOTS, GROUP])
        hT = buf("hT1", [P, SLOTS, 2 * FH, GROUP])
        w1, w2 = buf("w1_pair", [P, 2, F]), buf("w2_pair", [P, 2, FH, D])
        b1, b2 = buf("b1_pair", [P, 2, FH]), buf("b2_pair", [P, 2, D])
        gamma, beta = buf("gamma", [P, D]), buf("beta", [P, D])
        wr, br = buf("wr", [P, E]), buf("br", [P, E])
        average = buf("average", [P, P])
        mean_row, mean_column = buf("mean_row", [P, D]), buf("mean_column", [P, P])
        stats = buf("stats1", [P, TILES, 6])
        mean, var, rstd, t0, t1 = (buf(n, [P, TILES])[:, :] for n in ("mean1", "var1", "rstd1", "t10", "t11"))
        route, route_exp = buf("route", [P, E]), buf("route_exp", [P, E])
        top, top_index = buf("top", [P, 8]), buf("top_index", [P, 8], U32)
        share = buf("share", [P, 2])
        a, b = buf("route_a", [P, 1]), buf("route_b", [P, 1])
        bias = buf("bias", [P, D])

        small_in = sem("small_in")
        experts_in = sem("experts_in")
        chain = sem("dve_chain1")
        xn_ready = sem("xn_ready")
        constants_ready = sem("constants_ready")
        beta_added = sem("beta_added")
        mean_ready = sem("mean_ready")
        mean_used = sem("mean_used")
        route_ready = sem("route_ready")
        exp_ready = sem("exp_ready")
        index_ready = sem("index_ready")
        staged = sem("staged")
        turned = sem("turned")
        xT_ready = sem("xT_ready")
        up_ready = sem("up_ready")
        gelu_ready = sem("gelu_ready")
        down_ready = sem("down_ready")
        z_ready = sem("z_ready")
        final_chain = sem("final_chain1")
        FINAL_STEPS = 4

        with nc.Block() as block:

            @block.sync
            def _(sp):
                for to, name in ((wr, "Wr"),):
                    sp.dma_start(to[:, :], io[name]).then_inc(small_in, 16)
                for to, name in ((br, "br"), (gamma, "gamma"), (beta, "beta")):
                    sp.dma_start(to[:, :], io[name].partition_broadcast(P)).then_inc(small_in, 16)
                sp.wait_ge(index_ready, 1)
                for n in range(2):
                    e = sp.value_load(top_index[0:1, n:n + 1], min_val=0, max_val=E - 1)
                    one = bass.ds(e, 1)
                    sp.dma_start(w1[:, n, :], io["W1a"][one, :, :].rearrange("a d f -> (a d) f")).then_inc(experts_in, 16)
                    sp.dma_start(w2[:, n, :, :], io["W2a"][one, :, :].rearrange("a (f p) d -> p (a f) d", p=P)).then_inc(experts_in, 16)
                    sp.dma_start(b1[:, n, :], io["b1a"][one, :, :].rearrange("a p f -> (a p) f")).then_inc(experts_in, 16)
                    sp.dma_start(b2[:, n, :], io["b2a"][one, :].rearrange("a d -> (a d)").partition_broadcast(P)).then_inc(experts_in, 16)
                sp.wait_ge(experts_in, 128)

            @block.gpsimd
            def _(pool):
                nc.gpsimd.memset(average[:, :], 1.0 / N).then_inc(constants_ready, 1)
                pool.wait_ge(constants_ready, 1)
                pool.wait_ge(small_in, 64)
                pool.wait_ge(xn_ready, GROUPS)
                with pool.Fori(0, GROUPS) as g:
                    rows = group_of(x1, g).rearrange("p (s d) -> p s d", d=D)
                    nc.gpsimd.tensor_tensor(rows, rows, beta[:, :].unsqueeze(1).to_broadcast([P, SUB, D]), ALU.add)\
                        .then_inc(beta_added, 1)

            @block.vector
            def _(dve):
                ch = Chain(dve, chain)
                with dve.Fori(0, TILES) as t:
                    nc.vector.bn_stats(stats[:, bass.ds(t, 1), :].rearrange("p a n -> p (a n)"), row(x1, t)).then_inc(chain, 1)
                ch.n = TILES
                ch.wait()
                row_statistics(nc, ch, stats, mean, var, t0, t1)
                ch.link(nc.vector.tensor_scalar(var, var, LN_EPS, None, ALU.add))
                inverse_root(nc, ch, rstd, var, t0, t1)
                with dve.Fori(0, GROUPS) as g:
                    for s in range(SUB):
                        t = g * SUB + s
                        ins = nc.vector.tensor_scalar(row(xn, t), row(x1, t), mean[:, bass.ds(t, 1)], rstd[:, bass.ds(t, 1)],
                                                      ALU.subtract, ALU.mult)
                    ins.then_inc(xn_ready, 1)
                dve.wait_ge(mean_ready, 1)
                nc.vector.tensor_reduce(mean_row[:, :], ps[:, 0, :].rearrange("p (s d) -> p d s", s=SUB), AX.X, ALU.add)\
                    .then_inc(mean_used, 1)
                dve.wait_ge(mean_ready, 2)
                nc.vector.tensor_scalar(mean_column[:, :], ps[:, 1, 0:1].to_broadcast([P, P]), float(N) / P, None, ALU.mult)\
                    .then_inc(mean_used, 1)
                dve.wait_ge(mean_ready, 3)
                dve.wait_ge(small_in, 64)
                r, ex = route[:, :], route_exp[:, :]
                ch.link(nc.vector.tensor_tensor(r, ps[:, 2, 0:E], br[:, :], ALU.add))

                def softmax(x, n, times):
                    e = ex[:, 0:n]
                    ch.link(nc.vector.tensor_reduce(a[:, :], x, AX.X, ALU.max))
                    nc.vector.tensor_scalar(x, x, a[:, :], None, ALU.subtract).then_inc(route_ready, 1)
                    dve.wait_ge(exp_ready, times)
                    ch.link(nc.vector.tensor_reduce(b[:, :], e, AX.X, ALU.add))
                    ch.link(nc.vector.reciprocal(b[:, :], b[:, :]))
                    ch.link(nc.vector.tensor_scalar(x, e, b[:, :], None, ALU.mult))

                softmax(r, E, 1)
                capacity = float(-(-N * 5 // (4 * E)))
                ch.link(nc.vector.tensor_scalar(ex, r, float(N), 1e-30, ALU.mult, ALU.max))
                ch.link(nc.vector.reciprocal(ex, ex))
                ch.link(nc.vector.tensor_scalar(ex, ex, capacity, 1.0, ALU.mult, ALU.min))
                ch.link(nc.vector.tensor_tensor(r, r, ex, ALU.mult))
                softmax(r, E, 2)
                ch.link(nc.vector.max(top[:, :], r))
                nc.vector.max_index(top_index[:, :], top[:, :], r).then_inc(index_ready, 1)
                ch.link(nc.vector.tensor_copy(share[:, :], top[:, 0:2]))
                softmax(share[:, :], 2, 3)
                dve.wait_ge(experts_in, 128)
                for n in range(2):
                    ch.mark(nc.vector.tensor_scalar(w2[:, n, :, :], w2[:, n, :, :], share[:, n:n + 1], None, ALU.mult))
                ch.link(nc.vector.tensor_scalar(bias[:, :], b2[:, 0, :], share[:, 0:1], None, ALU.mult))
                nc.vector.scalar_tensor_tensor(out=bias[:, :], in0=b2[:, 1, :], scalar=share[:, 1:2], in1=bias[:, :],
                                               op0=ALU.mult, op1=ALU.add).then_inc(z_ready, SLOTS)
                dve.wait_ge(z_ready, SLOTS)
                with dve.Fori(0, GROUPS // 2) as i:
                    for u in range(2):
                        g = 2 * i + u
                        dve.wait_ge(turned, SLOTS + g + 1)
                        dve.wait_ge(down_ready, g + 1)
                        nc.vector.tensor_copy(xT[:, u, :], ps[:, u, :]).then_inc(xT_ready, 1)
                        z = group_of(xn, g)
                        zs = xn[:, bass.ds(g * SUB, SUB), :]
                        dve.wait_ge(staged, SLOTS + g + 1)
                        nc.vector.tensor_tensor(zs, zs, bias[:, :].unsqueeze(1).to_broadcast([P, SUB, D]), ALU.add)\
                            .then_inc(z_ready, 1)
                        dve.wait_ge(down_ready, SLOTS + g + 1)
                        dve.wait_ge(z_ready, SLOTS + 2 * g + 1)
                        nc.vector.tensor_tensor(z, ps[:, 6 + u, :], z, ALU.add).then_inc(z_ready, 1)
                        dve.wait_ge(z_ready, SLOTS + 2 * g + 2)
                        for s in range(SUB):
                            t = g * SUB + s
                            ins = nc.vector.bn_stats(stats[:, bass.ds(t, 1), :].rearrange("p a n -> p (a n)"), row(xn, t))
                        ins.then_inc(chain, 1)
                ch.n += GROUPS
                ch.wait()
                row_statistics(nc, ch, stats, mean, var, t0, t1)
                ch.link(nc.vector.tensor_scalar(var, var, LN_EPS, None, ALU.add))
                inverse_root(nc, ch, rstd, var, t0, t1)
                dve.wait_ge(beta_added, GROUPS)
                with dve.Fori(0, GROUPS) as g:
                    fc = Chain(dve, final_chain, g, FINAL_STEPS)
                    for s in range(SUB):
                        t = g * SUB + s
                        ins = nc.vector.tensor_scalar(row(xn, t), row(xn, t), mean[:, bass.ds(t, 1)], rstd[:, bass.ds(t, 1)],
                                                      ALU.subtract, ALU.mult)
                    fc.link(ins)
                    zs = xn[:, bass.ds(g * SUB, SUB), :]
                    fc.link(nc.vector.tensor_tensor(zs, zs, gamma[:, :].unsqueeze(1).to_broadcast([P, SUB, D]), ALU.mult))
                    fc.link(nc.vector.tensor_tensor(group_of(x1, g), group_of(xn, g), group_of(x1, g), ALU.add))
                    for s in range(SUB):
                        t = g * SUB + s
                        ins = nc.vector.bn_stats(sb["stats"][:, bass.ds(t, 1), :].rearrange("p a n -> p (a n)"), row(x1, t))
                    fc.mark(ins)
                    assert fc.n == FINAL_STEPS
                dve.wait_ge(final_chain, FINAL_STEPS * GROUPS)

            @block.scalar
            def _(act):
                act.sem_inc(staged, SLOTS)
                act.sem_inc(gelu_ready, 4)
                for times, (to, x) in enumerate(((route_exp[:, :], route[:, :]), (route_exp[:, :], route[:, :]),
                                                 (route_exp[:, 0:2], share[:, :]))):
                    act.wait_ge(route_ready, times + 1)
                    nc.scalar.activation(to, x, ACT.Exp).then_inc(exp_ready, 1)
                with act.Fori(0, GROUPS // 2) as i:
                    for u in range(2):
                        g = 2 * i + u
                        act.wait_ge(turned, g + 1)
                        nc.scalar.activation(stage[:, u, :], group_of(xn, g), ACT.Copy).then_inc(staged, 1)
                        act.wait_ge(down_ready, g + 1)
                        for n in range(4):
                            act.wait_ge(up_ready, 4 * g + n + 1)
                            nc.scalar.activation(hT[:, u, n, :], ps[:, 2 + n, :], ACT.Gelu, bias=b1[:, n // 2, n % 2:n % 2 + 1])\
                                .then_inc(gelu_ready, 1)

            @block.tensor
            def _(pe):
                pe.sem_inc(turned, SLOTS)
                pe.sem_inc(down_ready, SLOTS)
                pe.wait_ge(constants_ready, 1)
                for g in range(GROUPS):
                    pe.wait_ge(xn_ready, g + 1)
                    ins = nc.tensor.matmul(ps[:, 0, :], average[:, :], xn[:, g * SUB:(g + 1) * SUB, :].rearrange("p s d -> p (s d)"),
                                           start=(g == 0), stop=(g == GROUPS - 1))
                ins.then_inc(mean_ready, 1)
                pe.wait_ge(mean_used, 1)
                nc.tensor.matmul(ps[:, 1, 0:1], mean_row[:, :], average[:, 0:1], start=True, stop=True).then_inc(mean_ready, 1)
                pe.wait_ge(mean_used, 2)
                pe.wait_ge(small_in, 64)
                nc.tensor.matmul(ps[:, 2, 0:E], mean_column[:, :], wr[:, :], start=True, stop=True).then_inc(mean_ready, 1)

                pe.wait_ge(experts_in, 128)
                pe.wait_ge(z_ready, SLOTS)
                with pe.Fori(0, GROUPS // 2) as i:
                    for u in range(2):
                        g = 2 * i + u
                        pe.wait_ge(staged, SLOTS + g + 1)
                        for s in range(SUB):
                            ins = nc.tensor.transpose(ps[:, u, s * P:(s + 1) * P], stage[:, u, s * P:(s + 1) * P], sb["ident"][:, :])
                        ins.then_inc(turned, 1)
                        pe.wait_ge(xT_ready, g + 1)
                        for n in range(4):
                            pe.wait_ge(gelu_ready, 4 * g + n + 1)
                            nc.tensor.matmul(ps[:, 2 + n, :], w1[:, n // 2, (n % 2) * P:(n % 2 + 1) * P], xT[:, u, :],
                                             start=True, stop=True).then_inc(up_ready, 1)
                        pe.wait_ge(gelu_ready, 4 * g + 8)
                        pe.wait_ge(z_ready, 2 * g + 1)
                        for s in range(SUB):
                            for n in range(4):
                                ins = nc.tensor.matmul(ps[:, 6 + u, s * P:(s + 1) * P], hT[:, u, n, s * P:(s + 1) * P],
                                                       w2[:, n // 2, n % 2, :], start=(n == 0), stop=(n == 3))
                        ins.then_inc(down_ready, 1)


def project_nodes(nc, io, sb, ps):
    with ExitStack() as ctx:
        buf = lambda name, shape, dt=F32: ctx.enter_context(nc.sbuf_tensor(name, shape, dt))
        sem = lambda name: ctx.enter_context(nc.semaphore(name))
        x2 = tiles_of(sb["x1"][:, :, :])
        inp = buf("inp", [P, TILES, D + 1])
        stage = buf("stage2", [P, SLOTS, GROUP])
        xT = buf("xT2", [P, SLOTS, GROUP])
        h = buf("h2", [P, SLOTS, SUB, D])
        w, b, a = buf("w_node", [P, D]), buf("b_node", [P, D]), buf("a_node", [P, D])
        mean, var, rstd, t0, t1 = (buf(n, [P, TILES])[:, :] for n in ("mean2", "var2", "rstd2", "t20", "t21"))
        e, h_sum, valid, weight = (buf(n, [P, TILES])[:, :] for n in ("e", "h_sum", "valid", "weight"))
        top, top_all = buf("e_top", [P, 1]), buf("e_top_all", [P, 1])
        parts = sb["parts"][:, :, :].rearrange("p t (k n) -> p t k n", k=3)

        small_in = sem("small_in2")
        chain = sem("dve_chain2")
        group_chain = sem("group_chain2")
        GROUP_STEPS = 2
        staged = sem("staged2")
        turned = sem("turned2")
        xT_ready = sem("xT_ready2")
        inp_ready = sem("inp_ready")
        inp_kept = sem("inp_kept")
        h_biased = sem("h_biased")
        tanh_ready = sem("tanh_ready")
        top_ready = sem("top_ready")
        exponent_ready = sem("exponent_ready")
        exp_ready = sem("exp_ready2")

        with nc.Block() as block:

            @block.sync
            def _(sp):
                sp.dma_start(w[:, :], io["W_node"]).then_inc(small_in, 16)
                sp.dma_start(b[:, :], io["b_node"].partition_broadcast(P)).then_inc(small_in, 16)
                sp.dma_start(a[:, :], io["a_node"].partition_broadcast(P)).then_inc(small_in, 16)
                sp.wait_ge(small_in, 48)

            @block.vector
            def _(dve):
                dve.sem_inc(h_biased, SLOTS)
                dve.sem_inc(xT_ready, SLOTS)
                ch = Chain(dve, chain)
                row_statistics(nc, ch, sb["stats"], mean, var, t0, t1)
                ch.link(nc.vector.tensor_scalar(var, var, LN_EPS, None, ALU.add))
                inverse_root(nc, ch, rstd, var, t0, t1)
                dve.wait_ge(small_in, 48)
                with dve.Fori(0, GROUPS // 2) as i:
                    for u in range(2):
                        g = 2 * i + u
                        dve.wait_ge(turned, g + 1)
                        for s in range(SUB):
                            t = g * SUB + s
                            ins = nc.vector.tensor_scalar(stage[:, u, s * D:(s + 1) * D], row(x2, t), mean[:, bass.ds(t, 1)],
                                                          rstd[:, bass.ds(t, 1)], ALU.subtract, ALU.mult)
                        ins.then_inc(staged, 1)
                        dve.wait_ge(turned, SLOTS + g + 1)
                        nc.vector.tensor_copy(xT[:, u, :], ps[:, u, :]).then_inc(xT_ready, 1)
                        dve.wait_ge(inp_ready, g + 1)
                        dve.wait_ge(inp_kept, g + 1)
                        hu = h[:, u, :, :]
                        nc.vector.tensor_tensor(hu, ps[:, 2 + u, :].rearrange("p (s d) -> p s d", d=D),
                                                b[:, :].unsqueeze(1).to_broadcast([P, SUB, D]), ALU.add).then_inc(h_biased, 1)
                        gc = Chain(dve, group_chain, g, GROUP_STEPS)
                        dve.wait_ge(tanh_ready, g + 1)
                        gc.link(nc.vector.tensor_reduce(h_sum[:, bass.ds(g * SUB, SUB)], hu, AX.X, ALU.add))
                        gc.link(nc.vector.tensor_tensor(hu, hu, a[:, :].unsqueeze(1).to_broadcast([P, SUB, D]), ALU.mult))
                        nc.vector.tensor_reduce(e[:, bass.ds(g * SUB, SUB)], hu, AX.X, ALU.add).then_inc(chain, 1)
                        assert gc.n == GROUP_STEPS
                ch.n += GROUPS
                ch.wait()
                ch.link(nc.vector.tensor_scalar(valid, h_sum, 0.0, None, ALU.not_equal))
                ch.mark(nc.vector.tensor_tensor(t0, e, valid, ALU.mult))
                ch.link(nc.vector.tensor_scalar(t1, valid, 1e30, -1e30, ALU.mult, ALU.add))
                ch.link(nc.vector.tensor_tensor(e, t0, t1, ALU.add))
                nc.vector.tensor_reduce(top[:, :], e, AX.X, ALU.max).then_inc(top_ready, 1)
                dve.wait_ge(top_ready, 2)
                nc.vector.tensor_scalar(e, e, top_all[:, :], None, ALU.subtract).then_inc(exponent_ready, 1)
                dve.wait_ge(exp_ready, 1)
                ch.link(nc.vector.tensor_tensor(weight, weight, valid, ALU.mult))
                dve.wait_ge(inp_kept, GROUPS)
                ch.mark(nc.vector.tensor_tensor(inp[:, :, 0:D], inp[:, :, 0:D], weight.unsqueeze(2).to_broadcast([P, TILES, D]), ALU.mult))
                ch.link(nc.vector.tensor_copy(inp[:, :, D:D + 1], weight.unsqueeze(2)))
                for k in range(3):
                    ch.link(nc.vector.tensor_copy(parts[:, :, k, :], inp[:, :, :]))
                    if k < 2:
                        ch.link(nc.vector.tensor_tensor(inp[:, :, :], inp[:, :, :], parts[:, :, k, :], ALU.subtract))

            @block.gpsimd
            def _(pool):
                pool.wait_ge(top_ready, 1)
                nc.gpsimd.partition_all_reduce(top_all[:, :], top[:, :], P, bass.bass_isa.ReduceOp.max).then_inc(top_ready, 1)

            @block.scalar
            def _(act):
                with act.Fori(0, GROUPS // 2) as i:
                    for u in range(2):
                        g = 2 * i + u
                        act.wait_ge(inp_ready, g + 1)
                        nc.scalar.activation(inp[:, bass.ds(g * SUB, SUB), 0:D], ps[:, 2 + u, :].rearrange("p (s d) -> p s d", d=D),
                                             ACT.Copy).then_inc(inp_kept, 1)
                        act.wait_ge(h_biased, SLOTS + g + 1)
                        nc.scalar.activation(h[:, u, :, :], h[:, u, :, :], ACT.Tanh).then_inc(tanh_ready, 1)
                act.wait_ge(exponent_ready, 1)
                nc.scalar.activation(weight, e, ACT.Exp).then_inc(exp_ready, 1)

            @block.tensor
            def _(pe):
                pe.sem_inc(turned, SLOTS)
                pe.wait_ge(small_in, 48)
                with pe.Fori(0, GROUPS // 2) as i:
                    for u in range(2):
                        g = 2 * i + u
                        pe.wait_ge(staged, g + 1)
                        for s in range(SUB):
                            ins = nc.tensor.transpose(ps[:, u, s * P:(s + 1) * P], stage[:, u, s * P:(s + 1) * P], sb["ident"][:, :])
                        ins.then_inc(turned, 1)
                        pe.wait_ge(xT_ready, SLOTS + g + 1)
                        pe.wait_ge(h_biased, g + 1)
                        for s in range(SUB):
                            ins = nc.tensor.matmul(ps[:, 2 + u, s * D:(s + 1) * D], xT[:, u, s * P:(s + 1) * P], w[:, :],
                                                   start=True, stop=True)
                        ins.then_inc(inp_ready, 1)


def gather_nodes(nc, io, sb, ps):
    with ExitStack() as ctx:
        buf = lambda name, shape, dt=F32: ctx.enter_context(nc.sbuf_tensor(name, shape, dt))
        sem = lambda name: ctx.enter_context(nc.semaphore(name))
        RING = 4
        TURNS = PAIRS // RING
        W = 2 * GROUP
        K = 3 * (D + 1)
        edges = buf("edges", [P, RING, W], BF16)
        sums = buf("sums3", [P, SUB, 3, D + 1])
        parts, mask = sb["parts"], sb["mask"]

        edges_ready = [sem("edges_ready_dve"), sem("edges_ready_act")]
        pair_used = sem("pair_used3")
        sums_copied = sem("sums_copied3")
        rows_done = sem("rows_done3")
        chain = sem("epilogue_chain3")
        STEPS = 11

        def widen(eng, side, c, m):
            for u in range(side, RING, 2):
                k = PAIRS * c + RING * m + u
                eng.wait_ge(pair_used, k + 1)
                source = mask[:, bass.ds(k * W, W)]
                if side == 0:
                    ins = nc.vector.tensor_copy(edges[:, u, :], source)
                else:
                    ins = nc.scalar.activation(edges[:, u, :], source, ACT.Copy)
                ins.then_inc(edges_ready[side], 1)

        with nc.Block() as block:

            @block.tensor
            def _(pe):
                pe.sem_inc(pair_used, RING)

                def turn(c, cu, m, first, last):
                    for u in range(RING):
                        k = PAIRS * c + RING * m + u
                        pe.wait_ge(edges_ready[u % 2], TURNS * 2 * c + 2 * m + u // 2 + 1)
                        for h in range(2):
                            rows = parts[:, bass.ds((RING * m + u) * 2 + h, 1), :].rearrange("p a n -> p (a n)")
                            for s in range(SUB):
                                ins = nc.tensor.matmul(ps[:, 4 * cu + s, 0:K], edges[:, u, h * GROUP + s * P:h * GROUP + (s + 1) * P],
                                                       rows, start=first and u == 0 and h == 0,
                                                       stop=last and u == RING - 1 and h == 1)
                        ins.then_inc(pair_used, 1)

                with pe.Fori(0, GROUPS // 2) as i:
                    for cu in range(2):
                        c = 2 * i + cu
                        pe.wait_ge(sums_copied, c + 1)
                        turn(c, cu, 0, True, False)
                        with pe.Fori(1, TURNS - 1) as m:
                            turn(c, cu, m, False, False)
                        turn(c, cu, TURNS - 1, False, True)

            @block.scalar
            def _(act):
                act.sem_inc(sums_copied, SLOTS)
                with act.Fori(0, GROUPS // 2) as i:
                    for cu in range(2):
                        c = 2 * i + cu
                        with act.Fori(0, TURNS) as m:
                            widen(act, 1, c, m)
                        act.wait_ge(pair_used, RING + PAIRS * (c + 1))
                        act.wait_ge(rows_done, c + 1)
                        for s in range(SUB):
                            ins = nc.scalar.activation(sums[:, s, :, :].rearrange("p k n -> p (k n)"), ps[:, 4 * cu + s, 0:K], ACT.Copy)
                        ins.then_inc(sums_copied, 1)

            @block.vector
            def _(dve):
                dve.sem_inc(rows_done, 1)
                with dve.Fori(0, GROUPS) as c:
                    with dve.Fori(0, TURNS) as m:
                        widen(dve, 0, c, m)
                    ch = Chain(dve, chain, c, STEPS)
                    dve.wait_ge(sums_copied, SLOTS + c + 1)
                    a, b, d = (sums[:, :, k, :] for k in range(3))
                    ch.link(nc.vector.tensor_tensor(b, b, d, ALU.add))
                    ch.link(nc.vector.tensor_tensor(a, a, b, ALU.add))
                    den = sums[:, :, 1, D]
                    ch.link(nc.vector.tensor_scalar(den, sums[:, :, 0, D], 1e-30, None, ALU.max))
                    ch.link(nc.vector.reciprocal(den, den))
                    x = sb["x1"]
                    for s in range(SUB):
                        rows = x[:, bass.ds(c, 1), s * D:(s + 1) * D].rearrange("p a d -> p (a d)")
                        ins = nc.vector.scalar_tensor_tensor(out=rows, in0=sums[:, s, 0, 0:D], scalar=sums[:, s, 1, D:D + 1],
                                                             in1=rows, op0=ALU.mult, op1=ALU.add)
                        if s < SUB - 1:
                            ch.mark(ins)
                    ins.then_inc(rows_done, 1)
                    dve.wait_ge(rows_done, c + 2)
                    for s in range(SUB):
                        t = c * SUB + s
                        ins = nc.vector.bn_stats(sb["stats"][:, bass.ds(t, 1), :].rearrange("p a n -> p (a n)"), row(tiles_of(x[:, :, :]), t))
                        ch.mark(ins)
                    assert ch.n == STEPS
                dve.wait_ge(chain, STEPS * GROUPS)


def mix_routed_experts(nc, io, sb, ps):
    with ExitStack() as ctx:
        buf = lambda name, shape, dt=F32: ctx.enter_context(nc.sbuf_tensor(name, shape, dt))
        sem = lambda name: ctx.enter_context(nc.semaphore(name))
        x3 = tiles_of(sb["x1"][:, :, :])
        w1, w2 = buf("w1_all", [P, E, F]), buf("w2_all", [P, E, FH, D])
        b1, b2 = buf("b1_all", [P, E, FH]), buf("b2_all", [E, D])
        wg, bg = buf("wg", [P, E]), buf("bg", [P, E])
        stage = buf("stage3", [P, SLOTS, GROUP])
        xT = buf("xT3", [P, SLOTS, GROUP])
        hT = buf("hT3", [P, SLOTS, FH, GROUP])
        mean, var, rstd, t0, t1 = (buf(n, [P, TILES])[:, :] for n in ("mean3", "var3", "rstd3", "t30", "t31"))
        iota = buf("iota", [P, E])
        iota_i = buf("iota_i", [P, E], I32)
        gates, top = buf("gates", [P, SUB, E]), buf("gates_top", [P, SUB, 8])
        index_i, index = buf("gates_index_i", [P, SUB, 8], U32), buf("gates_index", [P, SUB, 8])
        chosen = buf("chosen", [P, SUB, E])
        chosenT = buf("chosenT", [E, SUB * P])

        weights_in = sem("weights_in")
        chain = sem("dve_chain3")
        group_chain = sem("group_chain3")
        iota_ready = sem("iota_ready")
        staged = sem("staged3")
        turned = sem("turned3")
        xT_ready = sem("xT_ready3")
        gates_ready = sem("gates_ready")
        gates_biased = sem("gates_biased")
        chosen_ready = sem("chosen_ready")
        chosen_turned = sem("chosen_turned")
        chosenT_ready = sem("chosenT_ready")
        bias_ready = sem("bias_ready")
        up_ready = sem("up_ready3")
        gelu_ready = sem("gelu_ready3")
        down_ready = sem("down_ready3")
        added = sem("added")
        rows_ready = sem("rows_ready")
        rows_out = sem("rows_out")
        GROUP_STEPS = 5 * SUB + 1

        with nc.Block() as block:

            @block.sync
            def _(sp):
                sp.dma_start(w1[:, :, :], io["W1b"].rearrange("e d f -> d e f")).then_inc(weights_in, 16)
                sp.dma_start(w2[:, :, :, :], io["W2b"].rearrange("e (f p) d -> p e f d", p=P)).then_inc(weights_in, 16)
                sp.dma_start(b1[:, :, :], io["b1b"].rearrange("e p f -> p e f")).then_inc(weights_in, 16)
                sp.dma_start(b2[:, :], io["b2b"]).then_inc(weights_in, 16)
                sp.dma_start(wg[:, :], io["Wg"]).then_inc(weights_in, 16)
                sp.dma_start(bg[:, :], io["bg"].partition_broadcast(P)).then_inc(weights_in, 16)
                with sp.Fori(0, GROUPS) as g:
                    sp.wait_ge(rows_ready, g + 1)
                    sp.dma_start(io["out"].rearrange("(t p) d -> p t d", p=P)[:, bass.ds(g * SUB, SUB), :],
                                 x3[:, bass.ds(g * SUB, SUB), :]).then_inc(rows_out, 16)
                sp.wait_ge(rows_out, 16 * GROUPS)

            @block.gpsimd
            def _(pool):
                nc.gpsimd.iota(iota_i[:, :], [[1, E]], base=0, channel_multiplier=0).then_inc(iota_ready, 1)
                pool.wait_ge(iota_ready, 1)
                nc.gpsimd.tensor_copy(iota[:, :], iota_i[:, :]).then_inc(iota_ready, 1)

            @block.vector
            def _(dve):
                dve.sem_inc(added, SLOTS)
                ch = Chain(dve, chain)
                row_statistics(nc, ch, sb["stats"], mean, var, t0, t1)
                ch.link(nc.vector.tensor_scalar(var, var, LN_EPS, None, ALU.add))
                inverse_root(nc, ch, rstd, var, t0, t1)
                dve.wait_ge(weights_in, 96)
                dve.wait_ge(iota_ready, 2)
                with dve.Fori(0, GROUPS // 2) as i:
                    for u in range(2):
                        g = 2 * i + u
                        dve.wait_ge(turned, g + 1)
                        for s in range(SUB):
                            t = g * SUB + s
                            ins = nc.vector.tensor_scalar(stage[:, u, s * D:(s + 1) * D], row(x3, t), mean[:, bass.ds(t, 1)],
                                                          rstd[:, bass.ds(t, 1)], ALU.subtract, ALU.mult)
                        ins.then_inc(staged, 1)
                        dve.wait_ge(turned, SLOTS + g + 1)
                        nc.vector.tensor_copy(xT[:, u, :], ps[:, 0, :]).then_inc(xT_ready, 1)
                        dve.wait_ge(gates_ready, g + 1)
                        gc = Chain(dve, group_chain, g, GROUP_STEPS)
                        gc.link(nc.vector.tensor_tensor(gates[:, :, :], ps[:, 7, 0:SUB * E].rearrange("p (s e) -> p s e", e=E),
                                                        bg[:, :].unsqueeze(1).to_broadcast([P, SUB, E]), ALU.add))
                        dve.sem_inc(gates_biased, 1)
                        for s in range(SUB):
                            gc.mark(nc.vector.max(top[:, s, :], gates[:, s, :]))
                        gc.wait()
                        dve.sem_inc(gates_biased, 1)
                        for s in range(SUB):
                            gc.mark(nc.vector.max_index(index_i[:, s, :], top[:, s, :], gates[:, s, :]))
                        gc.wait()
                        for s in range(SUB):
                            gc.mark(nc.vector.tensor_copy(index[:, s, :], index_i[:, s, :]))
                        gc.wait()
                        for s in range(SUB):
                            gc.mark(nc.vector.tensor_scalar(chosen[:, s, :], iota[:, :], index[:, s, 0:1], None, ALU.is_equal))
                        gc.wait()
                        for s in range(SUB):
                            ins = nc.vector.scalar_tensor_tensor(out=chosen[:, s, :], in0=iota[:, :], scalar=index[:, s, 1:2],
                                                                 in1=chosen[:, s, :], op0=ALU.is_equal, op1=ALU.add)
                            gc.mark(ins)
                        gc.wait()
                        dve.sem_inc(chosen_ready, 1)
                        assert gc.n == GROUP_STEPS
                        dve.wait_ge(chosen_turned, g + 1)
                        nc.vector.tensor_copy(chosenT[:, :], ps[0:E, 7, :]).then_inc(chosenT_ready, 1)
                        rows = lambda s: row(x3, g * SUB + s)
                        dve.wait_ge(bias_ready, g + 1)
                        nc.vector.tensor_tensor(group_of(x3, g), ps[:, 7, :], group_of(x3, g), ALU.add).then_inc(added, 1)
                        for e in range(E):
                            dve.wait_ge(down_ready, SLOTS + E * g + e + 1)
                            dve.wait_ge(added, SLOTS + (E + 1) * g + e + 1)
                            for s in range(SUB):
                                ins = nc.vector.scalar_tensor_tensor(out=rows(s), in0=ps[:, 5 + e % 2, s * D:(s + 1) * D],
                                                                     scalar=chosen[:, s, e:e + 1], in1=rows(s),
                                                                     op0=ALU.mult, op1=ALU.add)
                            ins.then_inc(added, 1)
                        dve.wait_ge(added, SLOTS + (E + 1) * (g + 1))
                        dve.sem_inc(rows_ready, 1)

            @block.scalar
            def _(act):
                act.sem_inc(gelu_ready, 2 * FH)
                with act.Fori(0, GROUPS) as g:
                    for e in range(E):
                        for f in range(FH):
                            n = e * FH + f
                            act.wait_ge(up_ready, E * FH * g + n + 1)
                            act.wait_ge(down_ready, E * g + e + 1)
                            nc.scalar.activation(hT[:, e % 2, f, :], ps[:, 1 + n % 4, :], ACT.Gelu, bias=b1[:, e, f:f + 1])\
                                .then_inc(gelu_ready, 1)

            @block.tensor
            def _(pe):
                pe.sem_inc(turned, SLOTS)
                pe.sem_inc(down_ready, SLOTS)
                pe.wait_ge(weights_in, 96)
                with pe.Fori(0, GROUPS // 2) as i:
                    for u in range(2):
                        g = 2 * i + u
                        pe.wait_ge(staged, g + 1)
                        for s in range(SUB):
                            ins = nc.tensor.transpose(ps[:, 0, s * P:(s + 1) * P], stage[:, u, s * P:(s + 1) * P], sb["ident"][:, :])
                        ins.then_inc(turned, 1)
                        pe.wait_ge(xT_ready, g + 1)
                        for s in range(SUB):
                            ins = nc.tensor.matmul(ps[:, 7, s * E:(s + 1) * E], xT[:, u, s * P:(s + 1) * P], wg[:, :],
                                                   start=True, stop=True)
                        ins.then_inc(gates_ready, 1)

                        def up(e):
                            for f in range(FH):
                                n = e * FH + f
                                pe.wait_ge(gelu_ready, E * FH * g + n + 1)
                                nc.tensor.matmul(ps[:, 1 + n % 4, :], w1[:, e, f * P:(f + 1) * P], xT[:, u, :],
                                                 start=True, stop=True).then_inc(up_ready, 1)

                        def down(e):
                            pe.wait_ge(gelu_ready, 2 * FH + E * FH * g + (e + 1) * FH)
                            pe.wait_ge(added, (E + 1) * g + e + (2 if e >= 2 else 1))
                            for s in range(SUB):
                                for f in range(FH):
                                    ins = nc.tensor.matmul(ps[:, 5 + e % 2, s * D:(s + 1) * D], hT[:, e % 2, f, s * P:(s + 1) * P],
                                                           w2[:, e, f, :], start=(f == 0), stop=(f == FH - 1))
                            ins.then_inc(down_ready, 1)

                        up(0)
                        pe.wait_ge(chosen_ready, g + 1)
                        for s in range(SUB):
                            ins = nc.tensor.transpose(ps[0:E, 7, s * P:(s + 1) * P], chosen[:, s, :], sb["ident"][:, :])
                        ins.then_inc(chosen_turned, 1)
                        pe.wait_ge(chosenT_ready, g + 1)
                        for s in range(SUB):
                            ins = nc.tensor.matmul(ps[:, 7, s * D:(s + 1) * D], chosenT[:, s * P:(s + 1) * P], b2[:, :],
                                                   start=True, stop=True)
                        ins.then_inc(bias_ready, 1)
                        for e in range(E):
                            if e + 1 < E:
                                up(e + 1)
                            down(e)


def build(nc, io):
    with ExitStack() as ctx:
        sb = {}
        sb["x1"] = ctx.enter_context(nc.sbuf_tensor("x1", [P, GROUPS, GROUP], F32))
        sb["stats"] = ctx.enter_context(nc.sbuf_tensor("stats", [P, TILES, 6], F32))
        sb["ident"] = ctx.enter_context(nc.sbuf_tensor("ident", [P, P], F32))
        ps = ctx.enter_context(nc.psum_tensor("ps", [P, 8, 512], F32))
        with ExitStack() as graph:
            sb["mask"] = graph.enter_context(nc.sbuf_tensor("mask", [P, TILES * N], mybir.dt.uint8))
            with ExitStack() as attention:
                sb["v16"] = attention.enter_context(nc.sbuf_tensor("v16", [P, TILES, 2 * D + 1], F16))
                sb["qT"] = attention.enter_context(nc.sbuf_tensor("qT", [P, 2, N], F16))
                prepare(nc, io, sb, ps)
                attend(nc, io, sb, ps)
            mix_shared_experts(nc, io, sb, ps)
            with ExitStack() as rows:
                sb["parts"] = rows.enter_context(nc.sbuf_tensor("parts", [P, TILES, 3 * (D + 1)], BF16))
                project_nodes(nc, io, sb, ps)
                gather_nodes(nc, io, sb, ps)
        mix_routed_experts(nc, io, sb, ps)


def kernel(x, adj, L0_gnn_Wq, L0_gnn_Wk, L0_ffn_Wr, L0_ffn_br, L0_ffn_W1, L0_ffn_b1, L0_ffn_W2, L0_ffn_b2,
           L0_ffn_gamma, L0_ffn_beta, L1_gnn_W, L1_gnn_b, L1_gnn_a, L1_ffn_Wg, L1_ffn_bg, L1_ffn_W1, L1_ffn_b1,
           L1_ffn_W2, L1_ffn_b2):
    import concourse.bacc as bacc
    from concourse.bass_utils import run_bass_kernel_spmd

    laid = {
        "x": x,
        "adj": np.asarray(adj).T.reshape(PAIRS, 2, P, GROUPS, GROUP).transpose(3, 0, 2, 1, 4)
                 .reshape(GROUPS * PAIRS, P, 2 * GROUP),
        "WqT": np.asarray(L0_gnn_Wq).T,
        "WkT": np.asarray(L0_gnn_Wk).T,
        "Wr": L0_ffn_Wr, "br": L0_ffn_br, "gamma": L0_ffn_gamma, "beta": L0_ffn_beta,
        "W1a": L0_ffn_W1, "b1a": np.asarray(L0_ffn_b1).reshape(E, FH, P).transpose(0, 2, 1), "W2a": L0_ffn_W2, "b2a": L0_ffn_b2,
        "W_node": L1_gnn_W, "b_node": L1_gnn_b, "a_node": np.asarray(L1_gnn_a).reshape(D),
        "Wg": L1_ffn_Wg, "bg": L1_ffn_bg,
        "W1b": L1_ffn_W1, "b1b": np.asarray(L1_ffn_b1).reshape(E, FH, P).transpose(0, 2, 1), "W2b": L1_ffn_W2, "b2b": L1_ffn_b2,
    }
    nc = bacc.Bacc("TRN2", target_bir_lowering=False, num_devices=1, dynamic_dma_scratch_size=1024)
    arrays, io = {}, {}
    for name, a in laid.items():
        a = np.ascontiguousarray(a)
        arrays[f"in_{name}"] = a
        io[name] = nc.dram_tensor(f"in_{name}", a.shape, mybir.dt.from_np(a.dtype), kind="ExternalInput").ap()
    io["feat"] = nc.dram_tensor("feat_spill", [P, GROUPS, SUB, D], F32).ap()
    io["out"] = nc.dram_tensor("out", [N, D], F32, kind="ExternalOutput").ap()
    build(nc, io)
    return run_bass_kernel_spmd(nc, [arrays], core_ids=[0]).results[0]["out"]
```

```python
from contextlib import ExitStack

import numpy as np

import concourse.bass as bass
from concourse import mybir

F32 = mybir.dt.float32
F32R = mybir.dt.float32r
F16 = mybir.dt.float16
BF16 = mybir.dt.bfloat16
FP8 = mybir.dt.float8e4
I32 = mybir.dt.int32
U32 = mybir.dt.uint32
ALU = mybir.AluOpType
ACT = mybir.ActivationFunctionType
AX = mybir.AxisListType

P = 128
N = 4096
D = 128
TILES = N // P
SUB = 4
GROUP = SUB * P
GROUPS = N // GROUP
PAIRS = TILES // 2
E = 8
F = 256
FH = F // P
LN_EPS = 1e-5
QK_SCALE = 64.0
V_SCALE = 16.0
SLOTS = 2
LEVEL = 60.0
MOST_LEVELS = 240
EPILOGUE_STEPS = 14


class Chain:

    def __init__(self, eng, sem, turn=0, per_turn=0):
        self.eng, self.sem, self.base, self.n = eng, sem, turn * per_turn, 0

    def mark(self, ins):
        self.n += 1
        ins.then_inc(self.sem, 1)

    def wait(self):
        self.eng.wait_ge(self.sem, self.base + self.n)

    def link(self, ins):
        self.mark(ins)
        self.wait()


def row_statistics(nc, ch, stats, mean, var, t0, t1):
    me, mo, ve, vo = (stats[:, :, i] for i in (1, 4, 2, 5))
    ch.mark(nc.vector.tensor_tensor(mean, me, mo, ALU.add))
    ch.mark(nc.vector.tensor_tensor(t0, me, mo, ALU.subtract))
    ch.link(nc.vector.tensor_tensor(t1, ve, vo, ALU.add))
    ch.mark(nc.vector.tensor_scalar(mean, mean, 0.5, None, ALU.mult))
    ch.link(nc.vector.scalar_tensor_tensor(out=t0, in0=t0, scalar=0.25, in1=t0, op0=ALU.mult, op1=ALU.mult))
    ch.link(nc.vector.scalar_tensor_tensor(out=var, in0=t1, scalar=1.0 / D, in1=t0, op0=ALU.mult, op1=ALU.add))


def inverse_root(nc, ch, y, v, t0, t1):
    ch.mark(nc.vector.tensor_scalar(y.bitcast(I32), v.bitcast(I32), -0.5, float(0x5F3759DF), ALU.mult, ALU.add))
    ch.link(nc.vector.tensor_scalar(t1, v, -0.5, None, ALU.mult))
    for _ in range(3):
        ch.link(nc.vector.tensor_tensor(t0, t1, y, ALU.mult))
        ch.link(nc.vector.tensor_tensor(t0, t0, y, ALU.mult))
        ch.link(nc.vector.scalar_tensor_tensor(out=y, in0=t0, scalar=1.5, in1=y, op0=ALU.add, op1=ALU.mult))


def tiles_of(ap):
    return ap.rearrange("p g (s d) -> p (g s) d", d=D)


def row(ap, t):
    return ap[:, bass.ds(t, 1), :].rearrange("p a d -> p (a d)")


def group_of(ap, g):
    return ap[:, bass.ds(g * SUB, SUB), :].rearrange("p s d -> p (s d)")


def pipelined(eng, count, stages):
    lag = max(l for l, _ in stages)

    def step(i, parity):
        for l, stage in stages:
            if not isinstance(i, int) or 0 <= i - l < count:
                stage(i - l, (parity - l) % 2)

    lead = lag + lag % 2
    for i in range(lead):
        step(i, i % 2)
    with eng.Fori(lead // 2, count // 2) as h:
        for parity in range(2):
            step(2 * h + parity, parity)
    for i in range(count, count + lag):
        step(i, i % 2)


def prepare(nc, io, sb, ps):
    with ExitStack() as ctx:
        small = lambda name, shape, dt=F32: ctx.enter_context(nc.sbuf_tensor(name, shape, dt))
        sem = lambda name: ctx.enter_context(nc.semaphore(name))
        room = sb["mask"][:, :].bitcast(F32)
        x = room[:, 0:4096].rearrange("p (t d) -> p t d", d=D)
        qk = room[:, 4096:12288].rearrange("p (g n) -> p g n", g=GROUPS)
        square = room[:, 12288:14336].rearrange("p (u s h) -> p u s h", u=2, h=D)
        feat = room[:, 14336:15360].rearrange("p (u s d) -> p u s d", u=2, d=D)
        featT = room[:, 15360:16384].rearrange("p (u n) -> p u n", u=2)
        unit = room[:, 16384:18432].rearrange("p (u s h) -> p u s h", u=2, h=D)
        w_qk = small("w_qk", [P, 2 * D])
        stats = small("stats0", [P, TILES, 6])
        mean, var, rstd, t0, t1 = (small(n, [P, TILES]) for n in ("mean0", "var0", "rstd0", "t00", "t01"))
        ss, rnorm, t2, t3 = (small(n, [P, 2 * TILES]) for n in ("ss", "rnorm", "t02", "t03"))
        hi, lo = sb["qT"][:, 0, :], sb["qT"][:, 1, :]
        kt = sb["x1"][:, :, :].bitcast(F16)
        v16 = sb["v16"]

        x_in = [sem(f"x_in{i}") for i in range(4)]
        w_in = sem("w_in")
        ident_ready = sem("ident_ready")
        dve_chain = sem("dve_chain0")
        feat_ready = sem("feat_ready")
        feat_turned = sem("feat_turned")
        v_hi_ready = sem("v_hi_ready")
        v_lo_ready = sem("v_lo_ready")
        feat_spilled = [sem(f"feat_spilled{u}") for u in range(2)]
        featT_ready = sem("featT_ready")
        qk_ready = sem("qk_ready")
        qk_copied = sem("qk_copied")
        qk_squared = sem("qk_squared")
        ss_ready = sem("ss_ready")
        norms_ready = sem("norms_ready")
        unit_q_ready = sem("unit_q_ready")
        unit_k_ready = sem("unit_k_ready")
        unit_turned = sem("unit_turned")
        unit_hi = sem("unit_hi")
        unit_lo = sem("unit_lo")

        def scale_rows(eng, unit_engine, g, u, side):
            eng.wait_ge(unit_turned, g + 1)
            halves = lambda ap: ap.rearrange("p (s b) h -> p s b h", b=2)[:, :, side, :]
            scale = rnorm[:, bass.ds(g * 8, 8)].rearrange("p (s b) -> p s b", b=2)[:, :, side].unsqueeze(2).to_broadcast([P, SUB, D])
            raw = qk[:, bass.ds(g, 1), :].rearrange("p a (s h) -> p (a s) h", h=D)
            unit_engine.tensor_tensor(halves(unit[:, u, :, :]), halves(raw), scale, ALU.mult)\
                .then_inc((unit_q_ready, unit_k_ready)[side], 1)

        with nc.Block() as block:

            @block.sync
            def _(sp):
                x_tiles = io["x"].rearrange("(t p) d -> p t d", p=P)
                for i in range(4):
                    sp.dma_start(x[:, 8 * i:8 * i + 8, :], x_tiles[:, 8 * i:8 * i + 8, :]).then_inc(x_in[i], 16)
                sp.dma_start(w_qk[:, 0:D], io["WqT"]).then_inc(w_in, 16)
                sp.dma_start(w_qk[:, D:2 * D], io["WkT"]).then_inc(w_in, 16)
                with sp.Fori(0, GROUPS // 2) as i:
                    for u in range(2):
                        sp.wait_ge(feat_ready, 2 * i + u + 1)
                        sp.dma_start(io["feat"][:, 2 * i + u, :, :], feat[:, u, :, :]).then_inc(feat_spilled[u], 16)
                for u in range(2):
                    sp.wait_ge(feat_spilled[u], 16 * (SLOTS // 2) + 16 * (GROUPS // 2))

            @block.gpsimd
            def _(pool):
                nc.gpsimd.memset(sb["ident"][:, :], 0.0).then_inc(ident_ready, 1)
                pool.wait_ge(ident_ready, 1)
                nc.gpsimd.affine_select(out=sb["ident"][:, :], in_=sb["ident"][:, :], compare_op=ALU.not_equal,
                                        fill=1.0, base=0, pattern=[[-1, P]], channel_multiplier=1).then_inc(ident_ready, 1)
                nc.gpsimd.memset(v16[:, :, D:D + 1], V_SCALE).then_inc(ident_ready, 1)
                pool.wait_ge(norms_ready, 1)
                pool.wait_ge(qk_copied, GROUPS)
                pipelined(pool, GROUPS, [(0, lambda g, u: scale_rows(pool, nc.gpsimd, g, u, 1))])

            @block.vector
            def _(dve):
                dve.sem_inc(v_lo_ready, SLOTS)
                dve.sem_inc(unit_lo, SLOTS)
                dve.sem_inc(ss_ready, SLOTS)
                for u in range(2):
                    dve.sem_inc(feat_spilled[u], 16)
                ch = Chain(dve, dve_chain)
                for t in range(TILES):
                    if t % 8 == 0:
                        dve.wait_ge(x_in[t // 8], 16)
                    ins = nc.vector.bn_stats(stats[:, t, :], x[:, t, :])
                ch.link(ins)
                row_statistics(nc, ch, stats, mean[:, :], var[:, :], t0[:, :], t1[:, :])
                ch.link(nc.vector.tensor_scalar(var[:, :], var[:, :], LN_EPS, None, ALU.add))
                inverse_root(nc, ch, rstd[:, :], var[:, :], t0[:, :], t1[:, :])

                def normalize(g, u):
                    dve.wait_ge(feat_turned, g + 1)
                    dve.wait_ge(v_hi_ready, g + 1)
                    dve.wait_ge(v_lo_ready, g + 1)
                    dve.wait_ge(feat_spilled[u], 8 * (g - u) + 16)
                    for s in range(SUB):
                        t = bass.ds(g * SUB + s, 1)
                        ins = nc.vector.tensor_scalar(feat[:, u, s, :], row(x, g * SUB + s), mean[:, t], rstd[:, t],
                                                      ALU.subtract, ALU.mult)
                    ins.then_inc(feat_ready, 1)

                def low_values(g, u):
                    dve.wait_ge(v_hi_ready, SLOTS + g + 1)
                    dve.wait_ge(feat_ready, g + 1)
                    tiles = bass.ds(g * SUB, SUB)
                    nc.vector.scalar_tensor_tensor(out=v16[:, tiles, D + 1:], in0=feat[:, u, :, :], scalar=V_SCALE,
                                                   in1=v16[:, tiles, 0:D], op0=ALU.mult, op1=ALU.subtract)\
                        .then_inc(v_lo_ready, 1)

                def keep_turned(g, u):
                    dve.wait_ge(feat_turned, SLOTS + g + 1)
                    nc.vector.tensor_copy(featT[:, u, :], ps[:, u, :]).then_inc(featT_ready, 1)

                def sum_squares(g, u):
                    dve.wait_ge(qk_squared, SLOTS + g + 1)
                    nc.vector.tensor_reduce(ss[:, bass.ds(g * 8, 8)], square[:, u, :, :], AX.X, ALU.add)\
                        .then_inc(ss_ready, 1)

                pipelined(dve, GROUPS, [(0, normalize), (1, low_values), (1, keep_turned), (2, sum_squares)])
                dve.wait_ge(ss_ready, SLOTS + GROUPS)
                ch.link(nc.vector.tensor_scalar(ss[:, :], ss[:, :], 1e-8, None, ALU.max))
                inverse_root(nc, ch, rnorm[:, :], ss[:, :], t2[:, :], t3[:, :])
                nc.vector.tensor_scalar(rnorm[:, :], rnorm[:, :], QK_SCALE, None, ALU.mult).then_inc(norms_ready, 1)
                dve.wait_ge(norms_ready, 1)
                dve.wait_ge(qk_copied, GROUPS)

                def low_halves(g, u):
                    dve.wait_ge(unit_turned, SLOTS + g + 1)
                    dve.wait_ge(unit_hi, g + 1)
                    cols = bass.ds(g * GROUP, GROUP)
                    nc.vector.tensor_tensor(lo[:, cols], ps[:, 2 * u, :], hi[:, cols], ALU.subtract)
                    k_lo = kt[:, bass.ds(g, 1), GROUP:].rearrange("p a n -> p (a n)")
                    k_hi = kt[:, bass.ds(g, 1), 0:GROUP].rearrange("p a n -> p (a n)")
                    nc.vector.tensor_tensor(k_lo, ps[:, 2 * u + 1, :], k_hi, ALU.subtract).then_inc(unit_lo, 1)

                pipelined(dve, GROUPS, [(0, lambda g, u: scale_rows(dve, nc.vector, g, u, 0)), (1, low_halves)])
                dve.wait_ge(unit_lo, SLOTS + GROUPS)

            @block.scalar
            def _(act):
                act.sem_inc(v_hi_ready, SLOTS)
                act.sem_inc(qk_squared, SLOTS)
                def high_values(g, u):
                    act.wait_ge(feat_ready, g + 1)
                    nc.scalar.activation(v16[:, bass.ds(g * SUB, SUB), 0:D], feat[:, u, :, :], ACT.Copy, scale=V_SCALE)\
                        .then_inc(v_hi_ready, 1)

                def keep_products(g, u):
                    act.wait_ge(qk_ready, g + 1)
                    products = ps[:, 2 + 2 * u:4 + 2 * u, :].rearrange("p b n -> p (b n)")
                    nc.scalar.activation(qk[:, bass.ds(g, 1), :].rearrange("p a n -> p (a n)"), products, ACT.Copy)\
                        .then_inc(qk_copied, 1)
                    act.wait_ge(ss_ready, g + 1)
                    nc.scalar.activation(square[:, u, :, :].rearrange("p s h -> p (s h)"), products, ACT.Square)\
                        .then_inc(qk_squared, 1)

                pipelined(act, GROUPS, [(0, high_values), (1, keep_products)])

                def high_halves(g, u):
                    act.wait_ge(unit_turned, SLOTS + g + 1)
                    nc.scalar.activation(hi[:, bass.ds(g * GROUP, GROUP)], ps[:, 2 * u, :], ACT.Copy)
                    nc.scalar.activation(kt[:, bass.ds(g, 1), 0:GROUP].rearrange("p a n -> p (a n)"),
                                         ps[:, 2 * u + 1, :], ACT.Copy).then_inc(unit_hi, 1)

                pipelined(act, GROUPS, [(0, high_halves)])
                act.wait_ge(unit_hi, GROUPS)

            @block.tensor
            def _(pe):
                pe.sem_inc(feat_turned, SLOTS)
                pe.sem_inc(unit_turned, SLOTS)
                pe.wait_ge(ident_ready, 2)
                pe.wait_ge(w_in, 32)
                def turn_features(g, u):
                    pe.wait_ge(feat_ready, g + 1)
                    for s in range(SUB):
                        ins = nc.tensor.transpose(ps[:, u, s * P:(s + 1) * P], feat[:, u, s, :], sb["ident"][:, :])
                    ins.then_inc(feat_turned, 1)

                def project(g, u):
                    pe.wait_ge(featT_ready, g + 1)
                    pe.wait_ge(qk_squared, g + 1)
                    for s in range(SUB):
                        bank, half = 2 + 2 * u + s // 2, s % 2
                        ins = nc.tensor.matmul(ps[:, bank, half * 2 * D:(half + 1) * 2 * D],
                                               featT[:, u, s * P:(s + 1) * P], w_qk[:, :], start=True, stop=True)
                    ins.then_inc(qk_ready, 1)

                pipelined(pe, GROUPS, [(0, turn_features), (1, project)])

                def turn_units(g, u):
                    pe.wait_ge(unit_q_ready, g + 1)
                    pe.wait_ge(unit_k_ready, g + 1)
                    pe.wait_ge(unit_lo, g + 1)
                    for side in range(2):
                        for s in range(SUB):
                            ins = nc.tensor.transpose(ps[:, 2 * u + side, s * P:(s + 1) * P],
                                                      unit[:, u, 2 * s + side, :], sb["ident"][:, :])
                    ins.then_inc(unit_turned, 1)

                pipelined(pe, GROUPS, [(0, turn_units)])


def attend(nc, io, sb, ps):
    with ExitStack() as ctx:
        buf = lambda name, shape, dt=F32: ctx.enter_context(nc.sbuf_tensor(name, shape, dt))
        sem = lambda name: ctx.enter_context(nc.semaphore(name))
        LOADS = 4
        TURNS = PAIRS // LOADS
        W = 2 * GROUP
        adj = buf("adj", [P, LOADS, W], I32)
        exps = buf("exps", [P, SLOTS, W])
        probs = adj[:, :, :].bitcast(F32)
        p_hi = buf("p_hi", [P, SLOTS, W], F16)
        p_lo = buf("p_lo", [P, SLOTS, W], F16)
        sums = buf("sums", [P, SUB, 2 * D + 1])
        x_feat = buf("x_feat", [P, 2, SUB, D])
        cols = [buf(n, [P, SUB]) for n in ("no_edge", "denominator", "keep")]
        qT, v16, mask = sb["qT"], sb["v16"], sb["mask"]
        kT = sb["x1"][:, :, :].bitcast(F16)

        adj_landed = [sem(f"adj_landed{u}") for u in range(LOADS)]
        rows_landed = sem("rows_landed")
        scores_ready = sem("scores_ready")
        exps_ready = sem("exps_ready")
        masked = sem("masked")
        mask_kept = sem("mask_kept")
        hi_ready = sem("hi_ready")
        lo_ready = sem("lo_ready")
        pair_used = sem("pair_used")
        sums_copied = sem("sums_copied")
        rows_done = sem("rows_done")
        epilogue_chain = sem("epilogue_chain")

        def chunks(eng, chunk):
            with eng.Fori(0, GROUPS - 1) as c:
                chunk(c, False)
            chunk(GROUPS - 1, True)

        def steps(eng, c, last_chunk, step):
            def turn(m, first, last):
                for u in range(LOADS):
                    step(c, m, u, first and u == 0, last and u == LOADS - 1, last_chunk and last and u >= LOADS - 2)
            turn(0, True, False)
            with eng.Fori(1, TURNS - 1) as m:
                turn(m, False, False)
            turn(TURNS - 1, False, True)

        with nc.Block() as block:

            @block.sync
            def _(sp):
                def turn(c, m):
                    for u in range(LOADS):
                        step = PAIRS * c + LOADS * m + u
                        sp.wait_ge(lo_ready, step + 1)
                        sp.wait_ge(mask_kept, step + 1)
                        sp.dma_start(adj[:, u, :], io["adj"][bass.ds(step, 1), :, :].rearrange("a p n -> (a p) n"))\
                            .then_inc(adj_landed[u], 16)

                with sp.Fori(0, GROUPS) as c:
                    turn(c, 0)
                    sp.wait_ge(rows_done, c + 1)
                    for r, rows in enumerate((io["x"].rearrange("(g s p) d -> p g s d", p=P, s=SUB), io["feat"])):
                        sp.dma_start(x_feat[:, r, :, :], rows[:, bass.ds(c, 1), :, :].rearrange("p a s d -> p (a s) d"))\
                            .then_inc(rows_landed, 16)
                    with sp.Fori(1, TURNS) as m:
                        turn(c, m)

            @block.tensor
            def _(pe):
                pe.sem_inc(pair_used, SLOTS)

                def scores(c, jp, u):
                    for h in range(2):
                        j = bass.ds(jp * 2 * P + h * P, P)
                        out = ps[:, 2 * (u % 2) + h, :]
                        for n, (q_half, k_half) in enumerate(((0, 0), (0, 1), (1, 0))):
                            keys = kT[:, bass.ds(c, 1), k_half * GROUP:(k_half + 1) * GROUP].rearrange("p a n -> p (a n)")
                            ins = nc.tensor.matmul(out, qT[:, q_half, j], keys, start=(n == 0), stop=(n == 2))
                    ins.then_inc(scores_ready, 1)

                def step(c, m, u, first, last, no_next):
                    jp = LOADS * m + u
                    k = PAIRS * c + jp
                    if not no_next:
                        pe.wait_ge(exps_ready, k + 1)
                        if isinstance(m, int) and jp + 2 >= PAIRS:
                            scores(c + 1, jp + 2 - PAIRS, u)
                        else:
                            scores(c, jp + 2, u)
                    pe.wait_ge(hi_ready, k + 1)
                    pe.wait_ge(lo_ready, LOADS + k + 1)
                    if first:
                        pe.wait_ge(sums_copied, 2 * (c + 1))
                    for h in range(2):
                        v = v16[:, bass.ds(2 * jp + h, 1), :].rearrange("p a n -> p (a n)")
                        for s in range(SUB):
                            i = slice(h * GROUP + s * P, h * GROUP + (s + 1) * P)
                            start, stop = first and h == 0, last and h == 1
                            for half in ("hi", "lo") if start else ("lo", "hi"):
                                if half == "hi":
                                    ins = nc.tensor.matmul(ps[:, 4 + s, 0:2 * D + 1], p_hi[:, u % 2, i], v,
                                                           start=start, stop=stop)
                                else:
                                    ins = nc.tensor.matmul(ps[:, 4 + s, 0:D + 1], p_lo[:, u % 2, i], v[:, 0:D + 1],
                                                           start=False, stop=False)
                    ins.then_inc(pair_used, 1)

                scores(0, 0, 0)
                scores(0, 1, 1)
                chunks(pe, lambda c, last: steps(pe, c, last, step))

            @block.scalar
            def _(act):
                act.sem_inc(sums_copied, 2)
                act.sem_inc(mask_kept, LOADS)

                def exponentials(k, u):
                    act.wait_ge(scores_ready, k + 1)
                    act.wait_ge(masked, k + 1)
                    nc.scalar.activation(exps[:, u % 2, :], ps[:, 2 * (u % 2):2 * (u % 2) + 2, :].rearrange("p b n -> p (b n)"),
                                         ACT.Exp, scale=1.0 / QK_SCALE ** 2).then_inc(exps_ready, 1)

                def step(c, m, u, first, last, no_next):
                    k = PAIRS * c + LOADS * m + u
                    if not (no_next and last):
                        exponentials(k + 1, u + 1)
                    act.wait_ge(masked, SLOTS + k + 1)
                    nc.scalar.activation(mask[:, bass.ds(k * W, W)], probs[:, u, :], ACT.Sign).then_inc(mask_kept, 1)

                def chunk(c, last):
                    steps(act, c, last, step)
                    act.wait_ge(pair_used, SLOTS + PAIRS * (c + 1))
                    act.wait_ge(rows_done, c + 1)
                    for s in range(2):
                        ins = nc.scalar.activation(sums[:, s, :], ps[:, 4 + s, 0:2 * D + 1], ACT.Copy)
                    ins.then_inc(sums_copied, 1)

                act.wait_ge(scores_ready, 1)
                nc.scalar.activation(exps[:, 0, :], ps[:, 0:2, :].rearrange("p b n -> p (b n)"),
                                     ACT.Exp, scale=1.0 / QK_SCALE ** 2).then_inc(exps_ready, 1)
                chunks(act, chunk)

            @block.vector
            def _(dve):
                dve.sem_inc(masked, SLOTS)
                dve.sem_inc(rows_done, 1)

                def step(c, m, u, first, last, no_next):
                    k = PAIRS * c + LOADS * m + u
                    dve.wait_ge(adj_landed[u], 16 * (TURNS * c + m + 1))
                    dve.wait_ge(exps_ready, k + 1)
                    nc.vector.scalar_tensor_tensor(out=probs[:, u, :], in0=adj[:, u, :], scalar=0.0,
                                                   in1=exps[:, u % 2, :], op0=ALU.is_gt, op1=ALU.mult)\
                        .then_inc(masked, 1)
                    dve.wait_ge(masked, SLOTS + k + 1)
                    dve.wait_ge(pair_used, k + 1)
                    nc.vector.tensor_copy(p_hi[:, u % 2, :], probs[:, u, :]).then_inc(hi_ready, 1)

                def chunk(c, last):
                    steps(dve, c, last, step)
                    dve.wait_ge(pair_used, SLOTS + PAIRS * (c + 1))
                    for s in range(2, SUB):
                        ins = nc.vector.tensor_copy(sums[:, s, :], ps[:, 4 + s, 0:2 * D + 1])
                    ins.then_inc(sums_copied, 1)
                    ch = Chain(dve, epilogue_chain, c, EPILOGUE_STEPS)
                    x, feat = x_feat[:, 0, :, :], x_feat[:, 1, :, :]
                    no_edge, den, keep = (t[:, :] for t in cols)
                    dve.wait_ge(sums_copied, 2 * (c + 2))
                    ch.mark(nc.vector.tensor_scalar(no_edge, sums[:, :, D], 0.0, None, ALU.is_le))
                    ch.link(nc.vector.tensor_tensor(sums[:, :, 0:D], sums[:, :, 0:D], sums[:, :, D + 1:], ALU.add))
                    ch.mark(nc.vector.tensor_tensor(den, sums[:, :, D], no_edge, ALU.add))
                    ch.link(nc.vector.tensor_scalar(keep, no_edge, 0.5, 0.5, ALU.mult, ALU.add))
                    ch.link(nc.vector.reciprocal(den, den))
                    ch.link(nc.vector.tensor_scalar(den, den, 0.5, None, ALU.mult))
                    dve.wait_ge(rows_landed, 32 * (c + 1))
                    for s in range(SUB):
                        ch.mark(nc.vector.scalar_tensor_tensor(out=x[:, s, :], in0=feat[:, s, :], scalar=keep[:, s:s + 1],
                                                               in1=x[:, s, :], op0=ALU.mult, op1=ALU.add))
                    ch.wait()
                    for s in range(SUB):
                        rows = sb["x1"][:, bass.ds(c, 1), s * D:(s + 1) * D].rearrange("p a d -> p (a d)")
                        ins = nc.vector.scalar_tensor_tensor(out=rows, in0=sums[:, s, 0:D], scalar=den[:, s:s + 1],
                                                             in1=x[:, s, :], op0=ALU.mult, op1=ALU.add)
                        if s < SUB - 1:
                            ch.mark(ins)
                    ins.then_inc(rows_done, 1)
                    dve.wait_ge(rows_done, c + 2)
                    for s in range(SUB):
                        t = c * SUB + s
                        ins = nc.vector.bn_stats(sb["stats"][:, bass.ds(t, 1), :].rearrange("p a n -> p (a n)"), row(tiles_of(sb["x1"][:, :, :]), t))
                    ch.mark(ins)
                    assert ch.n == EPILOGUE_STEPS

                chunks(dve, chunk)
                dve.wait_ge(epilogue_chain, EPILOGUE_STEPS * GROUPS)

            @block.gpsimd
            def _(pool):
                pool.sem_inc(lo_ready, LOADS)

                def step(c, m, u, first, last, no_next):
                    k = PAIRS * c + LOADS * m + u
                    pool.wait_ge(hi_ready, k + 1)
                    pool.wait_ge(pair_used, k + 1)
                    nc.gpsimd.tensor_tensor(p_lo[:, u % 2, :], probs[:, u, :], p_hi[:, u % 2, :], ALU.subtract)\
                        .then_inc(lo_ready, 1)

                with pool.Fori(0, GROUPS) as c:
                    with pool.Fori(0, TURNS) as m:
                        for u in range(LOADS):
                            step(c, m, u, False, False, False)


def mix_shared_experts(nc, io, sb, ps):
    with ExitStack() as ctx:
        buf = lambda name, shape, dt=F32: ctx.enter_context(nc.sbuf_tensor(name, shape, dt))
        sem = lambda name: ctx.enter_context(nc.semaphore(name))
        x1 = tiles_of(sb["x1"][:, :, :])
        xn = buf("xn1", [P, TILES, D])
        xT_hi, xT_lo = buf("xT1_hi", [P, GROUPS, GROUP], F32R), buf("xT1_lo", [P, GROUPS, GROUP], F32R)
        hT = buf("hT1", [P, SLOTS, 2 * FH, GROUP])
        w1, w2 = buf("w1_pair", [P, 2, F]), buf("w2_pair", [P, 2, FH, D])
        w1_hi, w1_lo = buf("w1_pair_hi", [P, 2, F], F32R), buf("w1_pair_lo", [P, 2, F], F32R)
        b1, b2 = buf("b1_pair", [P, 2, FH]), buf("b2_pair", [P, 2, D])
        gamma, beta = buf("gamma", [P, D]), buf("beta", [P, D])
        wr, br = buf("wr", [P, E]), buf("br", [P, E])
        average = buf("average", [P, P])
        mean_row, mean_column = buf("mean_row", [P, D]), buf("mean_column", [P, P])
        mean, var, rstd, t0, t1 = (buf(n, [P, TILES])[:, :] for n in ("mean1", "var1", "rstd1", "t10", "t11"))
        route, route_exp = buf("route", [P, E]), buf("route_exp", [P, E])
        top, top_index = buf("top", [P, 8]), buf("top_index", [P, 8], U32)
        share = buf("share", [P, 2])
        a, b = buf("route_a", [P, 1]), buf("route_b", [P, 1])
        bias = buf("bias", [P, D])
        DOWN_BANK, UP_BANK, TURN_BANK = 0, 2, 6

        small_in = sem("small_in")
        w1_in, experts_in = sem("w1_in1"), sem("experts_in")
        chain = sem("dve_chain1")
        xn_ready = sem("xn_ready")
        average_ready = sem("average_ready")
        beta_added = sem("beta_added")
        mean_ready = sem("mean_ready")
        mean_used = sem("mean_used")
        route_ready = sem("route_ready")
        exp_ready = sem("exp_ready")
        index_ready = sem("index_ready")
        turned = sem("turned")
        xT_hi_ready, xT_lo_ready = sem("xT_hi_ready"), sem("xT_lo_ready")
        w1_hi_ready, weights_ready = sem("w1_hi_ready1"), sem("weights_ready")
        up_ready = sem("up_ready")
        gelu_ready = sem("gelu_ready")
        down_ready = sem("down_ready")
        biased = sem("biased")
        z_ready = sem("z_ready")
        z_measured = sem("z_measured")
        norm_ready = sem("norm_ready")
        z_normal = sem("z_normal")
        z_scaled = sem("z_scaled")
        x2_ready = sem("x2_ready")
        x2_measured = sem("x2_measured")

        with nc.Block() as block:

            @block.sync
            def _(sp):
                sp.dma_start(wr[:, :], io["Wr"]).then_inc(small_in, 16)
                for to, name in ((br, "br"), (gamma, "gamma"), (beta, "beta")):
                    sp.dma_start(to[:, :], io[name].partition_broadcast(P)).then_inc(small_in, 16)
                sp.wait_ge(index_ready, 1)
                experts = [bass.ds(sp.value_load(top_index[0:1, n:n + 1], min_val=0, max_val=E - 1), 1) for n in range(2)]
                for n, one in enumerate(experts):
                    sp.dma_start(w1[:, n, :], io["W1a"][one, :, :].rearrange("a d f -> (a d) f")).then_inc(w1_in, 16)
                for n, one in enumerate(experts):
                    sp.dma_start(w2[:, n, :, :], io["W2a"][one, :, :].rearrange("a (f p) d -> p (a f) d", p=P)).then_inc(experts_in, 16)
                    sp.dma_start(b1[:, n, :], io["b1a"][one, :, :].rearrange("a p f -> (a p) f")).then_inc(experts_in, 16)
                    sp.dma_start(b2[:, n, :], io["b2a"][one, :].rearrange("a d -> (a d)").partition_broadcast(P)).then_inc(experts_in, 16)
                sp.wait_ge(experts_in, 96)

            @block.gpsimd
            def _(pool):
                nc.gpsimd.memset(average[:, :], 1.0 / N).then_inc(average_ready, 1)
                pool.wait_ge(small_in, 64)
                pool.wait_ge(xn_ready, GROUPS)
                spread = lambda v: v[:, :].unsqueeze(1).to_broadcast([P, SUB, D])
                tiles = lambda x, g: x[:, bass.ds(g * SUB, SUB), :]
                with pool.Fori(0, GROUPS) as g:
                    nc.gpsimd.tensor_tensor(tiles(x1, g), tiles(x1, g), spread(beta), ALU.add).then_inc(beta_added, 1)
                pool.wait_ge(turned, SLOTS + GROUPS)
                pool.wait_ge(weights_ready, 1)
                with pool.Fori(0, GROUPS) as g:
                    nc.gpsimd.tensor_tensor(tiles(xn, g), tiles(xn, g), spread(bias), ALU.add).then_inc(biased, 1)
                with pool.Fori(0, GROUPS) as g:
                    pool.wait_ge(z_normal, g + 1)
                    nc.gpsimd.tensor_tensor(tiles(xn, g), tiles(xn, g), spread(gamma), ALU.mult).then_inc(z_scaled, 1)

            @block.vector
            def _(dve):
                dve.sem_inc(xT_lo_ready, SLOTS)
                dve.sem_inc(z_ready, SLOTS)
                ch = Chain(dve, chain)
                row_statistics(nc, ch, sb["stats"], mean, var, t0, t1)
                ch.link(nc.vector.tensor_scalar(var, var, LN_EPS, None, ALU.add))
                inverse_root(nc, ch, rstd, var, t0, t1)
                with dve.Fori(0, GROUPS) as g:
                    for s in range(SUB):
                        t = g * SUB + s
                        ins = nc.vector.tensor_scalar(row(xn, t), row(x1, t), mean[:, bass.ds(t, 1)], rstd[:, bass.ds(t, 1)],
                                                      ALU.subtract, ALU.mult)
                    ins.then_inc(xn_ready, 1)
                dve.wait_ge(mean_ready, 1)
                nc.vector.tensor_reduce(mean_row[:, :], ps[:, 0, :].rearrange("p (s d) -> p d s", s=SUB), AX.X, ALU.add)\
                    .then_inc(mean_used, 1)
                dve.wait_ge(mean_ready, 2)
                nc.vector.tensor_scalar(mean_column[:, :], ps[:, 1, 0:1].to_broadcast([P, P]), float(N) / P, None, ALU.mult)\
                    .then_inc(mean_used, 1)
                dve.wait_ge(mean_ready, 3)
                dve.wait_ge(small_in, 64)
                r, ex = route[:, :], route_exp[:, :]
                ch.link(nc.vector.tensor_tensor(r, ps[:, 2, 0:E], br[:, :], ALU.add))

                def softmax(x, n, times):
                    e = ex[:, 0:n]
                    ch.link(nc.vector.tensor_reduce(a[:, :], x, AX.X, ALU.max))
                    nc.vector.tensor_scalar(x, x, a[:, :], None, ALU.subtract).then_inc(route_ready, 1)
                    dve.wait_ge(exp_ready, times)
                    ch.link(nc.vector.tensor_reduce(b[:, :], e, AX.X, ALU.add))
                    ch.link(nc.vector.reciprocal(b[:, :], b[:, :]))
                    ch.link(nc.vector.tensor_scalar(x, e, b[:, :], None, ALU.mult))

                softmax(r, E, 1)
                capacity = float(-(-N * 5 // (4 * E)))
                ch.link(nc.vector.tensor_scalar(ex, r, float(N), 1e-30, ALU.mult, ALU.max))
                ch.link(nc.vector.reciprocal(ex, ex))
                ch.link(nc.vector.tensor_scalar(ex, ex, capacity, 1.0, ALU.mult, ALU.min))
                ch.link(nc.vector.tensor_tensor(r, r, ex, ALU.mult))
                softmax(r, E, 2)
                ch.link(nc.vector.max(top[:, :], r))
                nc.vector.max_index(top_index[:, :], top[:, :], r).then_inc(index_ready, 1)
                ch.link(nc.vector.tensor_copy(share[:, :], top[:, 0:2]))

                def keep_low(g, u):
                    dve.wait_ge(xT_hi_ready, g + 1)
                    nc.vector.tensor_tensor(xT_lo[:, bass.ds(g, 1), :].rearrange("p a n -> p (a n)"), ps[:, TURN_BANK + u, :],
                                            xT_hi[:, bass.ds(g, 1), :].rearrange("p a n -> p (a n)"), ALU.subtract)\
                        .then_inc(xT_lo_ready, 1)

                pipelined(dve, GROUPS, [(0, keep_low)])
                softmax(share[:, :], 2, 3)
                dve.wait_ge(experts_in, 96)
                for n in range(2):
                    ch.mark(nc.vector.tensor_scalar(w2[:, n, :, :], w2[:, n, :, :], share[:, n:n + 1], None, ALU.mult))
                ch.link(nc.vector.tensor_scalar(bias[:, :], b2[:, 0, :], share[:, 0:1], None, ALU.mult))
                ch.link(nc.vector.scalar_tensor_tensor(out=bias[:, :], in0=b2[:, 1, :], scalar=share[:, 1:2], in1=bias[:, :],
                                                       op0=ALU.mult, op1=ALU.add))
                dve.wait_ge(w1_hi_ready, 1)
                nc.vector.tensor_tensor(w1_lo[:, :, :], w1[:, :, :], w1_hi[:, :, :], ALU.subtract).then_inc(weights_ready, 1)

                def add_outputs(g, u):
                    dve.wait_ge(down_ready, SLOTS + g + 1)
                    dve.wait_ge(biased, g + 1)
                    nc.vector.tensor_tensor(group_of(xn, g), ps[:, DOWN_BANK + u, :], group_of(xn, g), ALU.add).then_inc(z_ready, 1)

                stats = sb["stats"]

                def measure_z(g, u):
                    dve.wait_ge(z_ready, SLOTS + g + 1)
                    for s in range(SUB):
                        t = g * SUB + s
                        ins = nc.vector.bn_stats(stats[:, bass.ds(t, 1), :].rearrange("p a n -> p (a n)"), row(xn, t))
                    ins.then_inc(z_measured, 1)

                pipelined(dve, GROUPS, [(0, add_outputs), (1, measure_z)])
                dve.wait_ge(z_measured, GROUPS)
                row_statistics(nc, ch, stats, mean, var, t0, t1)
                ch.link(nc.vector.tensor_scalar(var, var, LN_EPS, None, ALU.add))
                inverse_root(nc, ch, rstd, var, t0, t1)
                nc.vector.scalar_tensor_tensor(out=mean, in0=mean, scalar=-1.0, in1=rstd, op0=ALU.mult, op1=ALU.mult)\
                    .then_inc(norm_ready, 1)
                dve.wait_ge(beta_added, GROUPS)

                def add_rows(g, u):
                    dve.wait_ge(z_scaled, g + 1)
                    nc.vector.tensor_tensor(group_of(x1, g), group_of(xn, g), group_of(x1, g), ALU.add).then_inc(x2_ready, 1)

                def measure_x2(g, u):
                    dve.wait_ge(x2_ready, g + 1)
                    for s in range(SUB):
                        t = g * SUB + s
                        ins = nc.vector.bn_stats(stats[:, bass.ds(t, 1), :].rearrange("p a n -> p (a n)"), row(x1, t))
                    ins.then_inc(x2_measured, 1)

                pipelined(dve, GROUPS, [(0, add_rows), (1, measure_x2)])
                dve.wait_ge(x2_measured, GROUPS)

            @block.scalar
            def _(act):
                def exponential(times, to, x):
                    act.wait_ge(route_ready, times)
                    nc.scalar.activation(to, x, ACT.Exp).then_inc(exp_ready, 1)

                act.sem_inc(gelu_ready, 4)
                exponential(1, route_exp[:, :], route[:, :])
                exponential(2, route_exp[:, :], route[:, :])

                def keep_high(g, u):
                    act.wait_ge(turned, SLOTS + g + 1)
                    nc.scalar.activation(xT_hi[:, bass.ds(g, 1), :].rearrange("p a n -> p (a n)"), ps[:, TURN_BANK + u, :], ACT.Copy)\
                        .then_inc(xT_hi_ready, 1)

                pipelined(act, GROUPS, [(0, keep_high)])
                exponential(3, route_exp[:, 0:2], share[:, :])
                act.wait_ge(w1_in, 32)
                nc.scalar.activation(w1_hi[:, :, :], w1[:, :, :], ACT.Copy).then_inc(w1_hi_ready, 1)
                act.wait_ge(experts_in, 96)

                def gelus(g, u):
                    act.wait_ge(down_ready, g + 1)
                    for n in range(4):
                        act.wait_ge(up_ready, 4 * g + n + 1)
                        nc.scalar.activation(hT[:, u, n, :], ps[:, UP_BANK + n, :], ACT.Gelu, bias=b1[:, n // 2, n % 2:n % 2 + 1])\
                            .then_inc(gelu_ready, 1)

                pipelined(act, GROUPS, [(0, gelus)])
                act.wait_ge(norm_ready, 1)
                with act.Fori(0, GROUPS) as g:
                    for s in range(SUB):
                        t = g * SUB + s
                        ins = nc.scalar.activation(row(xn, t), row(xn, t), ACT.Identity, bias=mean[:, bass.ds(t, 1)],
                                                   scale=rstd[:, bass.ds(t, 1)])
                    ins.then_inc(z_normal, 1)

            @block.tensor
            def _(pe):
                pe.sem_inc(turned, SLOTS)
                pe.sem_inc(down_ready, SLOTS)
                pe.wait_ge(average_ready, 1)
                rows = lambda g: xn[:, g * SUB:(g + 1) * SUB, :].rearrange("p s d -> p (s d)")
                for g in range(GROUPS):
                    pe.wait_ge(xn_ready, g + 1)
                    ins = nc.tensor.matmul(ps[:, 0, :], average[:, :], rows(g), start=(g == 0), stop=(g == GROUPS - 1))
                ins.then_inc(mean_ready, 1)
                pe.wait_ge(mean_used, 1)
                nc.tensor.matmul(ps[:, 1, 0:1], mean_row[:, :], average[:, 0:1], start=True, stop=True).then_inc(mean_ready, 1)
                pe.wait_ge(mean_used, 2)
                pe.wait_ge(small_in, 64)
                nc.tensor.matmul(ps[:, 2, 0:E], mean_column[:, :], wr[:, :], start=True, stop=True).then_inc(mean_ready, 1)
                for g in range(GROUPS):
                    pe.wait_ge(xT_lo_ready, g + 1)
                    for s in range(SUB):
                        ins = nc.tensor.transpose(ps[:, TURN_BANK + g % 2, s * P:(s + 1) * P], xn[:, g * SUB + s, :], sb["ident"][:, :])
                    ins.then_inc(turned, 1)
                pe.wait_ge(weights_ready, 1)
                pe.wait_ge(xT_lo_ready, SLOTS + GROUPS)

                def up(g, u):
                    for n in range(4):
                        pe.wait_ge(gelu_ready, 4 * g + n + 1)
                        part = lambda w: w[:, n // 2, (n % 2) * P:(n % 2 + 1) * P]
                        token = lambda x: x[:, bass.ds(g, 1), :].rearrange("p a n -> p (a n)")
                        out = ps[:, UP_BANK + n, :]
                        nc.tensor.matmul(out, part(w1_lo), token(xT_hi), start=True, stop=False)
                        nc.tensor.matmul(out, part(w1_hi), token(xT_lo), start=False, stop=False)
                        nc.tensor.matmul(out, part(w1_hi), token(xT_hi), start=False, stop=True).then_inc(up_ready, 1)

                def down(g, u):
                    pe.wait_ge(gelu_ready, 4 * g + 8)
                    pe.wait_ge(z_ready, g + 1)
                    for s in range(SUB):
                        for n in range(4):
                            ins = nc.tensor.matmul(ps[:, DOWN_BANK + u, s * P:(s + 1) * P], hT[:, u, n, s * P:(s + 1) * P],
                                                   w2[:, n // 2, n % 2, :], start=(n == 0), stop=(n == 3))
                    ins.then_inc(down_ready, 1)

                pipelined(pe, GROUPS, [(0, up), (1, down)])


def project_nodes(nc, io, sb, ps):
    with ExitStack() as ctx:
        buf = lambda name, shape, dt=F32: ctx.enter_context(nc.sbuf_tensor(name, shape, dt))
        sem = lambda name: ctx.enter_context(nc.semaphore(name))
        x2 = tiles_of(sb["x1"][:, :, :])
        inp, e, valid = sb["inp"], sb["e"][:, :], sb["valid"][:, :]
        stage = buf("stage2", [P, SLOTS, GROUP])
        xT = buf("xT2", [P, SLOTS, GROUP])
        hT = buf("hT2", [P, SLOTS, GROUP])
        w, b, a = buf("w_node", [P, D]), buf("b_node", [P, 1]), buf("a_and_one", [P, 2])
        mean, var, rstd, t0, t1 = (buf(n, [P, TILES])[:, :] for n in ("mean2", "var2", "rstd2", "t20", "t21"))
        e_sum = buf("e_and_sum", [P, TILES, 2])
        ends, ends_all = buf("ends", [P, 2]), buf("ends_all", [P, 2])
        TURN_BANK, ROW_BANK, COLUMN_BANK, SCORE_BANK = 0, 2, 4, 6

        small_in = sem("small_in2")
        ones_ready = sem("ones_ready")
        chain = sem("dve_chain2")
        staged = sem("staged2")
        turned = sem("turned2")
        xT_ready = sem("xT_ready2")
        projected = sem("projected")
        inp_kept = sem("inp_kept")
        tanh_ready = sem("tanh_ready")
        scored = sem("scored")
        scores_kept = sem("scores_kept")
        ends_ready = sem("ends_ready")

        with nc.Block() as block:

            @block.sync
            def _(sp):
                sp.dma_start(w[:, :], io["W_node"]).then_inc(small_in, 16)
                sp.dma_start(b[:, :], io["b_node"]).then_inc(small_in, 16)
                sp.dma_start(a[:, 0:1], io["a_node"]).then_inc(small_in, 16)

            @block.gpsimd
            def _(pool):
                nc.gpsimd.memset(a[:, 1:2], 1.0).then_inc(ones_ready, 1)
                nc.gpsimd.memset(inp[:, :, D:D + 1], 1.0).then_inc(ones_ready, 1)
                nc.gpsimd.memset(sb["todo"][:, :], 1.0).then_inc(ones_ready, 1)
                pool.wait_ge(ends_ready, 1)
                nc.gpsimd.partition_all_reduce(ends_all[:, :], ends[:, :], P, bass.bass_isa.ReduceOp.max).then_inc(ends_ready, 1)

            @block.vector
            def _(dve):
                dve.sem_inc(scores_kept, SLOTS)
                ch = Chain(dve, chain)
                row_statistics(nc, ch, sb["stats"], mean, var, t0, t1)
                ch.link(nc.vector.tensor_scalar(var, var, LN_EPS, None, ALU.add))
                inverse_root(nc, ch, rstd, var, t0, t1)

                def normalize(g, u):
                    dve.wait_ge(turned, g + 1)
                    for s in range(SUB):
                        t = g * SUB + s
                        ins = nc.vector.tensor_scalar(stage[:, u, s * D:(s + 1) * D], row(x2, t), mean[:, bass.ds(t, 1)],
                                                      rstd[:, bass.ds(t, 1)], ALU.subtract, ALU.mult)
                    ins.then_inc(staged, 1)

                def keep_turned(g, u):
                    dve.wait_ge(turned, SLOTS + g + 1)
                    dve.wait_ge(projected, g + 1)
                    nc.vector.tensor_copy(xT[:, u, :], ps[:, TURN_BANK + u, :]).then_inc(xT_ready, 1)

                def keep_scores(g, u):
                    dve.wait_ge(scored, SLOTS + g + 1)
                    nc.vector.tensor_copy(e_sum[:, bass.ds(g * SUB, SUB), :].rearrange("p s n -> p (s n)"),
                                          ps[:, SCORE_BANK + u, 0:2 * SUB]).then_inc(scores_kept, 1)

                pipelined(dve, GROUPS, [(0, normalize), (1, keep_turned), (3, keep_scores)])
                dve.wait_ge(scores_kept, SLOTS + GROUPS)
                ch.link(nc.vector.tensor_scalar(valid, e_sum[:, :, 1], 0.0, None, ALU.not_equal))
                ch.mark(nc.vector.tensor_tensor(t0, e_sum[:, :, 0], valid, ALU.mult))
                ch.link(nc.vector.tensor_scalar(t1, valid, 1e30, -1e30, ALU.mult, ALU.add))
                ch.mark(nc.vector.tensor_tensor(e, t0, t1, ALU.add))
                ch.link(nc.vector.tensor_tensor(t0, t1, t0, ALU.subtract))
                ch.mark(nc.vector.tensor_reduce(ends[:, 0:1], e, AX.X, ALU.max))
                nc.vector.tensor_reduce(ends[:, 1:2], t0, AX.X, ALU.max).then_inc(ends_ready, 1)
                dve.wait_ge(ends_ready, 2)
                ch.mark(nc.vector.tensor_scalar(e, e, ends_all[:, 0:1], None, ALU.subtract))
                span = t1[:, 0:1]
                ch.link(nc.vector.tensor_tensor(span, ends_all[:, 0:1], ends_all[:, 1:2], ALU.add))
                ch.link(nc.vector.tensor_scalar(span, span, 1.0 / LEVEL, 0.5, ALU.mult, ALU.add))
                ch.link(nc.vector.tensor_scalar(span, span, 1.0, float(MOST_LEVELS), ALU.max, ALU.min))
                ch.link(nc.vector.tensor_copy(sb["levels"][:, :], span))

            @block.scalar
            def _(act):
                act.sem_inc(inp_kept, SLOTS)
                act.wait_ge(small_in, 48)

                def keep_projection(g, u):
                    act.wait_ge(projected, SLOTS + g + 1)
                    act.wait_ge(scored, g + 1)
                    nc.scalar.activation(hT[:, u, :], ps[:, COLUMN_BANK + u, :], ACT.Tanh, bias=b[:, 0:1]).then_inc(tanh_ready, 1)
                    nc.scalar.activation(inp[:, bass.ds(g * SUB, SUB), 0:D], ps[:, ROW_BANK + u, :].rearrange("p (s d) -> p s d", d=D),
                                         ACT.Copy).then_inc(inp_kept, 1)

                pipelined(act, GROUPS, [(0, keep_projection)])
                act.wait_ge(inp_kept, SLOTS + GROUPS)

            @block.tensor
            def _(pe):
                pe.sem_inc(turned, SLOTS)
                pe.sem_inc(projected, SLOTS)
                pe.sem_inc(scored, SLOTS)
                pe.wait_ge(small_in, 48)
                pe.wait_ge(ones_ready, 1)

                def turn(g, u):
                    pe.wait_ge(staged, g + 1)
                    for s in range(SUB):
                        ins = nc.tensor.transpose(ps[:, TURN_BANK + u, s * P:(s + 1) * P], stage[:, u, s * P:(s + 1) * P], sb["ident"][:, :])
                    ins.then_inc(turned, 1)

                def project(g, u):
                    pe.wait_ge(xT_ready, g + 1)
                    pe.wait_ge(inp_kept, g + 1)
                    nc.tensor.matmul(ps[:, COLUMN_BANK + u, :], w[:, :], xT[:, u, :], start=True, stop=True)
                    for s in range(SUB):
                        ins = nc.tensor.matmul(ps[:, ROW_BANK + u, s * D:(s + 1) * D], xT[:, u, s * P:(s + 1) * P], w[:, :],
                                               start=True, stop=True)
                    ins.then_inc(projected, 1)

                def score(g, u):
                    pe.wait_ge(tanh_ready, g + 1)
                    pe.wait_ge(scores_kept, g + 1)
                    for s in range(SUB):
                        ins = nc.tensor.matmul(ps[:, SCORE_BANK + u, 2 * s:2 * s + 2], hT[:, u, s * P:(s + 1) * P], a[:, :],
                                               start=True, stop=True)
                    ins.then_inc(scored, 1)

                pipelined(pe, GROUPS, [(0, turn), (1, project), (2, score)])


def gather_nodes(nc, io, sb, ps):
    with ExitStack() as ctx:
        buf = lambda name, shape, dt=F32: ctx.enter_context(nc.sbuf_tensor(name, shape, dt))
        sem = lambda name: ctx.enter_context(nc.semaphore(name))
        RING = 4
        VALUE_SLOTS = 4
        TURNS = PAIRS // RING
        W = 2 * GROUP
        K = 2 * (D + 1)
        LEAST = float(np.exp(-LEVEL - 1.0))
        edges = buf("edges", [P, RING, W], F32R)
        parts = buf("parts", [P, TILES, K], F32R)
        values = buf("values", [P, VALUE_SLOTS, SUB, D + 1])
        sums = buf("sums3", [P, SUB, D + 1])
        exponent, weight = buf("exponent", [P, TILES]), buf("weight", [P, TILES])
        take, inverse = buf("take", [P, SUB])[:, :], buf("inverse", [P, SUB])[:, :]
        inp, e, valid, todo, mask, x = sb["inp"], sb["e"], sb["valid"], sb["todo"], sb["mask"], sb["x1"]

        exponent_ready = sem("exponent_ready")
        exp_ready = sem("exp_ready2")
        weight_ready = sem("weight_ready")
        e_raised = sem("e_raised")
        values_ready = sem("values_ready")
        parts_hi_ready, parts_lo_ready = sem("parts_hi_ready"), sem("parts_lo_ready")
        edges_ready = [sem("edges_ready_dve"), sem("edges_ready_act")]
        pair_used = sem("pair_used3")
        sums_copied = sem("sums_copied3")
        chain = sem("epilogue_chain3")
        STEPS = 12

        def levels(eng, body):
            count = eng.value_load(sb["levels"][0:1, 0:1], min_val=1, max_val=MOST_LEVELS)
            with eng.Fori(0, count) as level:
                body(level)

        def widen(eng, side, c, m):
            for u in range(side, RING, 2):
                eng.wait_ge(pair_used, PAIRS * c[0] + RING * m + u + 1)
                source = mask[:, bass.ds((PAIRS * c[1] + RING * m + u) * W, W)]
                if side == 0:
                    ins = nc.vector.tensor_copy(edges[:, u, :], source)
                else:
                    ins = nc.scalar.activation(edges[:, u, :], source, ACT.Copy)
                ins.then_inc(edges_ready[side], 1)

        with nc.Block() as block:

            @block.tensor
            def _(pe):
                pe.sem_inc(pair_used, RING)

                def turn(level, c, cu, m, first, last, first_chunk):
                    if first_chunk:
                        pe.wait_ge(parts_lo_ready, VALUE_SLOTS + GROUPS * level + 2 * m + 2)
                    for u in range(RING):
                        pe.wait_ge(edges_ready[u % 2], TURNS * 2 * (GROUPS * level + c) + 2 * m + u // 2 + 1)
                        for h in range(2):
                            rows = parts[:, bass.ds((RING * m + u) * 2 + h, 1), :].rearrange("p a n -> p (a n)")
                            for s in range(SUB):
                                ins = nc.tensor.matmul(ps[:, 4 * cu + s, 0:K], edges[:, u, h * GROUP + s * P:h * GROUP + (s + 1) * P],
                                                       rows, start=first and u == 0 and h == 0,
                                                       stop=last and u == RING - 1 and h == 1)
                        ins.then_inc(pair_used, 1)

                def chunk(level, c, cu, first_chunk):
                    pe.wait_ge(sums_copied, GROUPS * level + c + 1)
                    turn(level, c, cu, 0, True, False, first_chunk)
                    with pe.Fori(1, TURNS - 1) as m:
                        turn(level, c, cu, m, False, False, first_chunk)
                    turn(level, c, cu, TURNS - 1, False, True, first_chunk)

                def body(level):
                    chunk(level, 0, 0, True)
                    chunk(level, 1, 1, False)
                    with pe.Fori(1, GROUPS // 2) as i:
                        for cu in range(2):
                            chunk(level, 2 * i + cu, cu, False)

                levels(pe, body)

            @block.scalar
            def _(act):
                def body(level):
                    act.wait_ge(exponent_ready, level + 1)
                    nc.scalar.activation(weight[:, :], exponent[:, :], ACT.Exp).then_inc(exp_ready, 1)

                    def keep_high(g, u):
                        act.wait_ge(values_ready, GROUPS * level + g + 1)
                        act.wait_ge(pair_used, RING + GROUPS * PAIRS * level)
                        nc.scalar.activation(parts[:, bass.ds(g * SUB, SUB), 0:D + 1], values[:, u, :, :], ACT.Copy)\
                            .then_inc(parts_hi_ready, 1)

                    with act.Fori(0, GROUPS // VALUE_SLOTS) as i:
                        for u in range(VALUE_SLOTS):
                            keep_high(VALUE_SLOTS * i + u, u)
                    with act.Fori(0, GROUPS) as c:
                        with act.Fori(0, TURNS) as m:
                            widen(act, 1, (GROUPS * level + c, c), m)

                levels(act, body)

            @block.gpsimd
            def _(pool):
                pool.sem_inc(parts_lo_ready, VALUE_SLOTS)

                def body(level):
                    with pool.Fori(0, GROUPS // VALUE_SLOTS) as i:
                        for u in range(VALUE_SLOTS):
                            g = VALUE_SLOTS * i + u
                            pool.wait_ge(parts_hi_ready, GROUPS * level + g + 1)
                            tiles = bass.ds(g * SUB, SUB)
                            nc.gpsimd.tensor_tensor(parts[:, tiles, D + 1:K], values[:, u, :, :], parts[:, tiles, 0:D + 1], ALU.subtract)\
                                .then_inc(parts_lo_ready, 1)

                levels(pool, body)

            @block.vector
            def _(dve):
                dve.sem_inc(sums_copied, SLOTS)
                dve.sem_inc(e_raised, 1)

                def epilogue(level, c, cu):
                    C = GROUPS * level + c
                    ch = Chain(dve, chain, C, STEPS)
                    dve.wait_ge(pair_used, RING + PAIRS * (C + 1))
                    banks = ps[:, 4 * cu:4 * cu + SUB, :]
                    ch.link(nc.vector.tensor_copy(sums[:, :, :], banks[:, :, D + 1:K]))
                    ch.link(nc.vector.tensor_tensor(sums[:, :, :], banks[:, :, 0:D + 1], sums[:, :, :], ALU.add))
                    dve.sem_inc(sums_copied, 1)
                    den, left = sums[:, :, D], todo[:, bass.ds(c * SUB, SUB)]
                    ch.mark(nc.vector.scalar_tensor_tensor(out=take, in0=den, scalar=LEAST, in1=left, op0=ALU.is_ge, op1=ALU.mult))
                    ch.link(nc.vector.tensor_scalar(inverse, den, LEAST, None, ALU.max))
                    ch.mark(nc.vector.tensor_tensor(left, left, take, ALU.subtract))
                    ch.link(nc.vector.reciprocal(inverse, inverse))
                    ch.link(nc.vector.tensor_tensor(inverse, inverse, take, ALU.mult))
                    for s in range(SUB):
                        rows = x[:, bass.ds(c, 1), s * D:(s + 1) * D].rearrange("p a d -> p (a d)")
                        ch.mark(nc.vector.scalar_tensor_tensor(out=rows, in0=sums[:, s, 0:D], scalar=inverse[:, s:s + 1],
                                                               in1=rows, op0=ALU.mult, op1=ALU.add))
                    ch.wait()
                    for s in range(SUB):
                        t = c * SUB + s
                        ins = nc.vector.bn_stats(sb["stats"][:, bass.ds(t, 1), :].rearrange("p a n -> p (a n)"), row(tiles_of(x[:, :, :]), t))
                    ch.mark(ins)
                    assert ch.n == STEPS

                def chunk(level, c, after_turn_0):
                    at = (GROUPS * level + c, c)
                    widen(dve, 0, at, 0)
                    if after_turn_0:
                        after_turn_0()
                    with dve.Fori(1, TURNS) as m:
                        widen(dve, 0, at, m)

                def body(level):
                    dve.wait_ge(e_raised, level + 1)
                    nc.vector.tensor_scalar(exponent[:, :], e[:, :], 0.0, None, ALU.min).then_inc(exponent_ready, 1)
                    nc.vector.tensor_scalar(e[:, :], e[:, :], LEVEL, None, ALU.add).then_inc(e_raised, 1)
                    dve.wait_ge(exp_ready, level + 1)
                    nc.vector.tensor_tensor(weight[:, :], weight[:, :], valid[:, :], ALU.mult).then_inc(weight_ready, 1)
                    with dve.Fori(0, GROUPS // VALUE_SLOTS) as i:
                        for u in range(VALUE_SLOTS):
                            g = VALUE_SLOTS * i + u
                            dve.wait_ge(weight_ready, level + 1)
                            dve.wait_ge(parts_lo_ready, GROUPS * level + g + 1)
                            tiles = bass.ds(g * SUB, SUB)
                            nc.vector.tensor_tensor(values[:, u, :, :], inp[:, tiles, :],
                                                    weight[:, tiles].unsqueeze(2).to_broadcast([P, SUB, D + 1]), ALU.mult)\
                                .then_inc(values_ready, 1)
                    chunk(level, 0, None)
                    chunk(level, 1, lambda: epilogue(level, 0, 0))
                    with dve.Fori(1, GROUPS // 2) as i:
                        for cu in range(2):
                            c = 2 * i + cu
                            chunk(level, c, lambda: epilogue(level, c - 1, 1 - cu))
                    epilogue(level, GROUPS - 1, 1)

                levels(dve, body)
                dve.wait_ge(chain, STEPS * GROUPS)


def mix_routed_experts(nc, io, sb, ps):
    with ExitStack() as ctx:
        buf = lambda name, shape, dt=F32: ctx.enter_context(nc.sbuf_tensor(name, shape, dt))
        sem = lambda name: ctx.enter_context(nc.semaphore(name))
        x3 = tiles_of(sb["x1"][:, :, :])
        w1, w2 = buf("w1_all", [P, E, F]), buf("w2_all", [P, E, FH, D])
        w1_hi, w1_lo = buf("w1_all_hi", [P, E, F], F32R), buf("w1_all_lo", [P, E, F], F32R)
        b1, b2 = buf("b1_all", [P, E, FH]), buf("b2_all", [E, D])
        wg, bg = buf("wg", [P, E]), buf("bg", [P, E])
        stage = buf("stage3", [P, SLOTS, GROUP])
        xT = buf("xT3", [P, SLOTS, GROUP])
        xT_hi, xT_lo = buf("xT3_hi", [P, SLOTS, GROUP], F32R), buf("xT3_lo", [P, SLOTS, GROUP], F32R)
        hT = buf("hT3", [P, SLOTS, FH, GROUP])
        mean, var, rstd, t0, t1 = (buf(n, [P, TILES])[:, :] for n in ("mean3", "var3", "rstd3", "t30", "t31"))
        iota = buf("iota", [P, E])
        iota_i = buf("iota_i", [P, E], I32)
        gates, top = buf("gates", [P, SUB, E]), buf("gates_top", [P, SUB, 8])
        index_i, index = buf("gates_index_i", [P, SUB, 8], U32), buf("gates_index", [P, SUB, 8])
        chosen = buf("chosen", [P, SLOTS, SUB, E])
        second = buf("second", [P, SUB, E])
        chosenT = buf("chosenT", [E, SUB * P])
        TURN_BANK, UP_BANK, DOWN_BANK, GATE_BANK = 0, 1, 5, 7

        w1_in, weights_in = sem("w1_in"), sem("weights_in")
        w1_hi_ready, w1_lo_ready = sem("w1_hi_ready"), sem("w1_lo_ready")
        chain = sem("dve_chain3")
        group_chain = sem("group_chain3")
        iota_ready = sem("iota_ready")
        staged = sem("staged3")
        turned = sem("turned3")
        xT_ready, xT_hi_ready, xT_lo_ready = sem("xT_ready3"), sem("xT_hi_ready3"), sem("xT_lo_ready3")
        gates_ready = sem("gates_ready")
        gates_biased = sem("gates_biased")
        chosen_ready = sem("chosen_ready")
        chosen_turned = sem("chosen_turned")
        chosenT_ready = sem("chosenT_ready")
        bias_ready = sem("bias_ready")
        bias_added = sem("bias_added")
        up_ready = sem("up_ready3")
        gelu_ready = sem("gelu_ready3")
        down_ready = sem("down_ready3")
        added = sem("added")
        rows_out = sem("rows_out")
        RANK_STEPS = 12

        def groups(eng, group):
            with eng.Fori(0, GROUPS // 2 - 1) as i:
                for u in range(2):
                    group(2 * i + u, u, False)
            group(GROUPS - 2, 0, False)
            group(GROUPS - 1, 1, True)

        with nc.Block() as block:

            @block.sync
            def _(sp):
                sp.dma_start(w1[:, :, :], io["W1b"].rearrange("e d f -> d e f")).then_inc(w1_in, 16)
                sp.dma_start(wg[:, :], io["Wg"]).then_inc(weights_in, 16)
                sp.dma_start(bg[:, :], io["bg"].partition_broadcast(P)).then_inc(weights_in, 16)
                sp.dma_start(b1[:, :, :], io["b1b"].rearrange("e p f -> p e f")).then_inc(weights_in, 16)
                sp.dma_start(b2[:, :], io["b2b"]).then_inc(weights_in, 16)
                sp.dma_start(w2[:, :, :, :], io["W2b"].rearrange("e (f p) d -> p e f d", p=P)).then_inc(weights_in, 16)
                with sp.Fori(0, GROUPS) as g:
                    sp.wait_ge(added, SLOTS + E * (g + 1))
                    sp.dma_start(io["out"].rearrange("(t p) d -> p t d", p=P)[:, bass.ds(g * SUB, SUB), :],
                                 x3[:, bass.ds(g * SUB, SUB), :]).then_inc(rows_out, 16)
                sp.wait_ge(rows_out, 16 * GROUPS)

            @block.gpsimd
            def _(pool):
                nc.gpsimd.iota(iota_i[:, :], [[1, E]], base=0, channel_multiplier=0).then_inc(iota_ready, 1)
                pool.wait_ge(iota_ready, 1)
                nc.gpsimd.tensor_copy(iota[:, :], iota_i[:, :]).then_inc(iota_ready, 1)

            @block.vector
            def _(dve):
                dve.sem_inc(added, SLOTS)
                ch = Chain(dve, chain)
                row_statistics(nc, ch, sb["stats"], mean, var, t0, t1)
                ch.link(nc.vector.tensor_scalar(var, var, LN_EPS, None, ALU.add))
                inverse_root(nc, ch, rstd, var, t0, t1)

                def normalize(g, u):
                    dve.wait_ge(turned, g + 1)
                    for s in range(SUB):
                        t = g * SUB + s
                        ins = nc.vector.tensor_scalar(stage[:, u, s * D:(s + 1) * D], row(x3, t), mean[:, bass.ds(t, 1)],
                                                      rstd[:, bass.ds(t, 1)], ALU.subtract, ALU.mult)
                    ins.then_inc(staged, 1)

                def keep_turned(g, u):
                    dve.wait_ge(turned, SLOTS + g + 1)
                    nc.vector.tensor_copy(xT[:, u, :], ps[:, TURN_BANK, :]).then_inc(xT_ready, 1)

                def keep_low(g, u):
                    dve.wait_ge(xT_ready, g + 1)
                    dve.wait_ge(xT_hi_ready, g + 1)
                    nc.vector.tensor_tensor(xT_lo[:, u, :], xT[:, u, :], xT_hi[:, u, :], ALU.subtract)\
                        .then_inc(xT_lo_ready, 1)

                def rank(g, gc):
                    dve.wait_ge(gates_ready, g + 1)
                    gc.link(nc.vector.tensor_tensor(gates[:, :, :], ps[:, GATE_BANK, 0:SUB * E].rearrange("p (s e) -> p s e", e=E),
                                                    bg[:, :].unsqueeze(1).to_broadcast([P, SUB, E]), ALU.add))
                    dve.sem_inc(gates_biased, 1)
                    for s in range(SUB):
                        gc.mark(nc.vector.max(top[:, s, :], gates[:, s, :]))
                    gc.wait()
                    dve.sem_inc(gates_biased, 1)
                    for s in range(SUB):
                        gc.mark(nc.vector.max_index(index_i[:, s, :], top[:, s, :], gates[:, s, :]))
                    gc.wait()

                def choose(g, u, gc):
                    places = iota[:, :].unsqueeze(1).to_broadcast([P, SUB, E])
                    gc.link(nc.vector.tensor_copy(index[:, :, :], index_i[:, :, :]))
                    gc.mark(nc.vector.tensor_tensor(chosen[:, u, :, :], places, index[:, :, 0:1].to_broadcast([P, SUB, E]), ALU.is_equal))
                    gc.link(nc.vector.tensor_tensor(second[:, :, :], places, index[:, :, 1:2].to_broadcast([P, SUB, E]), ALU.is_equal))
                    nc.vector.tensor_tensor(chosen[:, u, :, :], chosen[:, u, :, :], second[:, :, :], ALU.add)\
                        .then_inc(chosen_ready, 1)
                    assert gc.n == RANK_STEPS

                def keep_chosen(g):
                    dve.wait_ge(chosen_turned, g + 1)
                    nc.vector.tensor_copy(chosenT[:, :], ps[0:E, GATE_BANK, :]).then_inc(chosenT_ready, 1)

                def add_bias(g):
                    dve.wait_ge(bias_ready, g + 1)
                    nc.vector.tensor_tensor(group_of(x3, g), ps[:, GATE_BANK, :], group_of(x3, g), ALU.add).then_inc(bias_added, 1)

                def add_expert(g, u, e):
                    dve.wait_ge(down_ready, SLOTS + E * g + e + 1)
                    if e == 0:
                        dve.wait_ge(bias_added, g + 1)
                    else:
                        dve.wait_ge(added, SLOTS + E * g + e)
                    for s in range(SUB):
                        rows = row(x3, g * SUB + s)
                        ins = nc.vector.scalar_tensor_tensor(out=rows, in0=ps[:, DOWN_BANK + e % 2, s * D:(s + 1) * D],
                                                             scalar=chosen[:, u, s, e:e + 1], in1=rows,
                                                             op0=ALU.mult, op1=ALU.add)
                    ins.then_inc(added, 1)

                normalize(0, 0)
                dve.wait_ge(w1_hi_ready, 1)
                nc.vector.tensor_tensor(w1_lo[:, :, :], w1[:, :, :], w1_hi[:, :, :], ALU.subtract).then_inc(w1_lo_ready, 1)
                dve.wait_ge(weights_in, 80)
                dve.wait_ge(iota_ready, 2)
                keep_turned(0, 0)
                keep_low(0, 0)
                gc = Chain(dve, group_chain, 0, RANK_STEPS)
                rank(0, gc)
                choose(0, 0, gc)
                keep_chosen(0)
                add_bias(0)

                def group(g, u, last):
                    n, nu = g + 1, 1 - u
                    gc = Chain(dve, group_chain, n, RANK_STEPS)
                    prepare_next = {1: lambda: normalize(n, nu), 2: lambda: keep_turned(n, nu),
                                    3: lambda: keep_low(n, nu), 4: lambda: rank(n, gc),
                                    5: lambda: choose(n, nu, gc), 6: lambda: keep_chosen(n), 7: lambda: add_bias(n)}
                    for e in range(E):
                        if e in prepare_next and not last:
                            prepare_next[e]()
                        add_expert(g, u, e)

                groups(dve, group)

            @block.scalar
            def _(act):
                def keep_high(g, u):
                    act.wait_ge(xT_ready, g + 1)
                    nc.scalar.activation(xT_hi[:, u, :], xT[:, u, :], ACT.Copy).then_inc(xT_hi_ready, 1)

                def gelus(g, e):
                    for f in range(FH):
                        n = e * FH + f
                        act.wait_ge(up_ready, E * FH * g + n + 1)
                        act.wait_ge(down_ready, E * g + e + 1)
                        nc.scalar.activation(hT[:, e % 2, f, :], ps[:, UP_BANK + n % 4, :], ACT.Gelu, bias=b1[:, e, f:f + 1])\
                            .then_inc(gelu_ready, 1)

                act.sem_inc(gelu_ready, 2 * FH)
                act.wait_ge(w1_in, 16)
                nc.scalar.activation(w1_hi[:, :, :], w1[:, :, :], ACT.Copy).then_inc(w1_hi_ready, 1)
                keep_high(0, 0)

                def group(g, u, last):
                    for e in range(E):
                        gelus(g, e)
                        if e == 3 and not last:
                            keep_high(g + 1, 1 - u)

                groups(act, group)

            @block.tensor
            def _(pe):
                def turn(g, u):
                    pe.wait_ge(staged, g + 1)
                    for s in range(SUB):
                        ins = nc.tensor.transpose(ps[:, TURN_BANK, s * P:(s + 1) * P], stage[:, u, s * P:(s + 1) * P], sb["ident"][:, :])
                    ins.then_inc(turned, 1)

                def gate(g, u):
                    pe.wait_ge(xT_ready, g + 1)
                    if not isinstance(g, int) or g > 0:
                        pe.wait_ge(bias_added, g)
                    for s in range(SUB):
                        ins = nc.tensor.matmul(ps[:, GATE_BANK, s * E:(s + 1) * E], xT[:, u, s * P:(s + 1) * P], wg[:, :],
                                               start=True, stop=True)
                    ins.then_inc(gates_ready, 1)

                def turn_chosen(g, u):
                    pe.wait_ge(chosen_ready, g + 1)
                    for s in range(SUB):
                        ins = nc.tensor.transpose(ps[0:E, GATE_BANK, s * P:(s + 1) * P], chosen[:, u, s, :], sb["ident"][:, :])
                    ins.then_inc(chosen_turned, 1)

                def bias(g):
                    pe.wait_ge(chosenT_ready, g + 1)
                    for s in range(SUB):
                        ins = nc.tensor.matmul(ps[:, GATE_BANK, s * D:(s + 1) * D], chosenT[:, s * P:(s + 1) * P], b2[:, :],
                                               start=True, stop=True)
                    ins.then_inc(bias_ready, 1)

                def up(g, u, e):
                    if e == 0:
                        pe.wait_ge(xT_hi_ready, g + 1)
                        pe.wait_ge(xT_lo_ready, g + 1)
                    for f in range(FH):
                        n = e * FH + f
                        pe.wait_ge(gelu_ready, E * FH * g + n + 1)
                        cols = slice(f * P, (f + 1) * P)
                        out = ps[:, UP_BANK + n % 4, :]
                        nc.tensor.matmul(out, w1_lo[:, e, cols], xT_hi[:, u, :], start=True, stop=False)
                        nc.tensor.matmul(out, w1_hi[:, e, cols], xT_lo[:, u, :], start=False, stop=False)
                        nc.tensor.matmul(out, w1_hi[:, e, cols], xT_hi[:, u, :], start=False, stop=True).then_inc(up_ready, 1)

                def down(g, e):
                    pe.wait_ge(gelu_ready, 2 * FH + E * FH * g + (e + 1) * FH)
                    pe.wait_ge(added, E * g + e + 1)
                    for s in range(SUB):
                        for f in range(FH):
                            ins = nc.tensor.matmul(ps[:, DOWN_BANK + e % 2, s * D:(s + 1) * D], hT[:, e % 2, f, s * P:(s + 1) * P],
                                                   w2[:, e, f, :], start=(f == 0), stop=(f == FH - 1))
                    ins.then_inc(down_ready, 1)

                pe.sem_inc(turned, SLOTS)
                pe.sem_inc(down_ready, SLOTS)
                turn(0, 0)
                pe.wait_ge(w1_lo_ready, 1)
                pe.wait_ge(weights_in, 80)
                gate(0, 0)
                up(0, 0, 0)
                turn_chosen(0, 0)
                bias(0)

                def group(g, u, last):
                    n, nu = g + 1, 1 - u
                    prepare_next = {2: lambda: turn(n, nu), 3: lambda: gate(n, nu), 6: lambda: turn_chosen(n, nu),
                                    7: lambda: bias(n)}
                    for e in range(E):
                        if e + 1 < E:
                            up(g, u, e + 1)
                        elif not last:
                            up(n, nu, 0)
                        if e in prepare_next and not last:
                            prepare_next[e]()
                        down(g, e)

                groups(pe, group)


def build(nc, io):
    with ExitStack() as ctx:
        sb = {}
        sb["x1"] = ctx.enter_context(nc.sbuf_tensor("x1", [P, GROUPS, GROUP], F32))
        sb["stats"] = ctx.enter_context(nc.sbuf_tensor("stats", [P, TILES, 6], F32))
        sb["ident"] = ctx.enter_context(nc.sbuf_tensor("ident", [P, P], F32))
        ps = ctx.enter_context(nc.psum_tensor("ps", [P, 8, 512], F32))
        with ExitStack() as graph:
            sb["mask"] = graph.enter_context(nc.sbuf_tensor("mask", [P, TILES * N], mybir.dt.uint8))
            with ExitStack() as attention:
                sb["v16"] = attention.enter_context(nc.sbuf_tensor("v16", [P, TILES, 2 * D + 1], F16))
                sb["qT"] = attention.enter_context(nc.sbuf_tensor("qT", [P, 2, N], F16))
                prepare(nc, io, sb, ps)
                attend(nc, io, sb, ps)
            mix_shared_experts(nc, io, sb, ps)
            with ExitStack() as rows:
                for name, shape, dt in (("inp", [P, TILES, D + 1], F32), ("e", [P, TILES], F32), ("valid", [P, TILES], F32),
                                        ("todo", [P, TILES], F32), ("levels", [P, 1], I32)):
                    sb[name] = rows.enter_context(nc.sbuf_tensor(name, shape, dt))
                project_nodes(nc, io, sb, ps)
                gather_nodes(nc, io, sb, ps)
        mix_routed_experts(nc, io, sb, ps)


def kernel(x, adj, L0_gnn_Wq, L0_gnn_Wk, L0_ffn_Wr, L0_ffn_br, L0_ffn_W1, L0_ffn_b1, L0_ffn_W2, L0_ffn_b2,
           L0_ffn_gamma, L0_ffn_beta, L1_gnn_W, L1_gnn_b, L1_gnn_a, L1_ffn_Wg, L1_ffn_bg, L1_ffn_W1, L1_ffn_b1,
           L1_ffn_W2, L1_ffn_b2):
    import concourse.bacc as bacc
    from concourse.bass_utils import run_bass_kernel_spmd

    laid = {
        "x": x,
        "adj": np.asarray(adj).T.reshape(PAIRS, 2, P, GROUPS, GROUP).transpose(3, 0, 2, 1, 4)
                 .reshape(GROUPS * PAIRS, P, 2 * GROUP),
        "WqT": np.asarray(L0_gnn_Wq).T,
        "WkT": np.asarray(L0_gnn_Wk).T,
        "Wr": L0_ffn_Wr, "br": L0_ffn_br, "gamma": L0_ffn_gamma, "beta": L0_ffn_beta,
        "W1a": L0_ffn_W1, "b1a": np.asarray(L0_ffn_b1).reshape(E, FH, P).transpose(0, 2, 1), "W2a": L0_ffn_W2, "b2a": L0_ffn_b2,
        "W_node": L1_gnn_W, "b_node": np.asarray(L1_gnn_b).reshape(D, 1), "a_node": L1_gnn_a,
        "Wg": L1_ffn_Wg, "bg": L1_ffn_bg,
        "W1b": L1_ffn_W1, "b1b": np.asarray(L1_ffn_b1).reshape(E, FH, P).transpose(0, 2, 1), "W2b": L1_ffn_W2, "b2b": L1_ffn_b2,
    }
    nc = bacc.Bacc("TRN2", target_bir_lowering=False, num_devices=1, dynamic_dma_scratch_size=1024)
    arrays, io = {}, {}
    for name, a in laid.items():
        a = np.ascontiguousarray(a)
        arrays[f"in_{name}"] = a
        io[name] = nc.dram_tensor(f"in_{name}", a.shape, mybir.dt.from_np(a.dtype), kind="ExternalInput").ap()
    io["feat"] = nc.dram_tensor("feat_spill", [P, GROUPS, SUB, D], F32).ap()
    io["out"] = nc.dram_tensor("out", [N, D], F32, kind="ExternalOutput").ap()
    build(nc, io)
    return run_bass_kernel_spmd(nc, [arrays], core_ids=[0]).results[0]["out"]
```

```python
from contextlib import ExitStack

import numpy as np

import concourse.bass as bass
from concourse import mybir

F32 = mybir.dt.float32
F32R = mybir.dt.float32r
F16 = mybir.dt.float16
BF16 = mybir.dt.bfloat16
FP8 = mybir.dt.float8e4
I32 = mybir.dt.int32
U32 = mybir.dt.uint32
ALU = mybir.AluOpType
ACT = mybir.ActivationFunctionType
AX = mybir.AxisListType

P = 128
N = 4096
D = 128
TILES = N // P
SUB = 4
GROUP = SUB * P
GROUPS = N // GROUP
PAIRS = TILES // 2
E = 8
F = 256
FH = F // P
LN_EPS = 1e-5
QK_SCALE = 64.0
V_SCALE = 16.0
SLOTS = 2
LEVEL = 60.0
MOST_LEVELS = 240
SINK = -2.0 ** 40
EPILOGUE_STEPS = 11


class Chain:

    def __init__(self, eng, sem, turn=0, per_turn=0):
        self.eng, self.sem, self.base, self.n = eng, sem, turn * per_turn, 0

    def mark(self, ins):
        self.n += 1
        ins.then_inc(self.sem, 1)

    def wait(self):
        self.eng.wait_ge(self.sem, self.base + self.n)

    def link(self, ins):
        self.mark(ins)
        self.wait()


def row_statistics(nc, ch, stats, mean, var, t0, t1):
    me, mo, ve, vo = (stats[:, :, i] for i in (1, 4, 2, 5))
    ch.mark(nc.vector.tensor_tensor(mean, me, mo, ALU.add))
    ch.mark(nc.vector.tensor_tensor(t0, me, mo, ALU.subtract))
    ch.link(nc.vector.tensor_tensor(t1, ve, vo, ALU.add))
    ch.mark(nc.vector.tensor_scalar(mean, mean, 0.5, None, ALU.mult))
    ch.link(nc.vector.scalar_tensor_tensor(out=t0, in0=t0, scalar=0.25, in1=t0, op0=ALU.mult, op1=ALU.mult))
    ch.link(nc.vector.scalar_tensor_tensor(out=var, in0=t1, scalar=1.0 / D, in1=t0, op0=ALU.mult, op1=ALU.add))


def inverse_root(nc, ch, y, v, t0, t1):
    ch.mark(nc.vector.tensor_scalar(y.bitcast(I32), v.bitcast(I32), -0.5, float(0x5F3759DF), ALU.mult, ALU.add))
    ch.link(nc.vector.tensor_scalar(t1, v, -0.5, None, ALU.mult))
    for _ in range(3):
        ch.link(nc.vector.tensor_tensor(t0, t1, y, ALU.mult))
        ch.link(nc.vector.tensor_tensor(t0, t0, y, ALU.mult))
        ch.link(nc.vector.scalar_tensor_tensor(out=y, in0=t0, scalar=1.5, in1=y, op0=ALU.add, op1=ALU.mult))


def tiles_of(ap):
    return ap.rearrange("p g (s d) -> p (g s) d", d=D)


def row(ap, t):
    return ap[:, bass.ds(t, 1), :].rearrange("p a d -> p (a d)")


def group_of(ap, g):
    return ap[:, bass.ds(g * SUB, SUB), :].rearrange("p s d -> p (s d)")


def pipelined(eng, count, stages):
    lag = max(l for l, _ in stages)

    def step(i, parity):
        for l, stage in stages:
            if not isinstance(i, int) or 0 <= i - l < count:
                stage(i - l, (parity - l) % 2)

    lead = lag + lag % 2
    for i in range(lead):
        step(i, i % 2)
    with eng.Fori(lead // 2, count // 2) as h:
        for parity in range(2):
            step(2 * h + parity, parity)
    for i in range(count, count + lag):
        step(i, i % 2)


def prepare(nc, io, sb, ps):
    with ExitStack() as ctx:
        small = lambda name, shape, dt=F32: ctx.enter_context(nc.sbuf_tensor(name, shape, dt))
        sem = lambda name: ctx.enter_context(nc.semaphore(name))
        room = sb["mask"][:, :].bitcast(F32)
        x = room[:, 0:4096].rearrange("p (t d) -> p t d", d=D)
        qk = room[:, 4096:12288].rearrange("p (g n) -> p g n", g=GROUPS)
        square = room[:, 12288:14336].rearrange("p (u s h) -> p u s h", u=2, h=D)
        feat = room[:, 14336:15360].rearrange("p (u s d) -> p u s d", u=2, d=D)
        featT = room[:, 15360:16384].rearrange("p (u n) -> p u n", u=2)
        unit = room[:, 16384:18432].rearrange("p (u s h) -> p u s h", u=2, h=D)
        w_qk = small("w_qk", [P, 2 * D])
        stats = small("stats0", [P, TILES, 6])
        mean, var, rstd, t0, t1 = (small(n, [P, TILES]) for n in ("mean0", "var0", "rstd0", "t00", "t01"))
        ss, rnorm, t2, t3 = (small(n, [P, 2 * TILES]) for n in ("ss", "rnorm", "t02", "t03"))
        hi, lo = sb["qT"][:, 0, :], sb["qT"][:, 1, :]
        kt = sb["x1"][:, :, :].bitcast(F16)
        v16 = sb["v16"]

        x_in = [sem(f"x_in{i}") for i in range(4)]
        w_in = sem("w_in")
        ident_ready = sem("ident_ready")
        dve_chain = sem("dve_chain0")
        feat_ready = sem("feat_ready")
        feat_turned = sem("feat_turned")
        v_hi_ready = sem("v_hi_ready")
        v_lo_ready = sem("v_lo_ready")
        feat_spilled = [sem(f"feat_spilled{u}") for u in range(2)]
        featT_ready = sem("featT_ready")
        qk_ready = sem("qk_ready")
        qk_copied = sem("qk_copied")
        qk_squared = sem("qk_squared")
        ss_ready = sem("ss_ready")
        norms_ready = sem("norms_ready")
        unit_q_ready = sem("unit_q_ready")
        unit_k_ready = sem("unit_k_ready")
        unit_turned = sem("unit_turned")
        unit_hi = sem("unit_hi")
        unit_lo = sem("unit_lo")

        def scale_rows(eng, unit_engine, g, u, side):
            eng.wait_ge(unit_turned, g + 1)
            halves = lambda ap: ap.rearrange("p (s b) h -> p s b h", b=2)[:, :, side, :]
            scale = rnorm[:, bass.ds(g * 8, 8)].rearrange("p (s b) -> p s b", b=2)[:, :, side].unsqueeze(2).to_broadcast([P, SUB, D])
            raw = qk[:, bass.ds(g, 1), :].rearrange("p a (s h) -> p (a s) h", h=D)
            unit_engine.tensor_tensor(halves(unit[:, u, :, :]), halves(raw), scale, ALU.mult)\
                .then_inc((unit_q_ready, unit_k_ready)[side], 1)

        with nc.Block() as block:

            @block.sync
            def _(sp):
                x_tiles = io["x"].rearrange("(t p) d -> p t d", p=P)
                for i in range(4):
                    sp.dma_start(x[:, 8 * i:8 * i + 8, :], x_tiles[:, 8 * i:8 * i + 8, :]).then_inc(x_in[i], 16)
                sp.dma_start(w_qk[:, 0:D], io["WqT"]).then_inc(w_in, 16)
                sp.dma_start(w_qk[:, D:2 * D], io["WkT"]).then_inc(w_in, 16)
                with sp.Fori(0, GROUPS // 2) as i:
                    for u in range(2):
                        sp.wait_ge(feat_ready, 2 * i + u + 1)
                        sp.dma_start(io["feat"][:, 2 * i + u, :, :], feat[:, u, :, :]).then_inc(feat_spilled[u], 16)
                for u in range(2):
                    sp.wait_ge(feat_spilled[u], 16 * (SLOTS // 2) + 16 * (GROUPS // 2))

            @block.gpsimd
            def _(pool):
                nc.gpsimd.memset(sb["ident"][:, :], 0.0).then_inc(ident_ready, 1)
                pool.wait_ge(ident_ready, 1)
                nc.gpsimd.affine_select(out=sb["ident"][:, :], in_=sb["ident"][:, :], compare_op=ALU.not_equal,
                                        fill=1.0, base=0, pattern=[[-1, P]], channel_multiplier=1).then_inc(ident_ready, 1)
                nc.gpsimd.memset(v16[:, :, D:D + 1], V_SCALE).then_inc(ident_ready, 1)

                def low_values(g, u):
                    pool.wait_ge(v_hi_ready, SLOTS + g + 1)
                    pool.wait_ge(feat_ready, g + 1)
                    tiles = bass.ds(g * SUB, SUB)
                    nc.gpsimd.tensor_tensor(v16[:, tiles, D + 1:], feat[:, u, :, :], v16[:, tiles, 0:D], ALU.subtract)\
                        .then_inc(v_lo_ready, 1)

                pipelined(pool, GROUPS, [(0, low_values)])
                pool.wait_ge(norms_ready, 1)
                pool.wait_ge(qk_copied, GROUPS)
                pipelined(pool, GROUPS, [(0, lambda g, u: scale_rows(pool, nc.gpsimd, g, u, 1))])

            @block.vector
            def _(dve):
                dve.sem_inc(v_lo_ready, SLOTS)
                dve.sem_inc(unit_lo, SLOTS)
                dve.sem_inc(ss_ready, SLOTS)
                for u in range(2):
                    dve.sem_inc(feat_spilled[u], 16)
                ch = Chain(dve, dve_chain)
                for t in range(TILES):
                    if t % 8 == 0:
                        dve.wait_ge(x_in[t // 8], 16)
                    ins = nc.vector.bn_stats(stats[:, t, :], x[:, t, :])
                ch.link(ins)
                row_statistics(nc, ch, stats, mean[:, :], var[:, :], t0[:, :], t1[:, :])
                ch.link(nc.vector.tensor_scalar(var[:, :], var[:, :], LN_EPS, None, ALU.add))
                inverse_root(nc, ch, rstd[:, :], var[:, :], t0[:, :], t1[:, :])
                ch.link(nc.vector.tensor_scalar(rstd[:, :], rstd[:, :], V_SCALE, None, ALU.mult))

                def normalize(g, u):
                    dve.wait_ge(feat_turned, g + 1)
                    dve.wait_ge(v_hi_ready, g + 1)
                    dve.wait_ge(v_lo_ready, g + 1)
                    dve.wait_ge(feat_spilled[u], 8 * (g - u) + 16)
                    for s in range(SUB):
                        t = bass.ds(g * SUB + s, 1)
                        ins = nc.vector.tensor_scalar(feat[:, u, s, :], row(x, g * SUB + s), mean[:, t], rstd[:, t],
                                                      ALU.subtract, ALU.mult)
                    ins.then_inc(feat_ready, 1)

                def keep_turned(g, u):
                    dve.wait_ge(feat_turned, SLOTS + g + 1)
                    nc.vector.tensor_copy(featT[:, u, :], ps[:, u, :]).then_inc(featT_ready, 1)

                def sum_squares(g, u):
                    dve.wait_ge(qk_squared, SLOTS + g + 1)
                    nc.vector.tensor_reduce(ss[:, bass.ds(g * 8, 8)], square[:, u, :, :], AX.X, ALU.add)\
                        .then_inc(ss_ready, 1)

                pipelined(dve, GROUPS, [(1, keep_turned), (0, normalize), (2, sum_squares)])
                dve.wait_ge(ss_ready, SLOTS + GROUPS)
                ch.link(nc.vector.tensor_scalar(ss[:, :], ss[:, :], 1e-8 * V_SCALE ** 2, None, ALU.max))
                inverse_root(nc, ch, rnorm[:, :], ss[:, :], t2[:, :], t3[:, :])
                nc.vector.tensor_scalar(rnorm[:, :], rnorm[:, :], QK_SCALE, None, ALU.mult).then_inc(norms_ready, 1)
                dve.wait_ge(norms_ready, 1)
                dve.wait_ge(qk_copied, GROUPS)

                def low_halves(g, u):
                    dve.wait_ge(unit_turned, SLOTS + g + 1)
                    dve.wait_ge(unit_hi, g + 1)
                    cols = bass.ds(g * GROUP, GROUP)
                    nc.vector.tensor_tensor(lo[:, cols], ps[:, 2 * u, :], hi[:, cols], ALU.subtract)
                    k_lo = kt[:, bass.ds(g, 1), GROUP:].rearrange("p a n -> p (a n)")
                    k_hi = kt[:, bass.ds(g, 1), 0:GROUP].rearrange("p a n -> p (a n)")
                    nc.vector.tensor_tensor(k_lo, ps[:, 2 * u + 1, :], k_hi, ALU.subtract).then_inc(unit_lo, 1)

                pipelined(dve, GROUPS, [(0, lambda g, u: scale_rows(dve, nc.vector, g, u, 0)), (1, low_halves)])
                dve.wait_ge(unit_lo, SLOTS + GROUPS)

            @block.scalar
            def _(act):
                act.sem_inc(v_hi_ready, SLOTS)
                act.sem_inc(qk_squared, SLOTS)
                def high_values(g, u):
                    act.wait_ge(feat_ready, g + 1)
                    nc.scalar.activation(v16[:, bass.ds(g * SUB, SUB), 0:D], feat[:, u, :, :], ACT.Copy)\
                        .then_inc(v_hi_ready, 1)

                def keep_products(g, u):
                    act.wait_ge(qk_ready, g + 1)
                    products = ps[:, 2 + 2 * u:4 + 2 * u, :].rearrange("p b n -> p (b n)")
                    nc.scalar.activation(qk[:, bass.ds(g, 1), :].rearrange("p a n -> p (a n)"), products, ACT.Copy)\
                        .then_inc(qk_copied, 1)
                    act.wait_ge(ss_ready, g + 1)
                    nc.scalar.activation(square[:, u, :, :].rearrange("p s h -> p (s h)"), products, ACT.Square)\
                        .then_inc(qk_squared, 1)

                pipelined(act, GROUPS, [(0, high_values), (1, keep_products)])

                def high_halves(g, u):
                    act.wait_ge(unit_turned, SLOTS + g + 1)
                    nc.scalar.activation(hi[:, bass.ds(g * GROUP, GROUP)], ps[:, 2 * u, :], ACT.Copy)
                    nc.scalar.activation(kt[:, bass.ds(g, 1), 0:GROUP].rearrange("p a n -> p (a n)"),
                                         ps[:, 2 * u + 1, :], ACT.Copy).then_inc(unit_hi, 1)

                pipelined(act, GROUPS, [(0, high_halves)])
                act.wait_ge(unit_hi, GROUPS)

            @block.tensor
            def _(pe):
                pe.sem_inc(feat_turned, SLOTS)
                pe.sem_inc(unit_turned, SLOTS)
                pe.wait_ge(ident_ready, 2)
                pe.wait_ge(w_in, 32)
                def turn_features(g, u):
                    pe.wait_ge(feat_ready, g + 1)
                    for s in range(SUB):
                        ins = nc.tensor.transpose(ps[:, u, s * P:(s + 1) * P], feat[:, u, s, :], sb["ident"][:, :])
                    ins.then_inc(feat_turned, 1)

                def project(g, u):
                    pe.wait_ge(featT_ready, g + 1)
                    pe.wait_ge(qk_squared, g + 1)
                    for s in range(SUB):
                        bank, half = 2 + 2 * u + s // 2, s % 2
                        ins = nc.tensor.matmul(ps[:, bank, half * 2 * D:(half + 1) * 2 * D],
                                               featT[:, u, s * P:(s + 1) * P], w_qk[:, :], start=True, stop=True)
                    ins.then_inc(qk_ready, 1)

                pipelined(pe, GROUPS, [(1, project), (0, turn_features)])

                def turn_units(g, u):
                    pe.wait_ge(unit_q_ready, g + 1)
                    pe.wait_ge(unit_k_ready, g + 1)
                    pe.wait_ge(unit_lo, g + 1)
                    for side in range(2):
                        for s in range(SUB):
                            ins = nc.tensor.transpose(ps[:, 2 * u + side, s * P:(s + 1) * P],
                                                      unit[:, u, 2 * s + side, :], sb["ident"][:, :])
                    ins.then_inc(unit_turned, 1)

                pipelined(pe, GROUPS, [(0, turn_units)])


def attend(nc, io, sb, ps):
    with ExitStack() as ctx:
        buf = lambda name, shape, dt=F32: ctx.enter_context(nc.sbuf_tensor(name, shape, dt))
        sem = lambda name: ctx.enter_context(nc.semaphore(name))
        LOADS = 4
        TURNS = PAIRS // LOADS
        W = 2 * GROUP
        adj = buf("adj", [P, LOADS, W], I32)
        exps = buf("exps", [P, SLOTS, W])
        probs = adj[:, :, :].bitcast(F32)
        p_hi = buf("p_hi", [P, SLOTS, W], F16)
        p_lo = buf("p_lo", [P, SLOTS, W], F16)
        sums = buf("sums", [P, SUB, 2 * D + 1])
        x_feat = buf("x_feat", [P, 2, SUB, D])
        cols = [buf(n, [P, SUB]) for n in ("no_edge", "denominator", "keep")]
        qT, v16, mask = sb["qT"], sb["v16"], sb["mask"]
        kT = sb["x1"][:, :, :].bitcast(F16)

        adj_landed = [sem(f"adj_landed{u}") for u in range(LOADS)]
        rows_landed = sem("rows_landed")
        scores_ready = sem("scores_ready")
        exps_ready = sem("exps_ready")
        masked = sem("masked")
        mask_kept = sem("mask_kept")
        hi_ready = sem("hi_ready")
        lo_ready = sem("lo_ready")
        pair_used = sem("pair_used")
        sums_copied = sem("sums_copied")
        rows_done = sem("rows_done")
        epilogue_chain = sem("epilogue_chain")

        def chunks(eng, chunk):
            with eng.Fori(0, GROUPS - 1) as c:
                chunk(c, False)
            chunk(GROUPS - 1, True)

        def steps(eng, c, last_chunk, step):
            def turn(m, first, last):
                for u in range(LOADS):
                    step(c, m, u, first and u == 0, last and u == LOADS - 1, last_chunk and last and u >= LOADS - 2)
            turn(0, True, False)
            with eng.Fori(1, TURNS - 1) as m:
                turn(m, False, False)
            turn(TURNS - 1, False, True)

        with nc.Block() as block:

            @block.sync
            def _(sp):
                def turn(c, m):
                    for u in range(LOADS):
                        step = PAIRS * c + LOADS * m + u
                        sp.wait_ge(lo_ready, step + 1)
                        sp.wait_ge(mask_kept, step + 1)
                        sp.dma_start(adj[:, u, :], io["adj"][bass.ds(step, 1), :, :].rearrange("a p n -> (a p) n"))\
                            .then_inc(adj_landed[u], 16)

                with sp.Fori(0, GROUPS) as c:
                    with sp.Fori(0, TURNS - 1) as m:
                        turn(c, m)
                    sp.wait_ge(rows_done, c + 1)
                    for r, rows in enumerate((io["x"].rearrange("(g s p) d -> p g s d", p=P, s=SUB), io["feat"])):
                        sp.dma_start(x_feat[:, r, :, :], rows[:, bass.ds(c, 1), :, :].rearrange("p a s d -> p (a s) d"))\
                            .then_inc(rows_landed, 16)
                    turn(c, TURNS - 1)

            @block.tensor
            def _(pe):
                pe.sem_inc(pair_used, SLOTS)

                def scores(c, jp, u):
                    for h in range(2):
                        j = bass.ds(jp * 2 * P + h * P, P)
                        out = ps[:, 2 * (u % 2) + h, :]
                        for n, (q_half, k_half) in enumerate(((0, 0), (0, 1), (1, 0))):
                            keys = kT[:, bass.ds(c, 1), k_half * GROUP:(k_half + 1) * GROUP].rearrange("p a n -> p (a n)")
                            ins = nc.tensor.matmul(out, qT[:, q_half, j], keys, start=(n == 0), stop=(n == 2))
                    ins.then_inc(scores_ready, 1)

                def step(c, m, u, first, last, no_next):
                    jp = LOADS * m + u
                    k = PAIRS * c + jp
                    if not no_next:
                        pe.wait_ge(exps_ready, k + 1)
                        if isinstance(m, int) and jp + 2 >= PAIRS:
                            scores(c + 1, jp + 2 - PAIRS, u)
                        else:
                            scores(c, jp + 2, u)
                    pe.wait_ge(hi_ready, k + 1)
                    pe.wait_ge(lo_ready, LOADS + k + 1)
                    if first:
                        pe.wait_ge(sums_copied, 2 * (c + 1))
                    for h in range(2):
                        v = v16[:, bass.ds(2 * jp + h, 1), :].rearrange("p a n -> p (a n)")
                        for s in range(SUB):
                            i = slice(h * GROUP + s * P, h * GROUP + (s + 1) * P)
                            start, stop = first and h == 0, last and h == 1
                            for half in ("hi", "lo") if start else ("lo", "hi"):
                                if half == "hi":
                                    ins = nc.tensor.matmul(ps[:, 4 + s, 0:2 * D + 1], p_hi[:, u % 2, i], v,
                                                           start=start, stop=stop)
                                else:
                                    ins = nc.tensor.matmul(ps[:, 4 + s, 0:D + 1], p_lo[:, u % 2, i], v[:, 0:D + 1],
                                                           start=False, stop=False)
                    ins.then_inc(pair_used, 1)

                scores(0, 0, 0)
                scores(0, 1, 1)
                chunks(pe, lambda c, last: steps(pe, c, last, step))

            @block.scalar
            def _(act):
                act.sem_inc(sums_copied, 2)
                act.sem_inc(mask_kept, LOADS)

                def exponentials(k, u):
                    act.wait_ge(scores_ready, k + 1)
                    act.wait_ge(masked, k + 1)
                    nc.scalar.activation(exps[:, u % 2, :], ps[:, 2 * (u % 2):2 * (u % 2) + 2, :].rearrange("p b n -> p (b n)"),
                                         ACT.Exp, scale=1.0 / QK_SCALE ** 2).then_inc(exps_ready, 1)

                def step(c, m, u, first, last, no_next):
                    k = PAIRS * c + LOADS * m + u
                    if not (no_next and last):
                        exponentials(k + 1, u + 1)
                    act.wait_ge(masked, SLOTS + k + 1)
                    nc.scalar.activation(mask[:, bass.ds(k * W, W)], probs[:, u, :], ACT.Sign).then_inc(mask_kept, 1)

                def copy_sums(c):
                    act.wait_ge(pair_used, SLOTS + PAIRS * (c + 1))
                    act.wait_ge(rows_done, c + 1)
                    for s in range(2):
                        ins = nc.scalar.activation(sums[:, s, :], ps[:, 4 + s, 0:2 * D + 1], ACT.Copy)
                    ins.then_inc(sums_copied, 1)

                def chunk(c, last, first=False):
                    def at_step(c, m, u, first_step, last_step, no_next):
                        step(c, m, u, first_step, last_step, no_next)
                        if first_step and not first:
                            copy_sums(c - 1)
                    steps(act, c, last, at_step)

                act.wait_ge(scores_ready, 1)
                nc.scalar.activation(exps[:, 0, :], ps[:, 0:2, :].rearrange("p b n -> p (b n)"),
                                     ACT.Exp, scale=1.0 / QK_SCALE ** 2).then_inc(exps_ready, 1)
                chunk(0, False, first=True)
                with act.Fori(1, GROUPS - 1) as c:
                    chunk(c, False)
                chunk(GROUPS - 1, True)
                copy_sums(GROUPS - 1)

            @block.vector
            def _(dve):
                dve.sem_inc(masked, SLOTS)
                dve.sem_inc(rows_done, 1)

                def mask_exponentials(k, c, m, u):
                    dve.wait_ge(adj_landed[u], 16 * (TURNS * c + m + 1))
                    dve.wait_ge(exps_ready, k + 1)
                    nc.vector.scalar_tensor_tensor(out=probs[:, u, :], in0=adj[:, u, :], scalar=0.0,
                                                   in1=exps[:, u % 2, :], op0=ALU.is_gt, op1=ALU.mult)\
                        .then_inc(masked, 1)

                def high_halves(k, u):
                    dve.wait_ge(masked, SLOTS + k + 1)
                    dve.wait_ge(pair_used, k + 1)
                    nc.vector.tensor_copy(p_hi[:, u % 2, :], probs[:, u, :]).then_inc(hi_ready, 1)

                def ending(c):
                    ch = Chain(dve, epilogue_chain, c, EPILOGUE_STEPS)
                    x, feat = x_feat[:, 0, :, :], x_feat[:, 1, :, :]
                    no_edge, den, keep = (t[:, :] for t in cols)

                    def copy_sums():
                        dve.wait_ge(pair_used, SLOTS + PAIRS * (c + 1))
                        for s in range(2, SUB):
                            ins = nc.vector.tensor_copy(sums[:, s, :], ps[:, 4 + s, 0:2 * D + 1])
                        ins.then_inc(sums_copied, 1)

                    def join_halves():
                        dve.wait_ge(sums_copied, 2 * (c + 2))
                        ch.mark(nc.vector.tensor_scalar(no_edge, sums[:, :, D], 0.0, None, ALU.is_le))
                        ch.mark(nc.vector.tensor_tensor(sums[:, :, 0:D], sums[:, :, 0:D], sums[:, :, D + 1:], ALU.add))

                    def denominator():
                        ch.wait()
                        ch.mark(nc.vector.tensor_tensor(den, sums[:, :, D], no_edge, ALU.add))
                        ch.mark(nc.vector.tensor_scalar(keep, no_edge, 0.5 / V_SCALE, 0.5 / V_SCALE, ALU.mult, ALU.add))

                    def invert():
                        ch.wait()
                        ch.mark(nc.vector.reciprocal(den, den))

                    def halve():
                        ch.wait()
                        ch.mark(nc.vector.tensor_scalar(den, den, 0.5, None, ALU.mult))

                    def add_features():
                        dve.wait_ge(rows_landed, 32 * (c + 1))
                        for s in range(SUB):
                            ch.mark(nc.vector.scalar_tensor_tensor(out=x[:, s, :], in0=feat[:, s, :], scalar=keep[:, s:s + 1],
                                                                   in1=x[:, s, :], op0=ALU.mult, op1=ALU.add))

                    def add_sums():
                        ch.wait()
                        for s in range(SUB):
                            rows = sb["x1"][:, bass.ds(c, 1), s * D:(s + 1) * D].rearrange("p a d -> p (a d)")
                            ins = nc.vector.scalar_tensor_tensor(out=rows, in0=sums[:, s, 0:D], scalar=den[:, s:s + 1],
                                                                 in1=x[:, s, :], op0=ALU.mult, op1=ALU.add)
                        ins.then_inc(rows_done, 1)

                    def measure():
                        dve.wait_ge(rows_done, c + 2)
                        for s in range(SUB):
                            t = c * SUB + s
                            ins = nc.vector.bn_stats(sb["stats"][:, bass.ds(t, 1), :].rearrange("p a n -> p (a n)"),
                                                     row(tiles_of(sb["x1"][:, :, :]), t))
                        ch.mark(ins)
                        assert ch.n == EPILOGUE_STEPS

                    return [copy_sums, join_halves, denominator, invert, halve, add_features, add_sums, measure]

                def chunk(c, pieces):
                    for m in range(2):
                        for u in range(LOADS):
                            k = PAIRS * c + LOADS * m + u
                            if not (pieces and m == 0 and u == 1):
                                mask_exponentials(k, c, m, u)
                            high_halves(k, u)
                            if pieces and m == 0 and u == 0:
                                mask_exponentials(k + 1, c, m, u + 1)
                            if pieces:
                                pieces[LOADS * m + u]()
                    with dve.Fori(2, TURNS) as m:
                        for u in range(LOADS):
                            k = PAIRS * c + LOADS * m + u
                            mask_exponentials(k, c, m, u)
                            high_halves(k, u)

                chunk(0, [])
                with dve.Fori(1, GROUPS) as c:
                    chunk(c, ending(c - 1))
                for piece in ending(GROUPS - 1):
                    piece()
                dve.wait_ge(epilogue_chain, EPILOGUE_STEPS * GROUPS)

            @block.gpsimd
            def _(pool):
                pool.sem_inc(lo_ready, LOADS)

                def step(c, m, u, first, last, no_next):
                    k = PAIRS * c + LOADS * m + u
                    pool.wait_ge(hi_ready, k + 1)
                    pool.wait_ge(pair_used, k + 1)
                    nc.gpsimd.tensor_tensor(p_lo[:, u % 2, :], probs[:, u, :], p_hi[:, u % 2, :], ALU.subtract)\
                        .then_inc(lo_ready, 1)

                with pool.Fori(0, GROUPS) as c:
                    with pool.Fori(0, TURNS) as m:
                        for u in range(LOADS):
                            step(c, m, u, False, False, False)


def mix_shared_experts(nc, io, sb, ps):
    with ExitStack() as ctx:
        buf = lambda name, shape, dt=F32: ctx.enter_context(nc.sbuf_tensor(name, shape, dt))
        sem = lambda name: ctx.enter_context(nc.semaphore(name))
        x1 = tiles_of(sb["x1"][:, :, :])
        xn = buf("xn1", [P, TILES, D])
        xT_hi, xT_lo = buf("xT1_hi", [P, GROUPS, GROUP], F32R), buf("xT1_lo", [P, GROUPS, GROUP], F32R)
        hT = buf("hT1", [P, SLOTS, 2 * FH, GROUP])
        w1, w2 = buf("w1_pair", [P, 2, F]), buf("w2_pair", [P, 2, FH, D])
        w1_hi, w1_lo = buf("w1_pair_hi", [P, 2, F], F32R), buf("w1_pair_lo", [P, 2, F], F32R)
        b1, b2 = buf("b1_pair", [P, 2, FH]), buf("b2_pair", [P, 2, D])
        gamma, beta = buf("gamma", [P, D]), buf("beta", [P, D])
        wr, br = buf("wr", [P, E]), buf("br", [P, E])
        token_sums, mean_column = buf("token_sums", [P, GROUPS]), buf("mean_column", [P, P])
        shift = buf("shift1", [P, TILES])[:, :]
        mean, var, rstd, t0, t1 = (buf(n, [P, TILES])[:, :] for n in ("mean1", "var1", "rstd1", "t10", "t11"))
        route, route_exp = buf("route", [P, E]), buf("route_exp", [P, E])
        top, top_index = buf("top", [P, 8]), buf("top_index", [P, 8], U32)
        share = buf("share", [P, 2])
        a, b = buf("route_a", [P, 1]), buf("route_b", [P, 1])
        bias = buf("bias", [P, D])
        DOWN_BANK, UP_BANK, TURN_BANK, ROUTE_BANK = 0, 2, 6, 2
        STEPS = 18

        small_in = sem("small_in")
        w1_in, experts_in = sem("w1_in1"), sem("experts_in")
        chain = sem("dve_chain1")
        xn_dve, xn_act = sem("xn_dve"), sem("xn_act")
        shift_ready = sem("shift_ready")
        pair_chain = sem("pair_chain")
        beta_added = sem("beta_added")
        mean_ready = sem("mean_ready")
        logits_ready = sem("logits_ready")
        route_ready = sem("route_ready")
        exp_ready = sem("exp_ready")
        index_ready = sem("index_ready")
        turned = sem("turned")
        xT_hi_ready, xT_lo_ready = sem("xT_hi_ready"), sem("xT_lo_ready")
        w1_hi_ready, weights_ready = sem("w1_hi_ready1"), sem("weights_ready")
        up_ready = sem("up_ready")
        gelu_ready = sem("gelu_ready")
        down_ready = sem("down_ready")
        biased = sem("biased")
        z_ready = sem("z_ready")
        z_measured = sem("z_measured")
        norm_ready = sem("norm_ready")
        z_normal = sem("z_normal")
        z_scaled = sem("z_scaled")
        x2_ready = sem("x2_ready")
        x2_measured = sem("x2_measured")

        def load_expert(eng, n):
            eng.wait_ge(index_ready, 1)
            one = bass.ds(eng.value_load(top_index[0:1, n:n + 1], min_val=0, max_val=E - 1), 1)
            eng.dma_start(w1[:, n, :], io["W1a"][one, :, :].rearrange("a d f -> (a d) f")).then_inc(w1_in, 16)
            eng.dma_start(w2[:, n, :, :], io["W2a"][one, :, :].rearrange("a (f p) d -> p (a f) d", p=P)).then_inc(experts_in, 16)
            eng.dma_start(b2[:, n, :], io["b2a"][one, :].rearrange("a d -> (a d)").partition_broadcast(P)).then_inc(experts_in, 16)
            eng.dma_start(b1[:, n, :], io["b1a"][one, :, :].rearrange("a p f -> (a p) f")).then_inc(experts_in, 16)

        with nc.Block() as block:

            @block.sync
            def _(sp):
                sp.dma_start(wr[:, :], io["Wr"]).then_inc(small_in, 16)
                for to, name in ((br, "br"), (gamma, "gamma"), (beta, "beta")):
                    sp.dma_start(to[:, :], io[name].partition_broadcast(P)).then_inc(small_in, 16)
                load_expert(sp, 0)
                sp.wait_ge(experts_in, 96)

            @block.gpsimd
            def _(pool):
                pool.wait_ge(small_in, 64)
                pool.wait_ge(xn_dve, GROUPS)
                pool.wait_ge(xn_act, GROUPS)
                spread = lambda v: v[:, :].unsqueeze(1).to_broadcast([P, SUB, D])
                tiles = lambda x, g: x[:, bass.ds(g * SUB, SUB), :]
                with pool.Fori(0, GROUPS) as g:
                    nc.gpsimd.tensor_tensor(tiles(x1, g), tiles(x1, g), spread(beta), ALU.add).then_inc(beta_added, 1)
                pool.wait_ge(turned, SLOTS + GROUPS)
                pool.wait_ge(weights_ready, 1)
                with pool.Fori(0, GROUPS) as g:
                    nc.gpsimd.tensor_tensor(tiles(xn, g), tiles(xn, g), spread(bias), ALU.add).then_inc(biased, 1)
                with pool.Fori(0, GROUPS // 2) as i:
                    pool.wait_ge(z_normal, i + 1)
                    for u in range(2):
                        ins = nc.gpsimd.tensor_tensor(tiles(xn, 2 * i + u), tiles(xn, 2 * i + u), spread(gamma), ALU.mult)
                    ins.then_inc(z_scaled, 1)

            @block.vector
            def _(dve):
                dve.sem_inc(xT_lo_ready, SLOTS)
                dve.sem_inc(z_ready, SLOTS)
                ch = Chain(dve, chain)
                row_statistics(nc, ch, sb["stats"], mean, var, t0, t1)
                ch.link(nc.vector.tensor_scalar(var, var, LN_EPS, None, ALU.add))
                inverse_root(nc, ch, rstd, var, t0, t1)
                nc.vector.scalar_tensor_tensor(out=shift, in0=mean, scalar=-1.0, in1=rstd, op0=ALU.mult, op1=ALU.mult)\
                    .then_inc(shift_ready, 1)

                def normalize(g, u):
                    t = g * SUB
                    nc.vector.tensor_scalar(row(xn, t), row(x1, t), mean[:, bass.ds(t, 1)], rstd[:, bass.ds(t, 1)],
                                            ALU.subtract, ALU.mult).then_inc(xn_dve, 1)

                def keep_low(g, u):
                    dve.wait_ge(xT_hi_ready, g + 1)
                    nc.vector.tensor_reduce(token_sums[:, bass.ds(g, 1)], ps[:, TURN_BANK + u, :], AX.X, ALU.add)
                    nc.vector.tensor_tensor(xT_lo[:, bass.ds(g, 1), :].rearrange("p a n -> p (a n)"), ps[:, TURN_BANK + u, :],
                                            xT_hi[:, bass.ds(g, 1), :].rearrange("p a n -> p (a n)"), ALU.subtract)\
                        .then_inc(xT_lo_ready, 1)

                pipelined(dve, GROUPS, [(0, normalize), (1, keep_low)])
                dve.wait_ge(xT_lo_ready, SLOTS + GROUPS)
                ch.link(nc.vector.tensor_reduce(a[:, :], token_sums[:, :], AX.X, ALU.add))
                nc.vector.tensor_scalar(mean_column[:, :], a[:, 0:1].to_broadcast([P, P]), 1.0 / N, None, ALU.mult)\
                    .then_inc(mean_ready, 1)
                dve.wait_ge(logits_ready, 1)
                dve.wait_ge(small_in, 64)
                r, ex = route[:, :], route_exp[:, :]
                ch.link(nc.vector.tensor_tensor(r, ps[:, ROUTE_BANK, 0:E], br[:, :], ALU.add))

                def softmax(x, n, times):
                    e = ex[:, 0:n]
                    ch.link(nc.vector.tensor_reduce(a[:, :], x, AX.X, ALU.max))
                    nc.vector.tensor_scalar(x, x, a[:, :], None, ALU.subtract).then_inc(route_ready, 1)
                    dve.wait_ge(exp_ready, times)
                    ch.link(nc.vector.tensor_reduce(b[:, :], e, AX.X, ALU.add))
                    ch.link(nc.vector.reciprocal(b[:, :], b[:, :]))
                    ch.link(nc.vector.tensor_scalar(x, e, b[:, :], None, ALU.mult))

                softmax(r, E, 1)
                capacity = float(-(-N * 5 // (4 * E)))
                ch.link(nc.vector.tensor_scalar(ex, r, float(N), 1e-30, ALU.mult, ALU.max))
                ch.link(nc.vector.reciprocal(ex, ex))
                ch.link(nc.vector.tensor_scalar(ex, ex, capacity, 1.0, ALU.mult, ALU.min))
                ch.link(nc.vector.tensor_tensor(r, r, ex, ALU.mult))
                softmax(r, E, 2)
                ch.link(nc.vector.max(top[:, :], r))
                nc.vector.max_index(top_index[:, :], top[:, :], r).then_inc(index_ready, 1)
                ch.link(nc.vector.tensor_copy(share[:, :], top[:, 0:2]))
                softmax(share[:, :], 2, 3)
                dve.wait_ge(experts_in, 96)
                for n in range(2):
                    ch.mark(nc.vector.tensor_scalar(w2[:, n, :, :], w2[:, n, :, :], share[:, n:n + 1], None, ALU.mult))
                ch.link(nc.vector.tensor_scalar(bias[:, :], b2[:, 0, :], share[:, 0:1], None, ALU.mult))
                ch.link(nc.vector.scalar_tensor_tensor(out=bias[:, :], in0=b2[:, 1, :], scalar=share[:, 1:2], in1=bias[:, :],
                                                       op0=ALU.mult, op1=ALU.add))
                dve.wait_ge(w1_hi_ready, 1)
                nc.vector.tensor_tensor(w1_lo[:, :, :], w1[:, :, :], w1_hi[:, :, :], ALU.subtract).then_inc(weights_ready, 1)

                stats = sb["stats"]

                def measure(x, g):
                    for s in range(SUB):
                        t = g * SUB + s
                        ins = nc.vector.bn_stats(stats[:, bass.ds(t, 1), :].rearrange("p a n -> p (a n)"), row(x, t))
                    return ins

                def finish_outputs(i, _):
                    for u in range(2):
                        g = 2 * i + u
                        dve.wait_ge(down_ready, SLOTS + g + 1)
                        dve.wait_ge(biased, g + 1)
                        nc.vector.tensor_tensor(group_of(xn, g), ps[:, DOWN_BANK + u, :], group_of(xn, g), ALU.add).then_inc(z_ready, 1)
                        dve.wait_ge(z_ready, SLOTS + g + 1)
                        measure(xn, g).then_inc(z_measured, 1)
                    dve.wait_ge(z_measured, 2 * i + 2)
                    tiles = bass.ds(2 * SUB * i, 2 * SUB)
                    m, v, y, s0, s1 = (ap[:, tiles] for ap in (mean, var, rstd, t0, t1))
                    pc = Chain(dve, pair_chain, i, STEPS)
                    row_statistics(nc, pc, stats[:, tiles, :], m, v, s0, s1)
                    pc.link(nc.vector.tensor_scalar(v, v, LN_EPS, None, ALU.add))
                    inverse_root(nc, pc, y, v, s0, s1)
                    assert pc.n == STEPS
                    nc.vector.scalar_tensor_tensor(out=shift[:, tiles], in0=m, scalar=-1.0, in1=y, op0=ALU.mult, op1=ALU.mult)\
                        .then_inc(norm_ready, 1)

                def add_rows(i, _):
                    dve.wait_ge(z_scaled, i + 1)
                    dve.wait_ge(beta_added, GROUPS)
                    for u in range(2):
                        g = 2 * i + u
                        nc.vector.tensor_tensor(group_of(x1, g), group_of(xn, g), group_of(x1, g), ALU.add).then_inc(x2_ready, 1)
                    for u in range(2):
                        dve.wait_ge(x2_ready, 2 * i + u + 1)
                        measure(x1, 2 * i + u).then_inc(x2_measured, 1)

                pipelined(dve, GROUPS // 2, [(0, finish_outputs), (1, add_rows)])
                dve.wait_ge(x2_measured, GROUPS)

            @block.scalar
            def _(act):
                def exponential(times, to, x):
                    act.wait_ge(route_ready, times)
                    nc.scalar.activation(to, x, ACT.Exp).then_inc(exp_ready, 1)

                act.sem_inc(gelu_ready, 4)
                act.wait_ge(shift_ready, 1)

                def normalize(x, g, s):
                    t = g * SUB + s
                    return nc.scalar.activation(row(xn, t), row(x, t), ACT.Identity, bias=shift[:, bass.ds(t, 1)],
                                                scale=rstd[:, bass.ds(t, 1)])

                def normalize_three(g, u):
                    for s in range(1, SUB):
                        ins = normalize(x1, g, s)
                    ins.then_inc(xn_act, 1)

                def keep_high(g, u):
                    act.wait_ge(turned, SLOTS + g + 1)
                    nc.scalar.activation(xT_hi[:, bass.ds(g, 1), :].rearrange("p a n -> p (a n)"), ps[:, TURN_BANK + u, :], ACT.Copy)\
                        .then_inc(xT_hi_ready, 1)

                pipelined(act, GROUPS, [(0, normalize_three), (1, keep_high)])
                exponential(1, route_exp[:, :], route[:, :])
                exponential(2, route_exp[:, :], route[:, :])
                load_expert(act, 1)
                exponential(3, route_exp[:, 0:2], share[:, :])
                act.wait_ge(w1_in, 32)
                nc.scalar.activation(w1_hi[:, :, :], w1[:, :, :], ACT.Copy).then_inc(w1_hi_ready, 1)
                act.wait_ge(experts_in, 96)

                def gelus(g, u):
                    act.wait_ge(down_ready, g + 1)
                    for n in range(4):
                        act.wait_ge(up_ready, 4 * g + n + 1)
                        nc.scalar.activation(hT[:, u, n, :], ps[:, UP_BANK + n, :], ACT.Gelu, bias=b1[:, n // 2, n % 2:n % 2 + 1])\
                            .then_inc(gelu_ready, 1)

                def gelus_pair(i, _):
                    for u in range(2):
                        gelus(2 * i + u, u)

                def normalize_pair(i, _):
                    act.wait_ge(norm_ready, i + 1)
                    for u in range(2):
                        for s in range(SUB):
                            ins = normalize(xn, 2 * i + u, s)
                    ins.then_inc(z_normal, 1)

                pipelined(act, GROUPS // 2, [(0, gelus_pair), (1, normalize_pair)])

            @block.tensor
            def _(pe):
                pe.sem_inc(turned, SLOTS)
                pe.sem_inc(down_ready, SLOTS)
                for g in range(GROUPS):
                    pe.wait_ge(xT_lo_ready, g + 1)
                    pe.wait_ge(xn_dve, g + 1)
                    pe.wait_ge(xn_act, g + 1)
                    for s in range(SUB):
                        ins = nc.tensor.transpose(ps[:, TURN_BANK + g % 2, s * P:(s + 1) * P], xn[:, g * SUB + s, :], sb["ident"][:, :])
                    ins.then_inc(turned, 1)
                pe.wait_ge(mean_ready, 1)
                pe.wait_ge(small_in, 64)
                nc.tensor.matmul(ps[:, ROUTE_BANK, 0:E], mean_column[:, :], wr[:, :], start=True, stop=True).then_inc(logits_ready, 1)
                pe.wait_ge(weights_ready, 1)
                pe.wait_ge(xT_lo_ready, SLOTS + GROUPS)

                def up(g, u):
                    for n in range(4):
                        pe.wait_ge(gelu_ready, 4 * g + n + 1)
                        part = lambda w: w[:, n // 2, (n % 2) * P:(n % 2 + 1) * P]
                        token = lambda x: x[:, bass.ds(g, 1), :].rearrange("p a n -> p (a n)")
                        out = ps[:, UP_BANK + n, :]
                        nc.tensor.matmul(out, part(w1_lo), token(xT_hi), start=True, stop=False)
                        nc.tensor.matmul(out, part(w1_hi), token(xT_lo), start=False, stop=False)
                        nc.tensor.matmul(out, part(w1_hi), token(xT_hi), start=False, stop=True).then_inc(up_ready, 1)

                def down(g, u):
                    pe.wait_ge(gelu_ready, 4 * g + 8)
                    pe.wait_ge(z_ready, g + 1)
                    for s in range(SUB):
                        for n in range(4):
                            ins = nc.tensor.matmul(ps[:, DOWN_BANK + u, s * P:(s + 1) * P], hT[:, u, n, s * P:(s + 1) * P],
                                                   w2[:, n // 2, n % 2, :], start=(n == 0), stop=(n == 3))
                    ins.then_inc(down_ready, 1)

                pipelined(pe, GROUPS, [(0, up), (1, down)])


def project_nodes(nc, io, sb, ps):
    with ExitStack() as ctx:
        buf = lambda name, shape, dt=F32: ctx.enter_context(nc.sbuf_tensor(name, shape, dt))
        sem = lambda name: ctx.enter_context(nc.semaphore(name))
        x2 = tiles_of(sb["x1"][:, :, :])
        inp, e, valid = sb["inp"], sb["e"][:, :], sb["valid"][:, :]
        stage = buf("stage2", [P, SLOTS, GROUP])
        xT = buf("xT2", [P, SLOTS, GROUP])
        hT = buf("hT2", [P, SLOTS, GROUP])
        w, b, a = buf("w_node", [P, D]), buf("b_node", [P, 1]), buf("a_and_one", [P, 2])
        mean, var, rstd, t0, t1 = (buf(n, [P, TILES])[:, :] for n in ("mean2", "var2", "rstd2", "t20", "t21"))
        e_sum = buf("e_and_sum", [P, TILES, 2])
        ends, ends_all = buf("ends", [P, 2]), buf("ends_all", [P, 2])
        TURN_BANK, ROW_BANK, COLUMN_BANK, SCORE_BANK = 0, 2, 4, 6

        small_in = sem("small_in2")
        ones_ready = sem("ones_ready")
        chain = sem("dve_chain2")
        staged = sem("staged2")
        turned = sem("turned2")
        xT_ready = sem("xT_ready2")
        projected = sem("projected")
        inp_kept = sem("inp_kept")
        tanh_ready = sem("tanh_ready")
        scored = sem("scored")
        scores_kept = sem("scores_kept")
        ends_ready = sem("ends_ready")

        with nc.Block() as block:

            @block.sync
            def _(sp):
                sp.dma_start(w[:, :], io["W_node"]).then_inc(small_in, 16)
                sp.dma_start(b[:, :], io["b_node"]).then_inc(small_in, 16)
                sp.dma_start(a[:, 0:1], io["a_node"]).then_inc(small_in, 16)

            @block.gpsimd
            def _(pool):
                nc.gpsimd.memset(a[:, 1:2], 1.0).then_inc(ones_ready, 1)
                nc.gpsimd.memset(inp[:, :, D:D + 1], 1.0).then_inc(ones_ready, 1)
                nc.gpsimd.memset(sb["todo"][:, :], 1.0).then_inc(ones_ready, 1)
                pool.wait_ge(ends_ready, 1)
                nc.gpsimd.partition_all_reduce(ends_all[:, :], ends[:, :], P, bass.bass_isa.ReduceOp.max).then_inc(ends_ready, 1)

            @block.vector
            def _(dve):
                dve.sem_inc(scores_kept, SLOTS)
                ch = Chain(dve, chain)
                row_statistics(nc, ch, sb["stats"], mean, var, t0, t1)
                ch.link(nc.vector.tensor_scalar(var, var, LN_EPS, None, ALU.add))
                inverse_root(nc, ch, rstd, var, t0, t1)

                def normalize(g, u):
                    dve.wait_ge(turned, g + 1)
                    for s in range(SUB):
                        t = g * SUB + s
                        ins = nc.vector.tensor_scalar(stage[:, u, s * D:(s + 1) * D], row(x2, t), mean[:, bass.ds(t, 1)],
                                                      rstd[:, bass.ds(t, 1)], ALU.subtract, ALU.mult)
                    ins.then_inc(staged, 1)

                def keep_turned(g, u):
                    dve.wait_ge(turned, SLOTS + g + 1)
                    dve.wait_ge(projected, g + 1)
                    nc.vector.tensor_copy(xT[:, u, :], ps[:, TURN_BANK + u, :]).then_inc(xT_ready, 1)

                def keep_scores(g, u):
                    dve.wait_ge(scored, SLOTS + g + 1)
                    nc.vector.tensor_copy(e_sum[:, bass.ds(g * SUB, SUB), :].rearrange("p s n -> p (s n)"),
                                          ps[:, SCORE_BANK + u, 0:2 * SUB]).then_inc(scores_kept, 1)

                pipelined(dve, GROUPS, [(0, normalize), (1, keep_turned), (3, keep_scores)])
                dve.wait_ge(scores_kept, SLOTS + GROUPS)
                ch.link(nc.vector.tensor_scalar(valid, e_sum[:, :, 1], 0.0, None, ALU.not_equal))
                ch.mark(nc.vector.tensor_tensor(t0, e_sum[:, :, 0], valid, ALU.mult))
                ch.link(nc.vector.tensor_scalar(t1, valid, 1e30, -1e30, ALU.mult, ALU.add))
                ch.mark(nc.vector.tensor_tensor(e, t0, t1, ALU.add))
                ch.link(nc.vector.tensor_tensor(t0, t1, t0, ALU.subtract))
                ch.mark(nc.vector.tensor_reduce(ends[:, 0:1], e, AX.X, ALU.max))
                nc.vector.tensor_reduce(ends[:, 1:2], t0, AX.X, ALU.max).then_inc(ends_ready, 1)
                dve.wait_ge(ends_ready, 2)
                ch.mark(nc.vector.tensor_scalar(e, e, ends_all[:, 0:1], None, ALU.subtract))
                span = t1[:, 0:1]
                ch.link(nc.vector.tensor_tensor(span, ends_all[:, 0:1], ends_all[:, 1:2], ALU.add))
                ch.link(nc.vector.tensor_scalar(span, span, 1.0 / LEVEL, 0.5, ALU.mult, ALU.add))
                ch.link(nc.vector.tensor_scalar(span, span, 1.0, float(MOST_LEVELS), ALU.max, ALU.min))
                ch.link(nc.vector.tensor_copy(sb["levels"][:, :], span))

            @block.scalar
            def _(act):
                act.sem_inc(inp_kept, SLOTS)
                act.wait_ge(small_in, 48)

                def keep_projection(g, u):
                    act.wait_ge(projected, SLOTS + g + 1)
                    act.wait_ge(scored, g + 1)
                    nc.scalar.activation(hT[:, u, :], ps[:, COLUMN_BANK + u, :], ACT.Tanh, bias=b[:, 0:1]).then_inc(tanh_ready, 1)
                    nc.scalar.activation(inp[:, bass.ds(g * SUB, SUB), 0:D], ps[:, ROW_BANK + u, :].rearrange("p (s d) -> p s d", d=D),
                                         ACT.Copy).then_inc(inp_kept, 1)

                pipelined(act, GROUPS, [(0, keep_projection)])
                act.wait_ge(inp_kept, SLOTS + GROUPS)

            @block.tensor
            def _(pe):
                pe.sem_inc(turned, SLOTS)
                pe.sem_inc(projected, SLOTS)
                pe.sem_inc(scored, SLOTS)
                pe.wait_ge(small_in, 48)
                pe.wait_ge(ones_ready, 1)

                def turn(g, u):
                    pe.wait_ge(staged, g + 1)
                    for s in range(SUB):
                        ins = nc.tensor.transpose(ps[:, TURN_BANK + u, s * P:(s + 1) * P], stage[:, u, s * P:(s + 1) * P], sb["ident"][:, :])
                    ins.then_inc(turned, 1)

                def project(g, u):
                    pe.wait_ge(xT_ready, g + 1)
                    pe.wait_ge(inp_kept, g + 1)
                    nc.tensor.matmul(ps[:, COLUMN_BANK + u, :], w[:, :], xT[:, u, :], start=True, stop=True)
                    for s in range(SUB):
                        ins = nc.tensor.matmul(ps[:, ROW_BANK + u, s * D:(s + 1) * D], xT[:, u, s * P:(s + 1) * P], w[:, :],
                                               start=True, stop=True)
                    ins.then_inc(projected, 1)

                def score(g, u):
                    pe.wait_ge(tanh_ready, g + 1)
                    pe.wait_ge(scores_kept, g + 1)
                    for s in range(SUB):
                        ins = nc.tensor.matmul(ps[:, SCORE_BANK + u, 2 * s:2 * s + 2], hT[:, u, s * P:(s + 1) * P], a[:, :],
                                               start=True, stop=True)
                    ins.then_inc(scored, 1)

                pipelined(pe, GROUPS, [(0, turn), (1, project), (2, score)])


def gather_nodes(nc, io, sb, ps):
    with ExitStack() as ctx:
        buf = lambda name, shape, dt=F32: ctx.enter_context(nc.sbuf_tensor(name, shape, dt))
        sem = lambda name: ctx.enter_context(nc.semaphore(name))
        RING = 4
        VALUE_SLOTS = 4
        TURNS = PAIRS // RING
        W = 2 * GROUP
        K = 2 * (D + 1)
        LEAST = float(np.exp(-LEVEL - 1.0))
        edges = buf("edges", [P, RING, W], F32R)
        parts = buf("parts", [P, TILES, K], F32R)
        values = buf("values", [P, VALUE_SLOTS, SUB, D + 1])
        sums = buf("sums3", [P, SUB, D + 1])
        exponent, weight = buf("exponent", [P, TILES]), buf("weight", [P, TILES])
        take, inverse = buf("take", [P, SUB])[:, :], buf("inverse", [P, SUB])[:, :]
        inp, e, valid, todo, mask, x = sb["inp"], sb["e"], sb["valid"], sb["todo"], sb["mask"], sb["x1"]

        exponent_ready = sem("exponent_ready")
        exp_ready = sem("exp_ready2")
        weight_ready = sem("weight_ready")
        e_raised = sem("e_raised")
        values_ready = sem("values_ready")
        parts_hi_ready, parts_lo_ready = sem("parts_hi_ready"), sem("parts_lo_ready")
        edges_ready = [sem("edges_ready_dve"), sem("edges_ready_act")]
        pair_used = sem("pair_used3")
        sums_copied = sem("sums_copied3")
        chain = sem("epilogue_chain3")
        STEPS = 12

        def levels(eng, body):
            count = eng.value_load(sb["levels"][0:1, 0:1], min_val=1, max_val=MOST_LEVELS)
            with eng.Fori(0, count) as level:
                body(level)

        def widen(eng, side, c, m, half=None):
            for u in range(side, RING, 2) if half is None else [side + 2 * half]:
                eng.wait_ge(pair_used, PAIRS * c[0] + RING * m + u + 1)
                source = mask[:, bass.ds((PAIRS * c[1] + RING * m + u) * W, W)]
                if side == 0:
                    ins = nc.vector.tensor_copy(edges[:, u, :], source)
                else:
                    ins = nc.scalar.activation(edges[:, u, :], source, ACT.Copy)
                ins.then_inc(edges_ready[side], 1)

        with nc.Block() as block:

            @block.tensor
            def _(pe):
                pe.sem_inc(pair_used, RING)

                def turn(level, c, cu, m, first, last, first_chunk):
                    if first_chunk:
                        pe.wait_ge(parts_lo_ready, VALUE_SLOTS + GROUPS * level + 2 * m + 2)
                    for u in range(RING):
                        pe.wait_ge(edges_ready[u % 2], TURNS * 2 * (GROUPS * level + c) + 2 * m + u // 2 + 1)
                        for h in range(2):
                            rows = parts[:, bass.ds((RING * m + u) * 2 + h, 1), :].rearrange("p a n -> p (a n)")
                            for s in range(SUB):
                                ins = nc.tensor.matmul(ps[:, 4 * cu + s, 0:K], edges[:, u, h * GROUP + s * P:h * GROUP + (s + 1) * P],
                                                       rows, start=first and u == 0 and h == 0,
                                                       stop=last and u == RING - 1 and h == 1)
                        ins.then_inc(pair_used, 1)

                def chunk(level, c, cu, first_chunk):
                    pe.wait_ge(sums_copied, GROUPS * level + c + 1)
                    turn(level, c, cu, 0, True, False, first_chunk)
                    with pe.Fori(1, TURNS - 1) as m:
                        turn(level, c, cu, m, False, False, first_chunk)
                    turn(level, c, cu, TURNS - 1, False, True, first_chunk)

                def body(level):
                    chunk(level, 0, 0, True)
                    chunk(level, 1, 1, False)
                    with pe.Fori(1, GROUPS // 2) as i:
                        for cu in range(2):
                            chunk(level, 2 * i + cu, cu, False)

                levels(pe, body)

            @block.scalar
            def _(act):
                def body(level):
                    act.wait_ge(exponent_ready, level + 1)
                    nc.scalar.activation(weight[:, :], exponent[:, :], ACT.Exp).then_inc(exp_ready, 1)

                    def keep_high(g, u):
                        act.wait_ge(values_ready, GROUPS * level + g + 1)
                        act.wait_ge(pair_used, RING + GROUPS * PAIRS * level)
                        nc.scalar.activation(parts[:, bass.ds(g * SUB, SUB), 0:D + 1], values[:, u, :, :], ACT.Copy)\
                            .then_inc(parts_hi_ready, 1)

                    with act.Fori(0, GROUPS // VALUE_SLOTS) as i:
                        for u in range(VALUE_SLOTS):
                            keep_high(VALUE_SLOTS * i + u, u)
                    with act.Fori(0, GROUPS) as c:
                        with act.Fori(0, TURNS) as m:
                            widen(act, 1, (GROUPS * level + c, c), m)

                levels(act, body)

            @block.gpsimd
            def _(pool):
                pool.sem_inc(parts_lo_ready, VALUE_SLOTS)

                def body(level):
                    with pool.Fori(0, GROUPS // VALUE_SLOTS) as i:
                        for u in range(VALUE_SLOTS):
                            g = VALUE_SLOTS * i + u
                            pool.wait_ge(parts_hi_ready, GROUPS * level + g + 1)
                            tiles = bass.ds(g * SUB, SUB)
                            nc.gpsimd.tensor_tensor(parts[:, tiles, D + 1:K], values[:, u, :, :], parts[:, tiles, 0:D + 1], ALU.subtract)\
                                .then_inc(parts_lo_ready, 1)

                levels(pool, body)

            @block.vector
            def _(dve):
                dve.sem_inc(sums_copied, SLOTS)
                dve.sem_inc(e_raised, 1)

                def ending(level, c, cu):
                    C = GROUPS * level + c
                    ch = Chain(dve, chain, C, STEPS)
                    den, left = sums[:, :, D], todo[:, bass.ds(c * SUB, SUB)]

                    def join_halves():
                        dve.wait_ge(pair_used, RING + PAIRS * (C + 1))
                        banks = ps[:, 4 * cu:4 * cu + SUB, :]
                        ch.link(nc.vector.tensor_copy(sums[:, :, :], banks[:, :, D + 1:K]))
                        ch.link(nc.vector.tensor_tensor(sums[:, :, :], banks[:, :, 0:D + 1], sums[:, :, :], ALU.add))
                        dve.sem_inc(sums_copied, 1)

                    def invert():
                        ch.mark(nc.vector.scalar_tensor_tensor(out=take, in0=den, scalar=LEAST, in1=left, op0=ALU.is_ge, op1=ALU.mult))
                        ch.link(nc.vector.tensor_scalar(inverse, den, LEAST, None, ALU.max))
                        ch.mark(nc.vector.tensor_tensor(left, left, take, ALU.subtract))
                        ch.link(nc.vector.reciprocal(inverse, inverse))
                        ch.mark(nc.vector.tensor_tensor(inverse, inverse, take, ALU.mult))

                    def add_rows():
                        ch.wait()
                        for s in range(SUB):
                            rows = x[:, bass.ds(c, 1), s * D:(s + 1) * D].rearrange("p a d -> p (a d)")
                            ch.mark(nc.vector.scalar_tensor_tensor(out=rows, in0=sums[:, s, 0:D], scalar=inverse[:, s:s + 1],
                                                                   in1=rows, op0=ALU.mult, op1=ALU.add))

                    def measure():
                        ch.wait()
                        for s in range(SUB):
                            t = c * SUB + s
                            ins = nc.vector.bn_stats(sb["stats"][:, bass.ds(t, 1), :].rearrange("p a n -> p (a n)"),
                                                     row(tiles_of(x[:, :, :]), t))
                        ch.mark(ins)
                        assert ch.n == STEPS

                    return [join_halves, invert, add_rows, measure]

                def chunk(level, c, pieces, first=False):
                    at = (GROUPS * level + c, c)
                    for m in range(1 if first else 0, 2):
                        for half in range(2):
                            widen(dve, 0, at, m, half)
                            if pieces and (m, half) != (0, 0):
                                pieces[2 * m + half - 1]()
                    widen(dve, 0, at, 2, 0)
                    if pieces:
                        pieces[3]()
                    widen(dve, 0, at, 2, 1)
                    widen(dve, 0, at, 3)

                def body(level):
                    dve.wait_ge(e_raised, level + 1)
                    nc.vector.tensor_scalar(exponent[:, :], e[:, :], 0.0, None, ALU.min).then_inc(exponent_ready, 1)
                    nc.vector.tensor_scalar(e[:, :], e[:, :], LEVEL, None, ALU.add).then_inc(e_raised, 1)
                    widen(dve, 0, (GROUPS * level, 0), 0)
                    dve.wait_ge(exp_ready, level + 1)
                    nc.vector.tensor_tensor(weight[:, :], weight[:, :], valid[:, :], ALU.mult).then_inc(weight_ready, 1)
                    with dve.Fori(0, GROUPS // VALUE_SLOTS) as i:
                        for u in range(VALUE_SLOTS):
                            g = VALUE_SLOTS * i + u
                            dve.wait_ge(weight_ready, level + 1)
                            dve.wait_ge(parts_lo_ready, GROUPS * level + g + 1)
                            tiles = bass.ds(g * SUB, SUB)
                            nc.vector.tensor_tensor(values[:, u, :, :], inp[:, tiles, :],
                                                    weight[:, tiles].unsqueeze(2).to_broadcast([P, SUB, D + 1]), ALU.mult)\
                                .then_inc(values_ready, 1)
                    chunk(level, 0, [], first=True)
                    chunk(level, 1, ending(level, 0, 0))
                    with dve.Fori(1, GROUPS // 2) as i:
                        for cu in range(2):
                            c = 2 * i + cu
                            chunk(level, c, ending(level, c - 1, 1 - cu))
                    for piece in ending(level, GROUPS - 1, 1):
                        piece()

                levels(dve, body)
                dve.wait_ge(chain, STEPS * GROUPS)


def mix_routed_experts(nc, io, sb, ps):
    with ExitStack() as ctx:
        buf = lambda name, shape, dt=F32: ctx.enter_context(nc.sbuf_tensor(name, shape, dt))
        sem = lambda name: ctx.enter_context(nc.semaphore(name))
        x3 = tiles_of(sb["x1"][:, :, :])
        w1, w2 = buf("w1_all", [P, E, F]), buf("w2_all", [P, E, FH, D])
        w1_hi, w1_lo = buf("w1_all_hi", [P, E, F], F32R), buf("w1_all_lo", [P, E, F], F32R)
        b1, b2 = buf("b1_all", [P, E, FH]), buf("b2_all", [E, D])
        wg, bg = buf("wg", [P, E]), buf("bg", [P, E])
        stage = buf("stage3", [P, SLOTS, GROUP])
        xT = buf("xT3", [P, SLOTS, GROUP])
        xT_hi, xT_lo = buf("xT3_hi", [P, SLOTS, GROUP], F32R), buf("xT3_lo", [P, SLOTS, GROUP], F32R)
        hT = buf("hT3", [P, SLOTS, FH, GROUP])
        hT_hi, hT_lo = buf("hT3_hi", [P, SLOTS, FH, GROUP], F32R), buf("hT3_lo", [P, SLOTS, FH, GROUP], F32R)
        w2_hi, w2_lo = buf("w2_all_hi", [P, E, FH, D], F32R), buf("w2_all_lo", [P, E, FH, D], F32R)
        b2_hi, b2_lo = buf("b2_all_hi", [E, D], F32R), buf("b2_all_lo", [E, D], F32R)
        outT = buf("outT", [P, GROUP])
        mean, var, rstd, t0, t1 = (buf(n, [P, TILES])[:, :] for n in ("mean3", "var3", "rstd3", "t30", "t31"))
        iota = buf("iota", [P, E])
        iota_i = buf("iota_i", [P, E], I32)
        gates, top = buf("gates", [P, SUB, E]), buf("gates_top", [P, SUB, 8])
        index_i, index = buf("gates_index_i", [P, SUB, 8], U32), buf("gates_index", [P, SUB, 8])
        chosen = buf("chosen", [P, SLOTS, SUB, E])
        second = buf("second", [P, SUB, E])
        chosenT = buf("chosenT", [E, SLOTS, GROUP], F32R)
        idleT = buf("idleT", [E, SLOTS, GROUP], BF16)
        sink_rows = buf("sink_rows", [E, E, P])
        sink = buf("sink", [E, E, P], BF16)
        TURN_BANK, UP_BANK, OUT_BANK, GATE_BANK = 0, 1, 5, 7

        w1_in, weights_in = sem("w1_in"), sem("weights_in")
        w1_hi_ready, w1_lo_ready = sem("w1_hi_ready"), sem("w1_lo_ready")
        w2_hi_ready, w2_lo_ready = sem("w2_hi_ready"), sem("w2_lo_ready")
        sink_ready = sem("sink_ready")
        chain = sem("dve_chain3")
        group_chain = sem("group_chain3")
        iota_ready = sem("iota_ready")
        staged = sem("staged3")
        turned = sem("turned3")
        xT_ready, xT_hi_ready, xT_lo_ready = sem("xT_ready3"), sem("xT_hi_ready3"), sem("xT_lo_ready3")
        gates_ready = sem("gates_ready")
        gates_biased = sem("gates_biased")
        chosen_ready = sem("chosen_ready")
        chosen_turned = sem("chosen_turned")
        chosenT_ready = sem("chosenT_ready")
        idleT_ready = sem("idleT_ready")
        up_ready = sem("up_ready3")
        gelu_ready = sem("gelu_ready3")
        down_ready = sem("down_ready3")
        hi_ready = sem("hi_ready3")
        lo_ready = [sem("lo_ready_pool"), sem("lo_ready_dve")]
        out_copied = sem("out_copied")
        out_turned = sem("out_turned")
        rows_added = sem("rows_added")
        rows_out = sem("rows_out")
        RANK_STEPS = 12

        def groups(eng, group):
            group(0, 0, True, False)
            with eng.Fori(0, GROUPS // 2 - 1) as i:
                group(2 * i + 1, 1, False, False)
                group(2 * i + 2, 0, False, False)
            group(GROUPS - 1, 1, False, True)

        with nc.Block() as block:

            @block.sync
            def _(sp):
                sp.dma_start(w1[:, :, :], io["W1b"].rearrange("e d f -> d e f")).then_inc(w1_in, 16)
                sp.dma_start(wg[:, :], io["Wg"]).then_inc(weights_in, 16)
                sp.dma_start(bg[:, :], io["bg"].partition_broadcast(P)).then_inc(weights_in, 16)
                sp.dma_start(b1[:, :, :], io["b1b"].rearrange("e p f -> p e f")).then_inc(weights_in, 16)
                sp.dma_start(b2[:, :], io["b2b"]).then_inc(weights_in, 16)
                sp.dma_start(w2[:, :, :, :], io["W2b"].rearrange("e (f p) d -> p e f d", p=P)).then_inc(weights_in, 16)
                with sp.Fori(0, GROUPS) as g:
                    sp.wait_ge(rows_added, g + 1)
                    sp.dma_start(io["out"].rearrange("(t p) d -> p t d", p=P)[:, bass.ds(g * SUB, SUB), :],
                                 x3[:, bass.ds(g * SUB, SUB), :]).then_inc(rows_out, 16)
                sp.wait_ge(rows_out, 16 * GROUPS)

            @block.gpsimd
            def _(pool):
                nc.gpsimd.iota(iota_i[:, :], [[1, E]], base=0, channel_multiplier=0).then_inc(iota_ready, 1)
                pool.wait_ge(iota_ready, 1)
                nc.gpsimd.tensor_copy(iota[:, :], iota_i[:, :]).then_inc(iota_ready, 1)
                nc.gpsimd.memset(sink_rows[:, :, :], 0.0).then_inc(sink_ready, 1)
                pool.wait_ge(sink_ready, 1)
                nc.gpsimd.affine_select(out=sink_rows[:, :, :], in_=sink_rows[:, :, :], compare_op=ALU.not_equal,
                                        fill=SINK, base=0, pattern=[[-1, E], [0, P]], channel_multiplier=1).then_inc(sink_ready, 1)
                pool.wait_ge(sink_ready, 2)
                nc.gpsimd.tensor_copy(sink[:, :, :], sink_rows[:, :, :]).then_inc(sink_ready, 1)
                pool.wait_ge(w2_hi_ready, 1)
                nc.gpsimd.tensor_tensor(w2_lo[:, :, :, :], w2[:, :, :, :], w2_hi[:, :, :, :], ALU.subtract).then_inc(w2_lo_ready, 1)
                with pool.Fori(0, GROUPS) as g:
                    for e in range(E):
                        n = E * g + e
                        pool.wait_ge(hi_ready, FH * n + 1)
                        nc.gpsimd.tensor_tensor(hT_lo[:, e % 2, 0, :], hT[:, e % 2, 0, :], hT_hi[:, e % 2, 0, :], ALU.subtract)\
                            .then_inc(lo_ready[0], 1)

            @block.vector
            def _(dve):
                for s in range(FH):
                    dve.sem_inc(lo_ready[s], SLOTS)
                ch = Chain(dve, chain)
                row_statistics(nc, ch, sb["stats"], mean, var, t0, t1)
                ch.link(nc.vector.tensor_scalar(var, var, LN_EPS, None, ALU.add))
                inverse_root(nc, ch, rstd, var, t0, t1)

                def normalize(g, u):
                    dve.wait_ge(turned, g + 1)
                    for s in range(SUB):
                        t = g * SUB + s
                        ins = nc.vector.tensor_scalar(stage[:, u, s * D:(s + 1) * D], row(x3, t), mean[:, bass.ds(t, 1)],
                                                      rstd[:, bass.ds(t, 1)], ALU.subtract, ALU.mult)
                    ins.then_inc(staged, 1)

                def keep_turned(g, u):
                    dve.wait_ge(turned, SLOTS + g + 1)
                    nc.vector.tensor_copy(xT[:, u, :], ps[:, TURN_BANK, :]).then_inc(xT_ready, 1)

                def keep_low(g, u):
                    dve.wait_ge(xT_ready, g + 1)
                    dve.wait_ge(xT_hi_ready, g + 1)
                    nc.vector.tensor_tensor(xT_lo[:, u, :], xT[:, u, :], xT_hi[:, u, :], ALU.subtract)\
                        .then_inc(xT_lo_ready, 1)

                def rank(g, gc):
                    dve.wait_ge(gates_ready, g + 1)
                    gc.link(nc.vector.tensor_tensor(gates[:, :, :], ps[:, GATE_BANK, 0:SUB * E].rearrange("p (s e) -> p s e", e=E),
                                                    bg[:, :].unsqueeze(1).to_broadcast([P, SUB, E]), ALU.add))
                    dve.sem_inc(gates_biased, 1)
                    for s in range(SUB):
                        gc.mark(nc.vector.max(top[:, s, :], gates[:, s, :]))
                    gc.wait()
                    dve.sem_inc(gates_biased, 1)
                    for s in range(SUB):
                        gc.mark(nc.vector.max_index(index_i[:, s, :], top[:, s, :], gates[:, s, :]))
                    gc.wait()

                def choose(g, u, gc):
                    places = iota[:, :].unsqueeze(1).to_broadcast([P, SUB, E])
                    gc.link(nc.vector.tensor_copy(index[:, :, :], index_i[:, :, :]))
                    gc.mark(nc.vector.tensor_tensor(chosen[:, u, :, :], places, index[:, :, 0:1].to_broadcast([P, SUB, E]), ALU.is_equal))
                    gc.link(nc.vector.tensor_tensor(second[:, :, :], places, index[:, :, 1:2].to_broadcast([P, SUB, E]), ALU.is_equal))
                    nc.vector.tensor_tensor(chosen[:, u, :, :], chosen[:, u, :, :], second[:, :, :], ALU.add)\
                        .then_inc(chosen_ready, 1)
                    assert gc.n == RANK_STEPS

                def keep_chosen(g, u):
                    dve.wait_ge(chosen_turned, g + 1)
                    nc.vector.tensor_copy(chosenT[:, u, :], ps[0:E, GATE_BANK, :]).then_inc(chosenT_ready, 1)
                    dve.wait_ge(chosenT_ready, g + 1)
                    nc.vector.tensor_scalar(idleT[:, u, :], chosenT[:, u, :], -1.0, 1.0, ALU.mult, ALU.add)\
                        .then_inc(idleT_ready, 1)

                def split_hidden(g, e):
                    for f in range(FH):
                        dve.wait_ge(gelu_ready, 2 * FH + E * FH * g + e * FH + f + 1)
                        dve.wait_ge(down_ready, E * g + e + 1)
                        nc.vector.tensor_copy(hT_hi[:, e % 2, f, :], hT[:, e % 2, f, :]).then_inc(hi_ready, 1)
                    dve.wait_ge(hi_ready, FH * (E * g + e + 1))
                    nc.vector.tensor_tensor(hT_lo[:, e % 2, 1, :], hT[:, e % 2, 1, :], hT_hi[:, e % 2, 1, :], ALU.subtract)\
                        .then_inc(lo_ready[1], 1)

                def add_outputs(g):
                    dve.wait_ge(out_turned, g + 2)
                    nc.vector.tensor_tensor(group_of(x3, g), ps[:, GATE_BANK, :], group_of(x3, g), ALU.add).then_inc(rows_added, 1)

                normalize(0, 0)
                dve.wait_ge(w1_hi_ready, 1)
                nc.vector.tensor_tensor(w1_lo[:, :, :], w1[:, :, :], w1_hi[:, :, :], ALU.subtract).then_inc(w1_lo_ready, 1)
                dve.wait_ge(weights_in, 80)
                dve.wait_ge(iota_ready, 2)
                keep_turned(0, 0)
                keep_low(0, 0)
                gc = Chain(dve, group_chain, 0, RANK_STEPS)
                rank(0, gc)
                choose(0, 0, gc)
                keep_chosen(0, 0)
                dve.wait_ge(w2_hi_ready, 2)
                nc.vector.tensor_tensor(b2_lo[:, :], b2[:, :], b2_hi[:, :], ALU.subtract).then_inc(w2_lo_ready, 1)

                def group(g, u, first, last):
                    n, nu = g + 1, 1 - u
                    gc = Chain(dve, group_chain, n, RANK_STEPS)
                    prepare_next = {1: lambda: normalize(n, nu), 3: lambda: keep_turned(n, nu), 4: lambda: rank(n, gc),
                                    5: lambda: (choose(n, nu, gc), keep_low(n, nu)), 7: lambda: keep_chosen(n, nu)}
                    for e in range(E):
                        if e == 2 and not first:
                            add_outputs(g - 1)
                        if e in prepare_next and not last:
                            prepare_next[e]()
                        split_hidden(g, e)

                groups(dve, group)
                add_outputs(GROUPS - 1)

            @block.scalar
            def _(act):
                act.sem_inc(out_copied, SLOTS)
                def keep_high(g, u):
                    act.wait_ge(xT_ready, g + 1)
                    nc.scalar.activation(xT_hi[:, u, :], xT[:, u, :], ACT.Copy).then_inc(xT_hi_ready, 1)

                def gelus(g, e):
                    for f in range(FH):
                        n = e * FH + f
                        act.wait_ge(up_ready, E * FH * g + n + 1)
                        act.wait_ge(lo_ready[f], E * g + e + 1)
                        nc.scalar.activation(hT[:, e % 2, f, :], ps[:, UP_BANK + n % 4, :], ACT.Gelu, bias=b1[:, e, f:f + 1])\
                            .then_inc(gelu_ready, 1)

                act.sem_inc(gelu_ready, 2 * FH)
                act.wait_ge(w1_in, 16)
                nc.scalar.activation(w1_hi[:, :, :], w1[:, :, :], ACT.Copy).then_inc(w1_hi_ready, 1)
                keep_high(0, 0)
                act.wait_ge(weights_in, 80)
                nc.scalar.activation(w2_hi[:, :, :, :], w2[:, :, :, :], ACT.Copy).then_inc(w2_hi_ready, 1)
                nc.scalar.activation(b2_hi[:, :], b2[:, :], ACT.Copy).then_inc(w2_hi_ready, 1)

                def copy_outputs(g, u):
                    act.wait_ge(down_ready, SLOTS + E * (g + 1))
                    act.wait_ge(out_turned, g + 1)
                    nc.scalar.activation(outT[:, :], ps[:, OUT_BANK + u, :], ACT.Copy).then_inc(out_copied, 1)

                def group(g, u, first, last):
                    for e in range(E):
                        gelus(g, e)
                        if e == 0 and not first:
                            copy_outputs(g - 1, 1 - u)
                        if e == 3 and not last:
                            keep_high(g + 1, 1 - u)

                groups(act, group)
                copy_outputs(GROUPS - 1, 1)

            @block.tensor
            def _(pe):
                def turn(g, u):
                    pe.wait_ge(staged, g + 1)
                    for s in range(SUB):
                        ins = nc.tensor.transpose(ps[:, TURN_BANK, s * P:(s + 1) * P], stage[:, u, s * P:(s + 1) * P], sb["ident"][:, :])
                    ins.then_inc(turned, 1)

                def gate(g, u):
                    pe.wait_ge(xT_ready, g + 1)
                    if not isinstance(g, int) or g > 1:
                        pe.wait_ge(rows_added, g - 1)
                    for s in range(SUB):
                        ins = nc.tensor.matmul(ps[:, GATE_BANK, s * E:(s + 1) * E], xT[:, u, s * P:(s + 1) * P], wg[:, :],
                                               start=True, stop=True)
                    ins.then_inc(gates_ready, 1)

                def turn_chosen(g, u):
                    pe.wait_ge(chosen_ready, g + 1)
                    for s in range(SUB):
                        ins = nc.tensor.transpose(ps[0:E, GATE_BANK, s * P:(s + 1) * P], chosen[:, u, s, :], sb["ident"][:, :])
                    ins.then_inc(chosen_turned, 1)

                def bias(g, u):
                    pe.wait_ge(out_copied, g + 1)
                    out = ps[:, OUT_BANK + u, :]
                    nc.tensor.matmul(out, b2_lo[:, :], chosenT[:, u, :], start=True, stop=False)
                    nc.tensor.matmul(out, b2_hi[:, :], chosenT[:, u, :], start=False, stop=False)

                def turn_outputs(g):
                    pe.wait_ge(out_copied, SLOTS + g + 1)
                    for s in range(SUB):
                        ins = nc.tensor.transpose(ps[:, GATE_BANK, s * P:(s + 1) * P], outT[:, s * P:(s + 1) * P], sb["ident"][:, :])
                    ins.then_inc(out_turned, 1)

                def up(g, u, e):
                    if e == 0:
                        pe.wait_ge(xT_hi_ready, g + 1)
                        pe.wait_ge(xT_lo_ready, g + 1)
                    for f in range(FH):
                        n = e * FH + f
                        pe.wait_ge(gelu_ready, E * FH * g + n + 1)
                        cols = slice(f * P, (f + 1) * P)
                        out = ps[:, UP_BANK + n % 4, :]
                        nc.tensor.matmul(out, w1_lo[:, e, cols], xT_hi[:, u, :], start=True, stop=False)
                        nc.tensor.matmul(out, w1_hi[:, e, cols], xT_lo[:, u, :], start=False, stop=False)
                        nc.tensor.matmul(out, w1_hi[:, e, cols], xT_hi[:, u, :], start=False, stop=False)
                        if e == 0:
                            pe.wait_ge(idleT_ready, g + 1)
                        nc.tensor.matmul(out, sink[:, e, :], idleT[:, u, :], start=False, stop=True).then_inc(up_ready, 1)

                def down(g, u, e):
                    pe.wait_ge(lo_ready[0], SLOTS + E * g + e + 1)
                    pe.wait_ge(lo_ready[1], SLOTS + E * g + e + 1)
                    out = ps[:, OUT_BANK + u, :]
                    for f in range(FH):
                        last = e == E - 1 and f == FH - 1
                        nc.tensor.matmul(out, w2_hi[:, e, f, :], hT_lo[:, e % 2, f, :], start=False, stop=False)
                        nc.tensor.matmul(out, w2_lo[:, e, f, :], hT_hi[:, e % 2, f, :], start=False, stop=False)
                        ins = nc.tensor.matmul(out, w2_hi[:, e, f, :], hT_hi[:, e % 2, f, :], start=False, stop=last)
                    ins.then_inc(down_ready, 1)

                pe.sem_inc(turned, SLOTS)
                pe.sem_inc(out_turned, 1)
                pe.sem_inc(down_ready, SLOTS)
                turn(0, 0)
                pe.wait_ge(w1_lo_ready, 1)
                pe.wait_ge(weights_in, 80)
                gate(0, 0)
                turn_chosen(0, 0)
                pe.wait_ge(sink_ready, 3)
                up(0, 0, 0)
                pe.wait_ge(w2_lo_ready, 2)

                def group(g, u, first, last):
                    n, nu = g + 1, 1 - u
                    prepare_next = {2: lambda: turn(n, nu), 3: lambda: gate(n, nu), 6: lambda: turn_chosen(n, nu)}
                    for e in range(E):
                        if e + 1 < E:
                            up(g, u, e + 1)
                        elif not last:
                            up(n, nu, 0)
                        if e == 0:
                            bias(g, u)
                        if e == 1 and not first:
                            turn_outputs(g - 1)
                        if e in prepare_next and not last:
                            prepare_next[e]()
                        down(g, u, e)

                groups(pe, group)
                turn_outputs(GROUPS - 1)


def build(nc, io):
    with ExitStack() as ctx:
        sb = {}
        sb["x1"] = ctx.enter_context(nc.sbuf_tensor("x1", [P, GROUPS, GROUP], F32))
        sb["stats"] = ctx.enter_context(nc.sbuf_tensor("stats", [P, TILES, 6], F32))
        sb["ident"] = ctx.enter_context(nc.sbuf_tensor("ident", [P, P], F32))
        ps = ctx.enter_context(nc.psum_tensor("ps", [P, 8, 512], F32))
        with ExitStack() as graph:
            sb["mask"] = graph.enter_context(nc.sbuf_tensor("mask", [P, TILES * N], mybir.dt.uint8))
            with ExitStack() as attention:
                sb["v16"] = attention.enter_context(nc.sbuf_tensor("v16", [P, TILES, 2 * D + 1], F16))
                sb["qT"] = attention.enter_context(nc.sbuf_tensor("qT", [P, 2, N], F16))
                prepare(nc, io, sb, ps)
                attend(nc, io, sb, ps)
            mix_shared_experts(nc, io, sb, ps)
            with ExitStack() as rows:
                for name, shape, dt in (("inp", [P, TILES, D + 1], F32), ("e", [P, TILES], F32), ("valid", [P, TILES], F32),
                                        ("todo", [P, TILES], F32), ("levels", [P, 1], I32)):
                    sb[name] = rows.enter_context(nc.sbuf_tensor(name, shape, dt))
                project_nodes(nc, io, sb, ps)
                gather_nodes(nc, io, sb, ps)
        mix_routed_experts(nc, io, sb, ps)


def kernel(x, adj, L0_gnn_Wq, L0_gnn_Wk, L0_ffn_Wr, L0_ffn_br, L0_ffn_W1, L0_ffn_b1, L0_ffn_W2, L0_ffn_b2,
           L0_ffn_gamma, L0_ffn_beta, L1_gnn_W, L1_gnn_b, L1_gnn_a, L1_ffn_Wg, L1_ffn_bg, L1_ffn_W1, L1_ffn_b1,
           L1_ffn_W2, L1_ffn_b2):
    import concourse.bacc as bacc
    from concourse.bass_utils import run_bass_kernel_spmd

    laid = {
        "x": x,
        "adj": np.asarray(adj).T.reshape(PAIRS, 2, P, GROUPS, GROUP).transpose(3, 0, 2, 1, 4)
                 .reshape(GROUPS * PAIRS, P, 2 * GROUP),
        "WqT": np.asarray(L0_gnn_Wq).T,
        "WkT": np.asarray(L0_gnn_Wk).T,
        "Wr": L0_ffn_Wr, "br": L0_ffn_br, "gamma": L0_ffn_gamma, "beta": L0_ffn_beta,
        "W1a": L0_ffn_W1, "b1a": np.asarray(L0_ffn_b1).reshape(E, FH, P).transpose(0, 2, 1), "W2a": L0_ffn_W2, "b2a": L0_ffn_b2,
        "W_node": L1_gnn_W, "b_node": np.asarray(L1_gnn_b).reshape(D, 1), "a_node": L1_gnn_a,
        "Wg": L1_ffn_Wg, "bg": L1_ffn_bg,
        "W1b": L1_ffn_W1, "b1b": np.asarray(L1_ffn_b1).reshape(E, FH, P).transpose(0, 2, 1), "W2b": L1_ffn_W2, "b2b": L1_ffn_b2,
    }
    nc = bacc.Bacc("TRN2", target_bir_lowering=False, num_devices=1, dynamic_dma_scratch_size=1024)
    arrays, io = {}, {}
    for name, a in laid.items():
        a = np.ascontiguousarray(a)
        arrays[f"in_{name}"] = a
        io[name] = nc.dram_tensor(f"in_{name}", a.shape, mybir.dt.from_np(a.dtype), kind="ExternalInput").ap()
    io["feat"] = nc.dram_tensor("feat_spill", [P, GROUPS, SUB, D], F32).ap()
    io["out"] = nc.dram_tensor("out", [N, D], F32, kind="ExternalOutput").ap()
    build(nc, io)
    return run_bass_kernel_spmd(nc, [arrays], core_ids=[0]).results[0]["out"]
```
